# Optimizing a Trainium2 kernel written in Bass

```python
import numpy as np
import jax
import jax.numpy as jnp

def _softmax(x, axis=-1):
    return jax.nn.softmax(x, axis=axis)

def _gelu(x):
    return jax.nn.gelu(x, approximate=True)

def _silu(x):
    return jax.nn.silu(x)

def _sigmoid(x):
    return jax.nn.sigmoid(x)

def _layernorm(x, axis=-1, eps=1e-05):
    m = jnp.mean(x, axis=axis, keepdims=True)
    v = jnp.var(x, axis=axis, keepdims=True)
    return (x - m) / jnp.sqrt(v + eps)

def _scatter_add(tgt, idx, src, axis=0):
    return tgt.at[idx].add(src)

def _segment_sum(src, seg, n):
    return jax.ops.segment_sum(src, seg, n)
kernel_name = 'mk_perceiver_d2_seqx_r4_3bd6bf'

def setup_inputs(seed: int=0):
    np.random.seed(seed)
    _w = jnp.asarray

    def _rec_inputs():
        import jax
        import jax.numpy as jnp
        _rk = jax.random.key(seed)
        x = 7.22e-05 + 1 * jax.random.normal(jax.random.fold_in(_rk, 1), (1, 128, 256), jnp.float32)
        _lenS = 128 - jax.random.randint(jax.random.fold_in(_rk, 7), (1,), 0, max(1, 128 // 4) + 1, jnp.int32)
        _lenS2 = 12544 - jax.random.randint(jax.random.fold_in(_rk, 8), (1,), 0, max(1, 12544 // 4) + 1, jnp.int32)
        _ctx_1024P = jax.random.normal(jax.random.fold_in(_rk, 11), (1, 16, 256), jnp.float32)
        _ctx_1024c = jax.random.dirichlet(jax.random.fold_in(_rk, 511), 0.3 * jnp.ones((16,), jnp.float32), (1, 12544))
        _ctx_1024t = jnp.einsum('bsk,bkd->bsd', _ctx_1024c, _ctx_1024P)
        _ctx_1024t = _ctx_1024t * jax.lax.rsqrt(jnp.mean(jnp.square(_ctx_1024t)) + 1e-12) * 0.953939
        ctx_1024 = 4.13588e-05 + 0.999923 * (_ctx_1024t + 0.3 * jax.random.normal(jax.random.fold_in(_rk, 611), (1, 12544, 256), jnp.float32))
        _validS = jnp.arange(128)[None, :] < _lenS[:, None]
        _validS2 = jnp.arange(12544)[None, :] < _lenS2[:, None]
        _causal = jnp.tril(jnp.ones((128, 128), dtype=bool))
        mask_BxS2_bk0 = jnp.logical_not(jnp.broadcast_to(_validS2[:, :], (1, 12544)))
        return (x, ctx_1024, mask_BxS2_bk0)
    x, ctx_1024, mask_BxS2_bk0 = _rec_inputs()

    def _L0_xattn_setup():
        import jax, jax.numpy as jnp
        import numpy as np
        HEADS = 16
        DIM_HEAD = 64
        SCALE = DIM_HEAD ** (-0.5)

        def _split_heads(x):
            b, l, n = x.shape
            return x.reshape(b, l, HEADS, DIM_HEAD).transpose(0, 2, 1, 3)
        key = jax.random.key(seed)
        ks = jax.random.split(key, 6)
        B, L, D = (4, 512, 256)
        inner = HEADS * DIM_HEAD
        s = lambda fan_in: 1.0 / np.sqrt(fan_in)
        return {'x1': jax.random.normal(ks[0], (B, L, D), jnp.float32), 'x2': jax.random.normal(ks[1], (B, L, D), jnp.float32), 'Wq': jax.random.normal(ks[2], (D, inner), jnp.float32) * s(D), 'Wkv': jax.random.normal(ks[3], (D, 2 * inner), jnp.float32) * s(D), 'Wo': jax.random.normal(ks[4], (inner, D), jnp.float32) * s(inner), 'bo': jax.random.normal(ks[5], (D,), jnp.float32) * 0.02}
    _L0_xattn_all = _L0_xattn_setup()
    _L0_xattn_in = {k: v for k, v in _L0_xattn_all.items() if k in ('Wq', 'Wkv', 'Wo', 'bo')}
    del _L0_xattn_all

    def _L0_attn_setup():
        import jax, jax.numpy as jnp
        import numpy as np
        MAX_W, MIN_W = (120, 24)
        key = jax.random.key(seed)
        ks = jax.random.split(key, 11)
        B, S, D, H = (2, 512, 256, 16)
        hd = D // H
        s = 1.0 / float(np.sqrt(D))
        return {'x': jax.random.normal(ks[0], (B, S, D), jnp.float32), 'alpha': jnp.float32(0.1), 'Wq': jax.random.normal(ks[1], (D, D), jnp.float32) * s, 'bq': jnp.zeros((D,), jnp.float32), 'Wk': jax.random.normal(ks[2], (D, D), jnp.float32) * s, 'bk': jnp.zeros((D,), jnp.float32), 'Wv': jax.random.normal(ks[3], (D, D), jnp.float32) * s, 'bv': jnp.zeros((D,), jnp.float32), 'W_o': jax.random.normal(ks[4], (H, hd, hd), jnp.float32), 'Wfc': jax.random.normal(ks[5], (D, D), jnp.float32) * s, 'bfc': jnp.zeros((D,), jnp.float32)}
    _L0_attn_all = _L0_attn_setup()
    _L0_attn_in = {k: v for k, v in _L0_attn_all.items() if k in ('alpha', 'Wq', 'bq', 'Wk', 'bk', 'Wv', 'bv', 'W_o', 'Wfc', 'bfc')}
    del _L0_attn_all

    def _L0_ffn_setup():
        import jax, jax.numpy as jnp
        import numpy as np
        D_MODEL = 256
        NUM_EXPERTS = 8
        TOP_K = 2
        B, S = (4, 512)
        key = jax.random.key(seed)
        ks = jax.random.split(key, 7)
        scale_in = 1.0 / np.sqrt(D_MODEL)
        scale_hid = 1.0 / np.sqrt(2 * D_MODEL)
        return {'x': jax.random.normal(ks[0], (B, S, D_MODEL), dtype=jnp.float32), 'Wg': jax.random.normal(ks[1], (D_MODEL, NUM_EXPERTS), dtype=jnp.float32) * scale_in, 'bg': jnp.zeros((NUM_EXPERTS,), dtype=jnp.float32), 'W1': jax.random.normal(ks[2], (NUM_EXPERTS, D_MODEL, 2 * D_MODEL), dtype=jnp.float32) * scale_in, 'b1': jnp.zeros((NUM_EXPERTS, 2 * D_MODEL), dtype=jnp.float32), 'W2': jax.random.normal(ks[3], (NUM_EXPERTS, 2 * D_MODEL, D_MODEL), dtype=jnp.float32) * scale_hid, 'b2': jnp.zeros((NUM_EXPERTS, D_MODEL), dtype=jnp.float32)}
    _L0_ffn_all = _L0_ffn_setup()
    _L0_ffn_in = {k: v for k, v in _L0_ffn_all.items() if k in ('Wg', 'bg', 'W1', 'b1', 'W2', 'b2')}
    del _L0_ffn_all

    def _L1_xattn_setup():
        import jax, jax.numpy as jnp
        import numpy as np
        B, LI, LC, H = (16, 512, 512, 256)
        key = jax.random.key(seed)
        k1, k2, k3, k4 = jax.random.split(key, 4)
        inp = jax.random.normal(k1, (B, LI, H), dtype=jnp.float32)
        ctx = jax.random.normal(k2, (B, LC, H), dtype=jnp.float32)
        context_mask = jnp.broadcast_to(jnp.arange(LC) >= 3 * LC // 4, (B, LC))
        W = jax.random.normal(k3, (H, H), dtype=jnp.float32) * (1.0 / np.sqrt(H))
        b = jax.random.normal(k4, (H,), dtype=jnp.float32) * 0.01
        return {'input': inp, 'context': ctx, 'context_mask': context_mask, 'W': W, 'b': b}
    _L1_xattn_all = _L1_xattn_setup()
    _L1_xattn_in = {k: v for k, v in _L1_xattn_all.items() if k in ('W', 'b')}
    del _L1_xattn_all

    def _L1_attn_setup():
        import jax, jax.numpy as jnp
        import numpy as np
        D_INNER = 256
        STATE = 16
        DT_RANK = 64
        LOG_EPS = -7.0
        CLAMP = 20.0
        key = jax.random.key(seed)
        ks = jax.random.split(key, 4)
        B, L = (2, 256)
        x = jax.random.normal(ks[0], (B, L, D_INNER), jnp.float32)
        W_xproj = jax.random.normal(ks[1], (D_INNER, DT_RANK + 2 * STATE), jnp.float32) * 0.02
        W_dt = jax.random.normal(ks[2], (DT_RANK, D_INNER), jnp.float32) * 0.02
        b_dt = jax.random.normal(ks[3], (D_INNER,), jnp.float32) * 0.02
        A_log = jnp.log(jnp.tile(jnp.arange(1, STATE + 1, dtype=jnp.float32), (D_INNER, 1)))
        D = jnp.ones((D_INNER,), jnp.float32)
        return {'x': x, 'W_xproj': W_xproj, 'W_dt': W_dt, 'b_dt': b_dt, 'A_log': A_log, 'D': D}
    _L1_attn_all = _L1_attn_setup()
    _L1_attn_in = {k: v for k, v in _L1_attn_all.items() if k in ('W_xproj', 'W_dt', 'b_dt', 'A_log', 'D')}
    del _L1_attn_all

    def _L1_ffn_setup():
        import jax, jax.numpy as jnp
        import numpy as np
        N_EXPERTS = 32
        TOP_K = 8
        N_GROUP = 4
        TOPK_GROUP = 2
        ROUTED_SCALING = 2.5

        def _gate(x, gate_w, gate_bias):
            T, E = (x.shape[0], gate_w.shape[0])
            logits = jnp.einsum('th,eh->te', x, gate_w)
            scores = jax.nn.sigmoid(logits)
            scores_choice = scores + gate_bias[None, :]
            grp = scores_choice.reshape(T, N_GROUP, E // N_GROUP)
            top2, _ = jax.lax.top_k(grp, 2)
            group_scores = top2.sum(-1)
            _, grp_idx = jax.lax.top_k(group_scores, TOPK_GROUP)
            group_mask = jax.nn.one_hot(grp_idx, N_GROUP, dtype=scores.dtype).sum(1)
            expert_mask = jnp.repeat(group_mask, E // N_GROUP, axis=1)
            masked = jnp.where(expert_mask > 0, scores_choice, 0.0)
            _, topk_idx = jax.lax.top_k(masked, TOP_K)
            topk_w = jnp.take_along_axis(scores, topk_idx, axis=1)
            topk_w = topk_w / (topk_w.sum(-1, keepdims=True) + 1e-20)
            topk_w = topk_w * ROUTED_SCALING
            return (topk_idx, topk_w)

        def _mlp(x, wg, wu, wd):
            return jnp.einsum('...i,hi->...h', jax.nn.silu(jnp.einsum('...h,ih->...i', x, wg)) * jnp.einsum('...h,ih->...i', x, wu), wd)
        key = jax.random.key(seed)
        ks = jax.random.split(key, 9)
        B, S, H, I = (2, 128, 256, 128)
        w = 0.02
        return {'hidden_states': jax.random.normal(ks[0], (B, S, H), jnp.float32), 'gate_w': jax.random.normal(ks[1], (N_EXPERTS, H), jnp.float32) * w, 'gate_bias': jax.random.normal(ks[2], (N_EXPERTS,), jnp.float32) * w, 'expert_gate': jax.random.normal(ks[3], (N_EXPERTS, I, H), jnp.float32) * w, 'expert_up': jax.random.normal(ks[4], (N_EXPERTS, I, H), jnp.float32) * w, 'expert_down': jax.random.normal(ks[5], (N_EXPERTS, H, I), jnp.float32) * w, 'shared_gate': jax.random.normal(ks[6], (2 * I, H), jnp.float32) * w, 'shared_up': jax.random.normal(ks[7], (2 * I, H), jnp.float32) * w, 'shared_down': jax.random.normal(ks[8], (H, 2 * I), jnp.float32) * w}
    _L1_ffn_all = _L1_ffn_setup()
    _L1_ffn_in = {k: v for k, v in _L1_ffn_all.items() if k in ('gate_w', 'gate_bias', 'expert_gate', 'expert_up', 'expert_down', 'shared_gate', 'shared_up', 'shared_down')}
    del _L1_ffn_all
    return {'x': x, 'ctx_1024': ctx_1024, 'mask_BxS2_bk0': mask_BxS2_bk0, 'L0_xattn_Wq': _L0_xattn_in['Wq'], 'L0_xattn_Wkv': _L0_xattn_in['Wkv'], 'L0_xattn_Wo': _L0_xattn_in['Wo'], 'L0_xattn_bo': _L0_xattn_in['bo'], 'L0_attn_alpha': _L0_attn_in['alpha'], 'L0_attn_Wq': _L0_attn_in['Wq'], 'L0_attn_bq': _L0_attn_in['bq'], 'L0_attn_Wk': _L0_attn_in['Wk'], 'L0_attn_bk': _L0_attn_in['bk'], 'L0_attn_Wv': _L0_attn_in['Wv'], 'L0_attn_bv': _L0_attn_in['bv'], 'L0_attn_W_o': _L0_attn_in['W_o'], 'L0_attn_Wfc': _L0_attn_in['Wfc'], 'L0_attn_bfc': _L0_attn_in['bfc'], 'L0_ffn_Wg': _L0_ffn_in['Wg'], 'L0_ffn_bg': _L0_ffn_in['bg'], 'L0_ffn_W1': _L0_ffn_in['W1'], 'L0_ffn_b1': _L0_ffn_in['b1'], 'L0_ffn_W2': _L0_ffn_in['W2'], 'L0_ffn_b2': _L0_ffn_in['b2'], 'L1_xattn_W': _L1_xattn_in['W'], 'L1_xattn_b': _L1_xattn_in['b'], 'L1_attn_W_xproj': _L1_attn_in['W_xproj'], 'L1_attn_W_dt': _L1_attn_in['W_dt'], 'L1_attn_b_dt': _L1_attn_in['b_dt'], 'L1_attn_A_log': _L1_attn_in['A_log'], 'L1_attn_D': _L1_attn_in['D'], 'L1_ffn_gate_w': _L1_ffn_in['gate_w'], 'L1_ffn_gate_bias': _L1_ffn_in['gate_bias'], 'L1_ffn_expert_gate': _L1_ffn_in['expert_gate'], 'L1_ffn_expert_up': _L1_ffn_in['expert_up'], 'L1_ffn_expert_down': _L1_ffn_in['expert_down'], 'L1_ffn_shared_gate': _L1_ffn_in['shared_gate'], 'L1_ffn_shared_up': _L1_ffn_in['shared_up'], 'L1_ffn_shared_down': _L1_ffn_in['shared_down']}

def reference(x, ctx_1024, mask_BxS2_bk0, L0_xattn_Wq, L0_xattn_Wkv, L0_xattn_Wo, L0_xattn_bo, L0_attn_alpha, L0_attn_Wq, L0_attn_bq, L0_attn_Wk, L0_attn_bk, L0_attn_Wv, L0_attn_bv, L0_attn_W_o, L0_attn_Wfc, L0_attn_bfc, L0_ffn_Wg, L0_ffn_bg, L0_ffn_W1, L0_ffn_b1, L0_ffn_W2, L0_ffn_b2, L1_xattn_W, L1_xattn_b, L1_attn_W_xproj, L1_attn_W_dt, L1_attn_b_dt, L1_attn_A_log, L1_attn_D, L1_ffn_gate_w, L1_ffn_gate_bias, L1_ffn_expert_gate, L1_ffn_expert_up, L1_ffn_expert_down, L1_ffn_shared_gate, L1_ffn_shared_up, L1_ffn_shared_down):
    import jax
    import jax.numpy as jnp

    def _L0_xattn_ref(x1, x2, Wq, Wkv, Wo, bo):
        import jax, jax.numpy as jnp
        import numpy as np
        HEADS = 16
        DIM_HEAD = 64
        SCALE = DIM_HEAD ** (-0.5)

        def _split_heads(x):
            b, l, n = x.shape
            return x.reshape(b, l, HEADS, DIM_HEAD).transpose(0, 2, 1, 3)
        q = x1 @ Wq
        kv = x2 @ Wkv
        k, v = jnp.split(kv, 2, axis=-1)
        q, k, v = map(_split_heads, (q, k, v))
        attn = jnp.einsum('bhid,bhjd->bhij', q, k) * SCALE
        attn = jax.nn.softmax(attn, axis=-1)
        out = jnp.einsum('bhij,bhjd->bhid', attn, v)
        b, h, l, d = out.shape
        out = out.transpose(0, 2, 1, 3).reshape(b, l, h * d)
        return out @ Wo + bo

    def _L0_attn_ref(x, alpha, Wq, bq, Wk, bk, Wv, bv, W_o, Wfc, bfc):
        import jax, jax.numpy as jnp
        import numpy as np
        MAX_W, MIN_W = (120, 24)
        B, S, D = x.shape
        H, hd, _ = W_o.shape
        fluct = jnp.abs(x[:, -1] - x[:, -2])
        a = jax.nn.sigmoid(alpha)
        ewma_prev = fluct[0, 0]
        signal = a * fluct.mean() + (1.0 - a) * ewma_prev
        scale = jax.nn.sigmoid(signal)
        w = jnp.floor(MIN_W + (MAX_W - MIN_W) * scale).astype(jnp.int32)
        half = w // 2
        q = (x @ Wq + bq).reshape(B, S, H, hd).transpose(0, 2, 1, 3)
        k = (x @ Wk + bk).reshape(B, S, H, hd).transpose(0, 2, 1, 3)
        v = (x @ Wv + bv).reshape(B, S, H, hd).transpose(0, 2, 1, 3)
        inv_sqrt = 1.0 / float(np.sqrt(hd))
        scores = jnp.einsum('bhqd,bhkd->bhqk', q, k) * inv_sqrt
        idx = jnp.arange(S)
        band = jnp.abs(idx[:, None] - idx[None, :]) <= half
        scores = jnp.where(band[None, None], scores, -1e+30)
        attn = jax.nn.softmax(scores, axis=-1)
        out = jnp.einsum('bhqk,bhkd->bhqd', attn, v)
        out = jnp.einsum('bhqd,hdk->bhqk', out, W_o)
        out = out.transpose(0, 2, 1, 3).reshape(B, S, D)
        return out @ Wfc + bfc

    def _L0_ffn_ref(x, Wg, bg, W1, b1, W2, b2):
        import jax, jax.numpy as jnp
        import numpy as np
        D_MODEL = 256
        NUM_EXPERTS = 8
        TOP_K = 2
        B, S = (4, 512)
        Bb, Ss, D = x.shape
        E = Wg.shape[1]
        xf = x.reshape(-1, D)
        logits = xf @ Wg + bg
        probs = jax.nn.softmax(logits, axis=-1)
        w, idx = jax.lax.top_k(probs, TOP_K)
        w = w / jnp.sum(w, axis=-1, keepdims=True)
        comb = jnp.sum(jax.nn.one_hot(idx, E, dtype=xf.dtype) * w[..., None], axis=1)
        h = jax.nn.relu(jnp.einsum('nd,edh->enh', xf, W1) + b1[:, None, :])
        y = jnp.einsum('enh,ehd->end', h, W2) + b2[:, None, :]
        out = jnp.einsum('end,ne->nd', y, comb)
        return out.reshape(Bb, Ss, D)

    def _L1_xattn_ref(input, context, context_mask, W, b):
        import jax, jax.numpy as jnp
        import numpy as np
        B, LI, LC, H = (16, 512, 512, 256)
        q = jax.nn.relu(jnp.einsum('bih,oh->bio', input, W) + b)
        k = jax.nn.relu(jnp.einsum('bjh,oh->bjo', context, W) + b)
        scores = jnp.einsum('bid,bjd->bij', q, k)
        scores = jnp.where(context_mask[:, None, :], -jnp.inf, scores)
        probs = jax.nn.softmax(scores, axis=2)
        return jnp.einsum('bij,bjd->bid', probs, k)

    def _L1_attn_ref(x, W_xproj, W_dt, b_dt, A_log, D):
        import jax, jax.numpy as jnp
        import numpy as np
        D_INNER = 256
        STATE = 16
        DT_RANK = 64
        LOG_EPS = -7.0
        CLAMP = 20.0
        proj = x @ W_xproj
        dt_inter = proj[..., :DT_RANK]
        B_ssm = proj[..., DT_RANK:DT_RANK + STATE]
        C_ssm = proj[..., DT_RANK + STATE:]
        delta = jax.nn.softplus(dt_inter @ W_dt + b_dt)
        A = -jnp.exp(A_log)
        log_delta_A = jnp.clip(delta[..., None] * A[None, None], LOG_EPS, CLAMP)
        delta_A = jnp.exp(log_delta_A)
        delta_B_u = delta[..., None] * B_ssm[:, :, None, :] * x[..., None]
        log_dA = jnp.log(jnp.clip(delta_A, 1e-07, None))
        log_R = jnp.cumsum(log_dA, axis=1)
        R = jnp.exp(jnp.minimum(log_R, CLAMP))
        exp_neg_log_R = jnp.exp(jnp.minimum(-log_R, CLAMP))
        S = jnp.cumsum(delta_B_u * exp_neg_log_R, axis=1)
        h = R * S
        y = jnp.einsum('bln,bldn->bld', C_ssm, h) + x * D
        return y

    def _L1_ffn_ref(hidden_states, gate_w, gate_bias, expert_gate, expert_up, expert_down, shared_gate, shared_up, shared_down):
        import jax, jax.numpy as jnp
        import numpy as np
        N_EXPERTS = 32
        TOP_K = 8
        N_GROUP = 4
        TOPK_GROUP = 2
        ROUTED_SCALING = 2.5

        def _gate(x, gate_w, gate_bias):
            T, E = (x.shape[0], gate_w.shape[0])
            logits = jnp.einsum('th,eh->te', x, gate_w)
            scores = jax.nn.sigmoid(logits)
            scores_choice = scores + gate_bias[None, :]
            grp = scores_choice.reshape(T, N_GROUP, E // N_GROUP)
            top2, _ = jax.lax.top_k(grp, 2)
            group_scores = top2.sum(-1)
            _, grp_idx = jax.lax.top_k(group_scores, TOPK_GROUP)
            group_mask = jax.nn.one_hot(grp_idx, N_GROUP, dtype=scores.dtype).sum(1)
            expert_mask = jnp.repeat(group_mask, E // N_GROUP, axis=1)
            masked = jnp.where(expert_mask > 0, scores_choice, 0.0)
            _, topk_idx = jax.lax.top_k(masked, TOP_K)
            topk_w = jnp.take_along_axis(scores, topk_idx, axis=1)
            topk_w = topk_w / (topk_w.sum(-1, keepdims=True) + 1e-20)
            topk_w = topk_w * ROUTED_SCALING
            return (topk_idx, topk_w)

        def _mlp(x, wg, wu, wd):
            return jnp.einsum('...i,hi->...h', jax.nn.silu(jnp.einsum('...h,ih->...i', x, wg)) * jnp.einsum('...h,ih->...i', x, wu), wd)
        orig_shape = hidden_states.shape
        H = orig_shape[-1]
        residuals = hidden_states
        x = hidden_states.reshape(-1, H)
        topk_idx, topk_w = _gate(x, gate_w, gate_bias)
        g = jnp.einsum('th,eih->eti', x, expert_gate)
        u = jnp.einsum('th,eih->eti', x, expert_up)
        outs = jnp.einsum('eti,ehi->eth', jax.nn.silu(g) * u, expert_down)
        outs_t = jnp.transpose(outs, (1, 0, 2))
        gathered = jnp.take_along_axis(outs_t, topk_idx[:, :, None], axis=1)
        final = (gathered * topk_w[:, :, None]).sum(1)
        shared = _mlp(residuals, shared_gate, shared_up, shared_down)
        return final.reshape(orig_shape) + shared
    x = x + _L0_xattn_ref(_layernorm(x, axis=-1), ctx_1024, L0_xattn_Wq, L0_xattn_Wkv, L0_xattn_Wo, L0_xattn_bo)
    x = x + _L0_attn_ref(_layernorm(x, axis=-1), L0_attn_alpha, L0_attn_Wq, L0_attn_bq, L0_attn_Wk, L0_attn_bk, L0_attn_Wv, L0_attn_bv, L0_attn_W_o, L0_attn_Wfc, L0_attn_bfc)
    x = x + _L0_ffn_ref(_layernorm(x, axis=-1), L0_ffn_Wg, L0_ffn_bg, L0_ffn_W1, L0_ffn_b1, L0_ffn_W2, L0_ffn_b2)
    x = x + _L1_xattn_ref(_layernorm(x, axis=-1), ctx_1024, mask_BxS2_bk0, L1_xattn_W, L1_xattn_b)
    x = x + _L1_attn_ref(_layernorm(x, axis=-1), L1_attn_W_xproj, L1_attn_W_dt, L1_attn_b_dt, L1_attn_A_log, L1_attn_D)
    x = x + _L1_ffn_ref(_layernorm(x, axis=-1), L1_ffn_gate_w, L1_ffn_gate_bias, L1_ffn_expert_gate, L1_ffn_expert_up, L1_ffn_expert_down, L1_ffn_shared_gate, L1_ffn_shared_up, L1_ffn_shared_down)
    return x

_drawn_inputs = setup_inputs


def setup_inputs(seed=0):
    import zlib

    import numpy as np

    out = dict(_drawn_inputs(seed))
    spreads = {'L0_attn_bq': (0.0, 0.1),
     'L0_attn_bk': (0.0, 2.0),
     'L0_attn_bv': (0.0, 0.1),
     'L0_attn_bfc': (0.0, 0.1),
     'L0_ffn_bg': (0.0, 0.1),
     'L0_ffn_b1': (0.0, 0.1),
     'L0_ffn_b2': (0.0, 0.1),
     'L1_attn_D': (1.0, 0.2)}
    factors = {'L1_xattn_b': 4.487,
     'L1_attn_W_dt': 50.129,
     'L1_attn_b_dt': 64.0,
     'L1_attn_A_log': 2.894,
     'L1_ffn_gate_w': 8.0,
     'L1_ffn_gate_bias': 8.0,
     'L1_ffn_expert_gate': 8.0,
     'L1_ffn_expert_up': 8.0,
     'L1_ffn_expert_down': 8.0,
     'L1_ffn_shared_gate': 8.0,
     'L1_ffn_shared_up': 8.0,
     'L1_ffn_shared_down': 8.0,
     'L1_attn_W_xproj': 3.565}
    for name, (base, spread) in spreads.items():
        noise = np.random.default_rng([zlib.crc32(name.encode()), seed]).standard_normal(out[name].shape)
        drawn = base * np.exp(spread * noise) if base else spread * noise
        out[name] = jnp.asarray(drawn.astype(out[name].dtype))
    for name, factor in factors.items():
        out[name] = (out[name] * factor).astype(out[name].dtype)
    return out
```

```python
from contextlib import ExitStack

import concourse.bass as bass
from concourse import mybir

F32 = mybir.dt.float32
F32R = mybir.dt.float32r
BF16 = mybir.dt.bfloat16
I32 = mybir.dt.int32
U8 = mybir.dt.uint8
ALU = mybir.AluOpType
ACT = mybir.ActivationFunctionType
AX_X = mybir.AxisListType.X

P = 128
D = 256
KT = D // P
EPS = 1e-5
BIG = 1e30
NT = 7
CK = NT * P
HK = CK // 2
H0, DH0 = 16, 64
H1, DH1 = 16, 16
HPT = P // DH1
E0, F0 = 8, 512
E1, F1 = 32, 128
NS1 = 2
EA = E1 + NS1
GR, TG, TE = 4, 2, 8
NST, DTR = 16, 64


def build(nc, t, out):
    with ExitStack() as top:
        def sb(name, shape, dt=F32, ctx=top):
            return ctx.enter_context(nc.sbuf_tensor(name, shape, dt))

        ps = top.enter_context(nc.psum_tensor("ps", [P, 8, 512], F32))
        named = {}

        def sem(name):
            if name not in named:
                named[name] = top.enter_context(nc.semaphore(name))
            return named[name]

        count = {}

        def link(eng, ins, name):
            count[name] = count.get(name, 0) + 1
            ins.then_inc(sem(name), 1)
            eng.wait_ge(sem(name), count[name])

        v = {}

        def keep(name, shape, dt=F32):
            v[name] = sb(name, shape, dt)
            return v[name]

        res = keep("res", [P, D])
        xn = keep("xn", [P, D])
        xnT = keep("xnT", [P, KT, P])
        st6 = keep("st6", [P, 6])
        mv = keep("mv", [P, 2])
        vare = keep("vare", [P, 1])
        sd = keep("sd", [P, 1])
        rstd = keep("rstd", [P, 1])
        ident = keep("ident", [P, P])
        keep("ones", [P, P])
        keep("row0", [P, P])
        keep("tri", [P, P])
        keep("hmask", [P, HPT])
        keep("below", [P, E1, E1])
        keep("disti", [P, 2, P], I32)
        keep("dist", [P, P])
        keep("brow", [1, 3 * D])
        for name in ("aq", "ak", "av", "afc"):
            keep(name, [P, KT, D])
        keep("awo", [P, KT, DH1])
        keep("abqk", [P, 2 * KT])
        keep("alpha", [P, 1])
        keep("zero", [P, 1])
        keep("wg0", [P, KT, E0])
        keep("bg", [P, E0])
        keep("b2", [E0, D])
        keep("wx", [P, KT, D])
        keep("bx", [P, KT])
        keep("wxp", [P, KT, DTR + 2 * NST])
        keep("wdt", [DTR, D])
        keep("bdt", [1, D])
        keep("dskip", [P, D])
        keep("wr1", [P, KT, E1])
        keep("br1", [P, E1])

        def norm_vector(dve, n):
            if n > 0:
                dve.wait_ge(sem("res_ready"), n)
            link(dve, nc.vector.bn_stats(st6[:, :], res[:, :]), "norm_chain")
            link(dve, nc.vector.bn_aggr(mv[:, :], st6[:, :]), "norm_chain")
            nc.vector.tensor_scalar(vare[:, :], mv[:, 1:2], EPS, None, ALU.add).then_inc(sem("var_ready"), 1)
            dve.wait_ge(sem("sd_ready"), n + 1)
            link(dve, nc.vector.reciprocal(rstd[:, :], sd[:, :]), "norm_chain")
            nc.vector.tensor_scalar(xn[:, :], res[:, :], mv[:, 0:1], rstd[:, 0:1], ALU.subtract,
                                    ALU.mult).then_inc(sem("xn_ready"), 1)
            dve.wait_ge(sem("xn_turned"), n + 1)
            nc.vector.tensor_copy(xnT[:, :, :], ps[:, 7, 0:D].rearrange("p (k q) -> p k q", k=KT)).then_inc(
                sem("xnT_ready"), 1)

        def norm_scalar(act, n):
            act.wait_ge(sem("var_ready"), n + 1)
            nc.scalar.activation(sd[:, :], vare[:, :], ACT.Sqrt).then_inc(sem("sd_ready"), 1)

        def norm_tensor(pe, n):
            pe.wait_ge(sem("xn_ready"), n + 1)
            for k in range(KT):
                mm = nc.tensor.transpose(ps[:, 7, k * P:(k + 1) * P], xn[:, k * P:(k + 1) * P], ident[:, :])
            mm.then_inc(sem("xn_turned"), 1)
            pe.wait_ge(sem("xnT_ready"), n + 1)

        norms = (norm_vector, norm_scalar, norm_tensor)
        stage_context(nc, t, sb, sem, link, ps, norms, v)
        with ExitStack() as experts:
            v["wg"] = sb("wg", [P, KT, EA * F1], F32, experts)
            v["wu"] = sb("wu", [P, KT, EA * F1], F32, experts)
            with ExitStack() as first:
                v["w1"] = sb("w1", [P, KT, E0, F0], F32, first)
                v["w2"] = sb("w2", [P, E0 * F0 // P, D], F32, first)
                v["b1"] = sb("b1", [P, E0, F0], F32, first)
                stage_band(nc, t, sb, sem, link, ps, norms, v)
                stage_mix0(nc, t, sb, sem, link, ps, norms, v)
            v["wd"] = sb("wd", [P, EA, D], F32, experts)
            stage_relu_context(nc, t, sb, sem, link, ps, norms, v)
            stage_scan(nc, t, sb, sem, link, ps, norms, v)
            stage_mix1(nc, t, sb, sem, link, ps, norms, v)
            finish(nc, sem, res, out, 6)


def finish(nc, sem, res, out, stages):
    with nc.Block() as block:
        @block.sync
        def _(sp):
            sp.wait_ge(sem("res_ready"), stages)
            sp.dma_start(out[:, :], res[:, :]).then_inc(sem("out_stored"), 16)
            sp.wait_ge(sem("out_stored"), 16)


def stage_context(nc, t, sb, sem, link, ps, norms, v):
    norm_vector, norm_scalar, norm_tensor = norms
    res, xnT, ident, ones = v["res"], v["xnT"], v["ident"], v["ones"]
    chunks = t["ctxN"].shape[0]
    pairs = chunks // 2
    steps = H0 * 2
    SCALE = DH0 ** -0.5
    with ExitStack() as keep:
        U = sb("U", [P, H0, D], F32, keep)
        den = sb("den", [P, H0], F32, keep)
        wq = sb("wq", [P, KT, H0 * DH0], F32, keep)
        wkT = sb("wkT", [DH0, H0, D], F32, keep)
        wv, wo = wq, wkT
        with ExitStack() as loop:
            qh = sb("qh", [P, H0, KT, P], F32R, loop)
            ql = sb("ql", [P, H0, KT, P], F32R, loop)
            rawT = sb("rawT", [P, KT, CK], F32, loop)
            rawN = sb("rawN", [P, NT, D], F32, loop)
            cTh = [sb(f"cTh{i}", [P, KT, CK], F32R, loop) for i in range(2)]
            cTl = [sb(f"cTl{i}", [P, KT, CK], F32R, loop) for i in range(2)]
            cNh = [sb(f"cNh{i}", [P, NT, D], F32R, loop) for i in range(2)]
            cNl = [sb(f"cNl{i}", [P, NT, D], F32R, loop) for i in range(2)]
            prob = [sb(f"prob{i}", [P, 2, HK], F32, loop) for i in range(2)]
            pTh = sb("pTh", [P, CK], F32R, loop)
            pTl = sb("pTl", [P, CK], F32R, loop)
            nm = sb("nm", [P, 2, H0], F32, loop)
            nmx = sb("nmx", [P, 1], F32, loop)
            al = sb("al", [P, 2], F32, loop)
            rs = sb("rs", [P, 2], F32, loop)
            qT = sb("qT", [DH0, H0, P], F32, loop)

            S = [ps[:, 2 * i:2 * i + 2, 0:HK] for i in range(2)]
            pT_ps = ps[:, 4:6, :].rearrange("p b n -> p (b n)")[:, 0:CK]
            O = [ps[:, 6 + i, 0:D] for i in range(2)]

            with nc.Block() as block:
                @block.sync
                def _(sp):
                    sp.dma_start(res[:, :], t["x"]).then_inc(sem("x_in"), 16)
                    sp.dma_start(wq[:, :, :], t["wq0"]).then_inc(sem("wq_in"), 16)
                    sp.dma_start(wkT[:, :, :], t["wkT0"]).then_inc(sem("wk_in"), 16)
                    sp.dma_start(rawT[:, :, :], t["ctxT"][0]).then_inc(sem("rawT_in"), 16)
                    sp.dma_start(rawN[:, :, :], t["ctxN"][0]).then_inc(sem("rawN_in"), 16)
                    sp.wait_ge(sem("q2_done"), 2)
                    sp.dma_start(wv[:, :, :], t["wv0"]).then_inc(sem("post_in"), 16)
                    sp.dma_start(wo[:, :, :], t["wo0"]).then_inc(sem("post_in"), 16)
                    with sp.Fori(1, chunks) as c:
                        sp.wait_ge(sem("cT_ready"), c)
                        sp.dma_start(rawT[:, :, :], t["ctxT"][bass.ds(c, 1)].rearrange("o p k n -> p (o k) n")).then_inc(sem("rawT_in"), 16)
                        sp.wait_ge(sem("cN_ready"), c)
                        sp.dma_start(rawN[:, :, :], t["ctxN"][bass.ds(c, 1)].rearrange("o p k n -> p (o k) n")).then_inc(sem("rawN_in"), 16)
                    sp.wait_ge(sem("cT_ready"), chunks)
                    sp.dma_start(rawT[:, :, :], t["ctxT"][0]).then_inc(sem("rawT_in"), 16)

                @block.gpsimd
                def _(pool):
                    def nought(x):
                        return v["zero"][:, 0:1].unsqueeze(2).broadcast_to([P, x.shape[1], x.shape[2]])

                    link(pool, nc.gpsimd.memset(v["zero"][:, :], 0.0), "pool_chain")
                    link(pool, nc.gpsimd.memset(v["ident"][:, :], 0.0), "pool_chain")
                    nc.gpsimd.affine_select(out=v["ident"][:, :], in_=v["ident"][:, :], compare_op=ALU.not_equal,
                                            fill=1.0, base=0, pattern=[[1, P]],
                                            channel_multiplier=-1).then_inc(sem("ident_ready"), 1)
                    for b in range(2):
                        pool.wait_ge(sem("rawT_in"), 16 * (b + 1))
                        link(pool, nc.gpsimd.tensor_copy(cTh[b][:, :, :], rawT[:, :, :]), "pool_chain")
                        nc.gpsimd.tensor_tensor(cTl[b][:, :, :], rawT[:, :, :], cTh[b][:, :, :].bitcast(F32),
                                                ALU.subtract).then_inc(sem("cT_ready"), 1)
                        pool.wait_ge(sem("rawN_in"), 16 * (b + 1))
                        link(pool, nc.gpsimd.tensor_copy(cNh[b][:, :, :], rawN[:, :, :]), "pool_chain")
                        nc.gpsimd.tensor_tensor(cNl[b][:, :, :], rawN[:, :, :], cNh[b][:, :, :].bitcast(F32),
                                                ALU.subtract).then_inc(sem("cN_ready"), 1)
                    link(pool, nc.gpsimd.memset(v["ones"][:, :], 1.0), "pool_chain")
                    link(pool, nc.gpsimd.memset(v["row0"][:, :], 0.0), "pool_chain")
                    nc.gpsimd.memset(v["row0"][0:1, :], 1.0)
                    link(pool, nc.gpsimd.memset(v["hmask"][:, :], 1.0), "pool_chain")
                    link(pool, nc.gpsimd.affine_select(out=v["hmask"][:, :], in_=v["hmask"][:, :], compare_op=ALU.is_ge,
                                                       fill=0.0, base=0, pattern=[[-DH1, HPT]],
                                                       channel_multiplier=1), "pool_chain")
                    nc.gpsimd.affine_select(out=v["hmask"][:, :], in_=v["hmask"][:, :], compare_op=ALU.is_ge,
                                            fill=0.0, base=DH1 - 1, pattern=[[DH1, HPT]], channel_multiplier=-1)
                    nc.gpsimd.affine_select(out=v["tri"][:, :], in_=v["ones"][:, :], compare_op=ALU.is_ge,
                                            fill=0.0, base=0, pattern=[[1, P]], channel_multiplier=-1)
                    link(pool, nc.gpsimd.memset(v["below"][:, :, :], 1.0), "pool_chain")
                    nc.gpsimd.affine_select(out=v["below"][:, :, :], in_=v["below"][:, :, :], compare_op=ALU.is_gt,
                                            fill=0.0, base=0, pattern=[[1, E1], [-1, E1]], channel_multiplier=0)
                    nc.gpsimd.iota(v["disti"][:, 0, :], pattern=[[2, P]], base=0, channel_multiplier=-2)
                    nc.gpsimd.iota(v["disti"][:, 1, :], pattern=[[-2, P]], base=0,
                                   channel_multiplier=2).then_inc(sem("consts_ready"), 1)
                    with pool.Fori(1, pairs) as i:
                        for b in range(2):
                            for raw, hi, lo, came, used, ready, n in (
                                    (rawT, cTh[b], cTl[b], "rawT_in", "scores_done", "cT_ready", 0),
                                    (rawN, cNh[b], cNl[b], "rawN_in", "pv_done", "cN_ready", 1)):
                                pool.wait_ge(sem(came), i * 32 + 16 * (b + 1))
                                pool.wait_ge(sem(used), i * steps + H0 * (b - 1))
                                nc.gpsimd.tensor_tensor(hi[:, :, :], raw[:, :, :], nought(raw),
                                                        ALU.add).then_inc(sem("split_hi"), 1)
                                pool.wait_ge(sem("split_hi"), i * 4 + (2 * b + n - 3))
                                nc.gpsimd.tensor_tensor(lo[:, :, :], raw[:, :, :], hi[:, :, :].bitcast(F32),
                                                        ALU.subtract).then_inc(sem(ready), 1)
                    pool.wait_ge(sem("rawT_in"), 16 * (chunks + 1))
                    pool.wait_ge(sem("scores_done"), H0 * (chunks - 1))
                    nc.gpsimd.tensor_copy(cTh[0][:, :, :], rawT[:, :, :]).then_inc(sem("split_hi"), 1)
                    pool.wait_ge(sem("split_hi"), 4 * (pairs - 1) + 1)
                    nc.gpsimd.tensor_tensor(cTl[0][:, :, :], rawT[:, :, :], cTh[0][:, :, :].bitcast(F32),
                                            ALU.subtract).then_inc(sem("cT_ready"), 1)

                @block.scalar
                def _(act):
                    act.dma_start(v["brow"][:, :], t["brow"]).then_inc(sem("post_in"), 16)
                    for name in ("aq", "ak", "av", "afc", "awo"):
                        act.dma_start(v[name][:, :, :], t[name]).then_inc(sem("band_in"), 16)
                    act.dma_start(v["abqk"][:, :], t["abqk"]).then_inc(sem("band_in"), 16)
                    act.dma_start(v["alpha"][:, :], t["alpha"].partition_broadcast(P)).then_inc(sem("band_in"), 16)
                    norm_scalar(act, 0)
                    for g in range(2):
                        act.wait_ge(sem("q2_done"), g + 1)
                        bank = 4 if g == 0 else 0
                        nc.scalar.activation(qh[:, 8 * g:8 * g + 8, :, :].rearrange("p h k q -> p (h k q)"),
                                             ps[:, bank:bank + 4, :].rearrange("p b n -> p (b n)"), ACT.Copy,
                                             scale=SCALE).then_inc(sem("qh_ready"), 1)

                    def exp_step(u):
                        par, h, b = (u // H0) % 2, u % H0, u % 2
                        nc.scalar.activation(al[:, b:b + 1], nm[:, 1 - par, h:h + 1], ACT.Exp,
                                             bias=nm[:, par, h:h + 1], scale=-1.0)
                        nc.scalar.activation(prob[b][:, :, :], S[b], ACT.Exp, bias=nm[:, par, h:h + 1],
                                             scale=1.0, accum_out=rs[:, b:b + 1]).then_inc(sem("exp_done"), 1)

                    act.wait_ge(sem("max_done"), 1)
                    exp_step(0)
                    with act.Fori(0, pairs) as i:
                        for u in range(steps):
                            act.wait_ge(sem("p_turned"), i * steps + (u + 1))
                            nc.scalar.activation(pTh[:, :], pT_ps, ACT.Copy).then_inc(sem("pTh_ready"), 1)
                            act.wait_ge(sem("max_done"), i * steps + (u + 2))
                            act.wait_ge(sem("pv_free"), i * steps + (u + 2))
                            exp_step(u + 1)

                @block.vector
                def _(dve):
                    dve.wait_ge(sem("x_in"), 16)
                    nc.vector.memset(U[:, :, :].rearrange("p h d -> p (h d)"), 0.0)
                    nc.vector.memset(den[:, :], 0.0)
                    nc.vector.memset(nm[:, :, :].rearrange("p a h -> p (a h)"), BIG).then_inc(sem("pv_free"), 2)
                    norm_vector(dve, 0)
                    dve.wait_ge(sem("qT_done"), 1)
                    nc.vector.tensor_copy(qT[:, :, :], ps[0:DH0, 0:4, :].rearrange("p b (h q) -> p (b h) q", h=4)).then_inc(
                        sem("qT_ready"), 1)
                    for g in range(2):
                        dve.wait_ge(sem("qh_ready"), g + 1)
                        bank = 4 if g == 0 else 0
                        hi = qh[:, 8 * g:8 * g + 8, :, :].rearrange("p h k q -> p (h k q)").bitcast(F32)
                        nc.vector.scalar_tensor_tensor(
                            ql[:, 8 * g:8 * g + 8, :, :].rearrange("p h k q -> p (h k q)"),
                            ps[:, bank:bank + 4, :].rearrange("p b n -> p (b n)"), SCALE, hi,
                            ALU.mult, ALU.subtract).then_inc(sem("ql_ready"), 1)

                    def max_step(u):
                        par, h, b = (u // H0) % 2, u % H0, u % 2
                        nc.vector.tensor_reduce(nmx[:, :], S[b], mybir.AxisListType.XY, ALU.max,
                                                negate=True).then_inc(sem("chunk_max"), 1)
                        return par, h

                    dve.wait_ge(sem("scores_done"), 1)
                    max_step(0)
                    dve.wait_ge(sem("chunk_max"), 1)
                    nc.vector.tensor_tensor(nm[:, 0, 0:1], nm[:, 1, 0:1], nmx[:, :], ALU.min).then_inc(sem("max_done"), 1)
                    with dve.Fori(0, pairs) as i:
                        for u in range(steps):
                            h, b = u % H0, u % 2
                            dve.wait_ge(sem("max_done"), i * steps + (u + 1))
                            dve.wait_ge(sem("scores_done"), i * steps + (u + 2))
                            par1, h1 = max_step(u + 1)
                            dve.wait_ge(sem("chunk_max"), i * steps + (u + 2))
                            nc.vector.tensor_tensor(nm[:, par1, h1:h1 + 1], nm[:, 1 - par1, h1:h1 + 1], nmx[:, :],
                                                    ALU.min).then_inc(sem("max_done"), 1)
                            dve.wait_ge(sem("pTh_ready"), i * steps + (u + 1))
                            nc.vector.tensor_tensor(pTl[:, :], pT_ps, pTh[:, :].bitcast(F32),
                                                    ALU.subtract).then_inc(sem("pTl_ready"), 1)
                            dve.wait_ge(sem("pv_free"), i * steps + (u + 2))
                            nc.vector.scalar_tensor_tensor(den[:, h:h + 1], den[:, h:h + 1], al[:, b:b + 1],
                                                           rs[:, b:b + 1], ALU.mult, ALU.add)
                            dve.wait_ge(sem("pv_done"), i * steps + (u + 1))
                            nc.vector.scalar_tensor_tensor(U[:, h, :], U[:, h, :], al[:, b:b + 1], O[b],
                                                           ALU.mult, ALU.add).then_inc(sem("pv_free"), 1)

                @block.tensor
                def _(pe):
                    pe.wait_ge(sem("ident_ready"), 1)
                    norm_tensor(pe, 0)
                    pe.wait_ge(sem("wq_in"), 16)
                    for h in range(H0):
                        for k in range(KT):
                            mm = nc.tensor.matmul(ps[0:DH0, h // 4, (h % 4) * P:(h % 4 + 1) * P],
                                                  wq[:, k, h * DH0:(h + 1) * DH0], xnT[:, k, :],
                                                  start=(k == 0), stop=(k == KT - 1))
                    mm.then_inc(sem("qT_done"), 1)
                    pe.wait_ge(sem("wk_in"), 16)
                    pe.wait_ge(sem("qT_ready"), 1)
                    for h in range(H0):
                        bank = 4 + h // 2 if h < 8 else (h - 8) // 2
                        for m in range(KT):
                            col = (h % 2) * D + m * P
                            mm = nc.tensor.matmul(ps[:, bank, col:col + P], wkT[:, h, m * P:(m + 1) * P],
                                                  qT[:, h, :], start=True, stop=True)
                        if h % 8 == 7:
                            mm.then_inc(sem("q2_done"), 1)
                    pe.wait_ge(sem("ql_ready"), 2)

                    def scores(u):
                        par, h, b = (u // H0) % 2, u % H0, u % 2
                        for half in range(2):
                            cols = slice(half * HK, (half + 1) * HK)
                            n = 0
                            for q, c in ((qh, cTh[par]), (qh, cTl[par]), (ql, cTh[par])):
                                for k in range(KT):
                                    mm = nc.tensor.matmul(S[b][:, half, :], q[:, h, k, :], c[:, k, cols],
                                                          start=(n == 0), stop=(n == 3 * KT - 1))
                                    n += 1
                        mm.then_inc(sem("scores_done"), 1)

                    pe.wait_ge(sem("cT_ready"), 1)
                    scores(0)
                    scores(1)
                    with pe.Fori(0, pairs) as i:
                        for u in range(steps):
                            par, b = u // H0, u % 2
                            pe.wait_ge(sem("exp_done"), i * steps + (u + 1))
                            for k in range(NT):
                                mm = nc.tensor.transpose(pT_ps[:, k * P:(k + 1) * P],
                                                         prob[b][:, :, :].rearrange("p a n -> p (a n)")[:, k * P:(k + 1) * P],
                                                         ident[:, :])
                            mm.then_inc(sem("p_turned"), 1)
                            if (u + 2) % H0 == 0:
                                pe.wait_ge(sem("cT_ready"), i * 2 + ((u + 2) // H0 + 1))
                            scores(u + 2)
                            if u % H0 == 0:
                                pe.wait_ge(sem("cN_ready"), i * 2 + (par + 1))
                            pe.wait_ge(sem("pv_free"), i * steps + (u + 1))
                            pe.wait_ge(sem("pTh_ready"), i * steps + (u + 1))
                            n = 0
                            for p, c in ((pTh, cNh[par]), (pTh, cNl[par]), (pTl, cNh[par])):
                                if n == 2 * NT:
                                    pe.wait_ge(sem("pTl_ready"), i * steps + (u + 1))
                                for k in range(NT):
                                    mm = nc.tensor.matmul(O[b], p[:, k * P:(k + 1) * P], c[:, k, :],
                                                          start=(n == 0), stop=(n == 3 * NT - 1))
                                    n += 1
                            mm.then_inc(sem("pv_done"), 1)

        with ExitStack() as post:
            rden = sb("rden", [P, H0], F32, post)
            UT = sb("UT", [P, H0, KT, P], F32, post)
            oT = sb("oT", [DH0, H0, P], F32, post)
            with nc.Block() as block:
                @block.vector
                def _(dve):
                    link(dve, nc.vector.reciprocal(rden[:, :], den[:, :]), "post_chain")
                    for h in range(H0):
                        ins = nc.vector.tensor_scalar(U[:, h, :], U[:, h, :], rden[:, h:h + 1], None, ALU.mult)
                        if h % 8 == 7:
                            ins.then_inc(sem("U_scaled"), 1)
                    dve.wait_ge(sem("U_turned"), 2)
                    nc.vector.tensor_copy(UT[:, 8:16, :, :].rearrange("p h k q -> p (h k q)"),
                                          ps[:, 4:8, :].rearrange("p b n -> p (b n)")).then_inc(sem("UT_b"), 1)
                    dve.wait_ge(sem("oT_done"), 1)
                    nc.vector.tensor_copy(oT[:, :, :], ps[0:DH0, 0:4, :].rearrange("p b (h q) -> p (b h) q", h=4)).then_inc(
                        sem("oT_ready"), 1)
                    dve.wait_ge(sem("y0_done"), 1)
                    nc.vector.tensor_tensor(res[:, :], res[:, :], ps[:, 4, 0:D], ALU.add).then_inc(sem("res_ready"), 1)

                @block.scalar
                def _(act):
                    act.wait_ge(sem("U_turned"), 1)
                    nc.scalar.copy(UT[:, 0:8, :, :].rearrange("p h k q -> p (h k q)"),
                                   ps[:, 0:4, :].rearrange("p b n -> p (b n)")).then_inc(sem("UT_a"), 1)

                @block.tensor
                def _(pe):
                    for h in range(H0):
                        if h % 8 == 0:
                            pe.wait_ge(sem("U_scaled"), h // 8 + 1)
                        for k in range(KT):
                            mm = nc.tensor.transpose(ps[:, h // 2, (h % 2) * D + k * P:(h % 2) * D + (k + 1) * P],
                                                     U[:, h, k * P:(k + 1) * P], ident[:, :])
                        if h % 8 == 7:
                            mm.then_inc(sem("U_turned"), 1)
                    pe.wait_ge(sem("post_in"), 48)
                    pe.wait_ge(sem("UT_a"), 1)
                    for h in range(H0):
                        if h == 8:
                            pe.wait_ge(sem("UT_b"), 1)
                        for k in range(KT):
                            mm = nc.tensor.matmul(ps[0:DH0, h // 4, (h % 4) * P:(h % 4 + 1) * P],
                                                  wv[:, k, h * DH0:(h + 1) * DH0], UT[:, h, k, :],
                                                  start=(k == 0), stop=(k == KT - 1))
                    mm.then_inc(sem("oT_done"), 1)
                    pe.wait_ge(sem("oT_ready"), 1)
                    pe.wait_ge(sem("consts_ready"), 1)
                    nc.tensor.matmul(ps[:, 4, 0:D], ones[0:1, :], v["brow"][0:1, 0:D], start=True, stop=False)
                    for h in range(H0):
                        mm = nc.tensor.matmul(ps[:, 4, 0:D], oT[:, h, :], wo[:, h, :], start=False, stop=(h == H0 - 1))
                    mm.then_inc(sem("y0_done"), 1)


def stage_mix1(nc, t, sb, sem, link, ps, norms, v):
    norm_vector, norm_scalar, norm_tensor = norms
    res, xnT, ident = v["res"], v["xnT"], v["ident"]
    wg, wu, wd, below = v["wg"], v["wu"], v["wd"], v["below"]
    FACTOR = 2.5
    EB = 4
    blocks = [range(e, min(e + EB, EA)) for e in range(0, EA, EB)]
    with ExitStack() as own:
        sc = sb("f_sc", [P, E1], F32, own)
        ch = sb("f_ch", [P, E1], F32, own)
        best = sb("f_best", [P, GR, 8], F32, own)
        gs = sb("f_gs", [P, GR], F32, own)
        gsel = sb("f_gsel", [P, GR], F32, own)
        grank = sb("f_grank", [P, GR], F32, own)
        gw = sb("f_gw", [P, GR, GR], F32, own)
        gt = sb("f_gt", [P, GR, GR], F32, own)
        wins = sb("f_wins", [P, E1, E1], F32, own)
        ties = sb("f_ties", [P, E1, E1], F32, own)
        rank = sb("f_rank", [P, E1], F32, own)
        sel = sb("f_sel", [P, E1], F32, own)
        one = sb("f_one", [P, 2], F32, own)
        comb = sb("f_comb", [P, EA], F32, own)
        gate = [sb(f"f_gate{i}", [P, EB * F1], F32, own) for i in range(2)]
        act_ = [sb(f"f_act{i}", [P, EB * F1], F32, own) for i in range(2)]
        actT = [sb(f"f_actT{i}", [P, EB, P], F32, own) for i in range(2)]

        with nc.Block() as block:
            @block.vector
            def _(dve):
                norm_vector(dve, 5)
                dve.wait_ge(sem("logits1_exp"), 1)
                link(dve, nc.vector.tensor_scalar(sc[:, :], sc[:, :], 1.0, None, ALU.add), "mix1_chain")
                link(dve, nc.vector.reciprocal(sc[:, :], sc[:, :]), "mix1_chain")
                link(dve, nc.vector.tensor_tensor(ch[:, :], sc[:, :], v["br1"][:, :], ALU.add), "mix1_chain")
                for k in range(GR):
                    ins = nc.vector.max(best[:, k, :], ch[:, k * 8:(k + 1) * 8])
                link(dve, ins, "mix1_chain")
                link(dve, nc.vector.tensor_tensor(gs[:, :], best[:, :, 0], best[:, :, 1], ALU.add), "mix1_chain")
                rank_select(nc, dve, link, "mix1_chain", gs[:, :], GR, TG, gw[:, :, :], gt[:, :, :], grank[:, :],
                            gsel[:, :], below)
                link(dve, nc.vector.tensor_tensor(ch[:, :].rearrange("p (g e) -> p g e", g=GR),
                                                  ch[:, :].rearrange("p (g e) -> p g e", g=GR),
                                                  gsel[:, :].unsqueeze(2).broadcast_to([P, GR, E1 // GR]), ALU.mult), "mix1_chain")
                rank_select(nc, dve, link, "mix1_chain", ch[:, :], E1, TE, wins[:, :, :], ties[:, :, :], rank[:, :],
                            sel[:, :], below)
                link(dve, nc.vector.tensor_tensor(sel[:, :], sel[:, :], sc[:, :], ALU.mult), "mix1_chain")
                link(dve, nc.vector.tensor_reduce(one[:, 0:1], sel[:, :], AX_X, ALU.add), "mix1_chain")
                link(dve, nc.vector.tensor_scalar(one[:, 0:1], one[:, 0:1], 1e-20, None, ALU.add), "mix1_chain")
                link(dve, nc.vector.reciprocal(one[:, 1:2], one[:, 0:1]), "mix1_chain")
                nc.vector.memset(comb[:, E1:EA], 1.0)
                link(dve, nc.vector.tensor_scalar(comb[:, 0:E1], sel[:, :], one[:, 1:2], FACTOR, ALU.mult, ALU.mult), "mix1_chain")
                for n, experts in enumerate(blocks):
                    b = n % 2
                    dve.wait_ge(sem("gate_ready"), n + 1)
                    for j, e in enumerate(experts):
                        cols = slice(j * F1, (j + 1) * F1)
                        ins = nc.vector.scalar_tensor_tensor(act_[b][:, cols], gate[b][:, cols], comb[:, e:e + 1],
                                                             ps[:, 2 + b, cols], ALU.mult, ALU.mult)
                    ins.then_inc(sem("act_ready"), 1)
                dve.wait_ge(sem("y5_done"), 1)
                nc.vector.tensor_tensor(res[:, :], res[:, :], ps[:, 7, 0:D], ALU.add).then_inc(sem("res_ready"), 1)

            @block.scalar
            def _(act):
                norm_scalar(act, 5)
                act.wait_ge(sem("logits1_done"), 1)
                nc.scalar.activation(sc[:, :], ps[:, 6, 0:E1], ACT.Exp, scale=-1.0).then_inc(sem("logits1_exp"), 1)

                def silu(n):
                    b, w = n % 2, len(blocks[n]) * F1
                    act.wait_ge(sem("gu_done"), n + 1)
                    if n >= 2:
                        act.wait_ge(sem("act_ready"), n - 1)
                    nc.scalar.activation(gate[b][:, 0:w], ps[:, b, 0:w], ACT.Silu).then_inc(sem("gate_ready"), 1)

                silu(0)
                for n, experts in enumerate(blocks):
                    b, w = n % 2, len(experts) * P
                    if n + 1 < len(blocks):
                        silu(n + 1)
                    act.wait_ge(sem("act_turned"), n + 1)
                    nc.scalar.copy(actT[b][:, 0:len(experts), :].rearrange("p e q -> p (e q)"),
                                   ps[:, 4 + b, 0:w]).then_inc(sem("actT_ready"), 1)

            @block.tensor
            def _(pe):
                norm_tensor(pe, 5)
                for k in range(KT):
                    mm = nc.tensor.matmul(ps[:, 6, 0:E1], xnT[:, k, :], v["wr1"][:, k, :], start=(k == 0), stop=(k == KT - 1))
                mm.then_inc(sem("logits1_done"), 1)
                pe.wait_ge(sem("mix1_in"), 32)
                pe.wait_ge(sem("wd_in"), 16)

                def gate_up(n):
                    e, w = blocks[n][0], len(blocks[n]) * F1
                    if n >= 2:
                        pe.wait_ge(sem("act_ready"), n - 1)
                    for bank, m in ((n % 2, wg), (2 + n % 2, wu)):
                        for k in range(KT):
                            mm = nc.tensor.matmul(ps[:, bank, 0:w], xnT[:, k, :], m[:, k, e * F1:e * F1 + w],
                                                  start=(k == 0), stop=(k == KT - 1))
                    mm.then_inc(sem("gu_done"), 1)

                def down(n):
                    pe.wait_ge(sem("actT_ready"), n + 1)
                    for j, e in enumerate(blocks[n]):
                        mm = nc.tensor.matmul(ps[:, 7, 0:D], actT[n % 2][:, j, :], wd[:, e, :],
                                              start=(e == 0), stop=(e == EA - 1))
                    return mm

                gate_up(0)
                gate_up(1)
                for n, experts in enumerate(blocks):
                    pe.wait_ge(sem("act_ready"), n + 1)
                    for j in range(len(experts)):
                        mm = nc.tensor.transpose(ps[:, 4 + n % 2, j * P:(j + 1) * P], act_[n % 2][:, j * F1:(j + 1) * F1], ident[:, :])
                    mm.then_inc(sem("act_turned"), 1)
                    if n + 2 < len(blocks):
                        gate_up(n + 2)
                    if n >= 1:
                        down(n - 1)
                down(len(blocks) - 1).then_inc(sem("y5_done"), 1)


def stage_scan(nc, t, sb, sem, link, ps, norms, v):
    norm_vector, norm_scalar, norm_tensor = norms
    res, xn, xnT, ones, tri = v["res"], v["xn"], v["xnT"], v["ones"], v["tri"]
    LOG_EPS, CLAMP = -7.0, 20.0
    BD = 64
    NB = D // BD
    W = BD * NST
    with ExitStack() as own:
        ea = sb("e_ea", [P, D * NST], F32, own)
        dtT = sb("e_dtT", [DTR, P], F32, own)
        bc = sb("e_bc", [P, 2 * NST], F32, own)
        z = sb("e_z", [P, D], F32, own)
        pos = sb("e_pos", [P, D], F32, own)
        u = sb("e_u", [P, D], F32, own)
        s1 = sb("e_s", [P, D], F32, own)
        s2 = sb("e_s2", [P, D], F32, own)
        poly = sb("e_poly", [P, D], F32, own)
        delta = sb("e_delta", [P, D], F32, own)
        dx = sb("e_dx", [P, D], F32, own)
        y = sb("e_y", [P, D], F32, own)
        la = [sb(f"e_la{i}", [P, W], F32, own) for i in range(2)]
        R = [sb(f"e_R{i}", [P, W], F32, own) for i in range(2)]
        inv = [sb(f"e_inv{i}", [P, W], F32, own) for i in range(2)]
        g = [sb(f"e_g{i}", [P, W], F32, own) for i in range(2)]

        def cn(x):
            return x.rearrange("p (c n) -> p c n", n=NST)

        def over_states(x):
            return x.unsqueeze(2).broadcast_to([P, BD, NST])

        def over_channels(x):
            return x.unsqueeze(1).broadcast_to([P, BD, NST])

        def bank2(n):
            return ps[:, n:n + 2, :].rearrange("p b n -> p (b n)")

        with nc.Block() as block:
            @block.sync
            def _(sp):
                sp.dma_start(ea[:, :], t["alog"].partition_broadcast(P)).then_inc(sem("alog_in"), 16)

            @block.gpsimd
            def _(pool):
                for n in range(NB):
                    b, cols = n % 2, slice(n * BD, (n + 1) * BD)
                    if n == 0:
                        pool.wait_ge(sem("dx_ready"), 1)
                        pool.wait_ge(sem("bc_ready"), 1)
                    if n >= 2:
                        pool.wait_ge(sem("sum_done"), n - 1)
                        pool.wait_ge(sem("y4_ready"), n - 1)
                    nc.gpsimd.tensor_tensor(cn(g[b][:, :]), over_states(dx[:, cols]), over_channels(bc[:, 0:NST]),
                                            ALU.mult).then_inc(sem("g_ready"), 1)
                    pool.wait_ge(sem("R_ready"), n + 1)
                    nc.gpsimd.tensor_tensor(cn(R[b][:, :]), cn(R[b][:, :]), over_channels(bc[:, NST:2 * NST]),
                                            ALU.mult).then_inc(sem("CR_ready"), 1)

            @block.scalar
            def _(act):
                norm_scalar(act, 4)
                act.wait_ge(sem("alog_in"), 16)
                nc.scalar.activation(ea[:, :], ea[:, :], ACT.Exp).then_inc(sem("ea_done"), 1)
                act.wait_ge(sem("absz_ready"), 1)
                nc.scalar.activation(u[:, :], u[:, :], ACT.Exp, scale=-1.0).then_inc(sem("u_ready"), 1)
                for n in range(NB):
                    b = n % 2
                    act.wait_ge(sem("neg_ready"), n + 1)
                    nc.scalar.activation(inv[b][:, :], inv[b][:, :], ACT.Exp).then_inc(sem("inv_ready"), 1)
                    if n >= 2:
                        act.wait_ge(sem("y4_ready"), n - 1)
                    nc.scalar.activation(R[b][:, :], bank2(2 * b), ACT.Exp).then_inc(sem("R_ready"), 1)

            @block.vector
            def _(dve):
                norm_vector(dve, 4)
                dve.wait_ge(sem("dt_done"), 1)
                nc.vector.tensor_copy(dtT[:, :], ps[0:DTR, 4, 0:P]).then_inc(sem("dtT_ready"), 1)
                nc.vector.tensor_copy(bc[:, :], ps[:, 5, 0:2 * NST]).then_inc(sem("bc_ready"), 1)
                dve.wait_ge(sem("z_done"), 1)
                link(dve, nc.vector.tensor_copy(z[:, :], ps[:, 6, 0:D]), "scan_chain")
                nc.vector.scalar_tensor_tensor(u[:, :], z[:, :], -1.0, z[:, :], ALU.mult, ALU.max).then_inc(sem("absz_ready"), 1)
                nc.vector.tensor_scalar(pos[:, :], z[:, :], 0.0, None, ALU.max)
                dve.wait_ge(sem("u_ready"), 1)
                link(dve, nc.vector.tensor_scalar(s1[:, :], u[:, :], 2.0, None, ALU.add), "scan_chain")
                link(dve, nc.vector.reciprocal(s1[:, :], s1[:, :]), "scan_chain")
                link(dve, nc.vector.tensor_tensor(s1[:, :], s1[:, :], u[:, :], ALU.mult), "scan_chain")
                link(dve, nc.vector.tensor_tensor(s2[:, :], s1[:, :], s1[:, :], ALU.mult), "scan_chain")
                link(dve, nc.vector.tensor_scalar(poly[:, :], s2[:, :], 1.0 / 15, None, ALU.mult), "scan_chain")
                for k in (13, 11, 9, 7, 5, 3):
                    link(dve, nc.vector.scalar_tensor_tensor(poly[:, :], poly[:, :], 1.0 / k, s2[:, :], ALU.add, ALU.mult), "scan_chain")
                link(dve, nc.vector.scalar_tensor_tensor(poly[:, :], poly[:, :], 1.0, s1[:, :], ALU.add, ALU.mult), "scan_chain")
                link(dve, nc.vector.scalar_tensor_tensor(delta[:, :], poly[:, :], 2.0, pos[:, :], ALU.mult, ALU.add), "scan_chain")
                nc.vector.tensor_tensor(dx[:, :], delta[:, :], xn[:, :], ALU.mult).then_inc(sem("dx_ready"), 1)
                dve.wait_ge(sem("late_in"), 96)
                link(dve, nc.vector.tensor_tensor(y[:, :], xn[:, :], v["dskip"][:, :], ALU.mult), "scan_chain")
                link(dve, nc.vector.tensor_tensor(res[:, :], res[:, :], y[:, :], ALU.add), "scan_chain")
                dve.wait_ge(sem("ea_done"), 1)

                def decay(n):
                    b = n % 2
                    if n >= 2:
                        dve.wait_ge(sem("logR_done"), n - 1)
                    link(dve, nc.vector.tensor_tensor(cn(la[b][:, :]), over_states(delta[:, n * BD:(n + 1) * BD]),
                                                      cn(ea[:, n * W:(n + 1) * W]), ALU.mult), "scan_chain")
                    nc.vector.tensor_scalar(la[b][:, :], la[b][:, :], -1.0, LOG_EPS, ALU.mult, ALU.max).then_inc(sem("la_ready"), 1)

                def inputs(n):
                    b = n % 2
                    dve.wait_ge(sem("logR_done"), n + 1)
                    if n >= 2:
                        dve.wait_ge(sem("gi_ready"), n - 1)
                    nc.vector.tensor_scalar(inv[b][:, :], bank2(2 * b), -1.0, CLAMP, ALU.mult, ALU.min).then_inc(sem("neg_ready"), 1)
                    dve.wait_ge(sem("g_ready"), n + 1)
                    dve.wait_ge(sem("inv_ready"), n + 1)
                    nc.vector.tensor_tensor(g[b][:, :], g[b][:, :], inv[b][:, :], ALU.mult).then_inc(sem("gi_ready"), 1)

                def outputs(n):
                    b = n % 2
                    dve.wait_ge(sem("sum_done"), n + 1)
                    dve.wait_ge(sem("CR_ready"), n + 1)
                    link(dve, nc.vector.tensor_tensor(inv[b][:, :], bank2(4 + 2 * b), R[b][:, :], ALU.mult), "scan_chain")
                    nc.vector.tensor_reduce(y[:, n * BD:(n + 1) * BD], cn(inv[b][:, :]), AX_X, ALU.add).then_inc(sem("y4_ready"), 1)
                    dve.wait_ge(sem("y4_ready"), n + 1)

                decay(0)
                decay(1)
                for n in range(NB):
                    inputs(n)
                    if n + 2 < NB:
                        decay(n + 2)
                    if n >= 1:
                        outputs(n - 1)
                outputs(NB - 1)
                nc.vector.tensor_tensor(res[:, :], res[:, :], y[:, :], ALU.add).then_inc(sem("res_ready"), 1)

            @block.tensor
            def _(pe):
                norm_tensor(pe, 4)
                pe.wait_ge(sem("late_in"), 96)
                for k in range(KT):
                    mm = nc.tensor.matmul(ps[0:DTR, 4, 0:P], v["wxp"][:, k, 0:DTR], xnT[:, k, :], start=(k == 0), stop=(k == KT - 1))
                for k in range(KT):
                    mm = nc.tensor.matmul(ps[:, 5, 0:2 * NST], xnT[:, k, :], v["wxp"][:, k, DTR:DTR + 2 * NST],
                                          start=(k == 0), stop=(k == KT - 1))
                mm.then_inc(sem("dt_done"), 1)
                nc.tensor.matmul(ps[:, 6, 0:D], ones[0:1, :], v["bdt"][:, :], start=True, stop=False)
                pe.wait_ge(sem("dtT_ready"), 1)
                nc.tensor.matmul(ps[:, 6, 0:D], dtT[:, :], v["wdt"][:, :], start=False, stop=True).then_inc(sem("z_done"), 1)
                pe.wait_ge(sem("bc_ready"), 1)
                pe.wait_ge(sem("absz_ready"), 1)

                def log_R(n):
                    pe.wait_ge(sem("la_ready"), n + 1)
                    if n >= 2:
                        pe.wait_ge(sem("R_ready"), n - 1)
                        pe.wait_ge(sem("neg_ready"), n - 1)
                    for k in range(2):
                        mm = nc.tensor.matmul(ps[:, 2 * (n % 2) + k, :], tri[:, :], la[n % 2][:, k * 512:(k + 1) * 512],
                                              start=True, stop=True)
                    mm.then_inc(sem("logR_done"), 1)

                def sums(n):
                    pe.wait_ge(sem("gi_ready"), n + 1)
                    if n >= 2:
                        pe.wait_ge(sem("y4_ready"), n - 1)
                    for k in range(2):
                        mm = nc.tensor.matmul(ps[:, 4 + 2 * (n % 2) + k, :], tri[:, :], g[n % 2][:, k * 512:(k + 1) * 512],
                                              start=True, stop=True)
                    mm.then_inc(sem("sum_done"), 1)

                log_R(0)
                log_R(1)
                for n in range(NB):
                    sums(n)
                    if n + 2 < NB:
                        log_R(n + 2)


def stage_relu_context(nc, t, sb, sem, link, ps, norms, v):
    norm_vector, norm_scalar, norm_tensor = norms
    res, xnT, ident, ones = v["res"], v["xnT"], v["ident"], v["ones"]
    wx, bx, wd = v["wx"], v["bx"], v["wd"]
    chunks = t["ctxN"].shape[0]
    with ExitStack() as own:
        cT = [sb(f"d_cT{i}", [P, KT, CK], F32, own) for i in range(2)]
        mrow = sb("d_mrow", [1, (chunks + 1) * CK], U8, own)
        mneg = [sb(f"d_mneg{i}", [1, CK], BF16, own) for i in range(2)]
        one_b = sb("d_one", [1, P], BF16, own)
        qT = sb("d_qT", [P, KT, P], F32, own)
        kT = sb("d_kT", [P, KT, CK], F32, own)
        kN = [sb(f"d_kN{i}", [P, NT, D], F32, own) for i in range(2)]
        prob = sb("d_prob", [P, 2, HK], F32, own)
        pT = sb("d_pT", [P, CK], F32, own)
        U = sb("d_U", [P, D], F32, own)
        den = sb("d_den", [P, 1], F32, own)
        rden = sb("d_rden", [P, 1], F32, own)
        nm = sb("d_nm", [P, 2], F32, own)
        nmx = sb("d_nmx", [P, 1], F32, own)
        al = sb("d_al", [P, 2], F32, own)
        rs = sb("d_rs", [P, 2], F32, own)
        S = ps[:, 2:4, 0:HK]
        KG = 2 * KT
        TG_ = (NT + 1) // 2
        PG = [range(0, 4), range(4, NT)]

        with nc.Block() as block:
            @block.sync
            def _(sp):
                sp.dma_start(cT[0][:, :, :], t["ctxT"][0]).then_inc(sem("dctx_in0"), 16)
                sp.dma_start(mrow[:, 0:chunks * CK], t["mask"]).then_inc(sem("dmask_in"), 16)
                sp.dma_start(mrow[:, chunks * CK:(chunks + 1) * CK], t["mask"][:, 0:CK]).then_inc(sem("dmask_in"), 16)
                sp.dma_start(cT[1][:, :, :], t["ctxT"][1]).then_inc(sem("dctx_in1"), 16)
                sp.dma_start(wd[:, :, :], t["wd1"]).then_inc(sem("wd_in"), 16)
                with sp.Fori(1, chunks // 2) as i:
                    for b in range(2):
                        sp.wait_ge(sem("dk_done"), i * (2 * KG) + KG * (b - 1))
                        sp.dma_start(cT[b][:, :, :], t["ctxT"][bass.ds(i * 2 + b, 1)].rearrange(
                            "o p k n -> p (o k) n")).then_inc(sem(f"dctx_in{b}"), 16)
                sp.wait_ge(sem("dk_done"), KG * (chunks - 1))
                sp.dma_start(cT[0][:, :, :], t["ctxT"][0]).then_inc(sem("dctx_in0"), 16)

            @block.scalar
            def _(act):
                norm_scalar(act, 3)
                act.wait_ge(sem("dq_done"), 1)
                act.wait_ge(sem("wx_in"), 32)
                for m in range(KT):
                    nc.scalar.activation(qT[:, m, :], ps[:, 6, m * P:(m + 1) * P], ACT.Relu, bias=bx[:, m:m + 1],
                                         scale=1.0).then_inc(sem("dq_ready"), 1)

                def keys(g):
                    m, half = g // 2, g % 2
                    nc.scalar.activation(kT[:, m, half * HK:(half + 1) * HK], ps[:, g % 2, 0:HK], ACT.Relu,
                                         bias=bx[:, m:m + 1], scale=1.0).then_inc(sem("dkT_ready"), 1)

                def exp_step(b):
                    nc.scalar.activation(al[:, b:b + 1], nm[:, 1 - b:2 - b], ACT.Exp, bias=nm[:, b:b + 1], scale=-1.0)
                    nc.scalar.activation(prob[:, :, :], S, ACT.Exp, bias=nm[:, b:b + 1], scale=1.0,
                                         accum_out=rs[:, b:b + 1]).then_inc(sem("dexp_done"), 1)

                for g in range(KG):
                    act.wait_ge(sem("dk_done"), g + 1)
                    keys(g)
                act.wait_ge(sem("dmax_done"), 1)
                exp_step(0)
                with act.Fori(0, chunks // 2) as i:
                    for b in range(2):
                        act.wait_ge(sem("ds_done"), i * 2 + (b + 1))
                        for g in range(KG):
                            act.wait_ge(sem("dk_done"), i * (2 * KG) + (KG * (b + 1) + g + 1))
                            keys(g)
                        for n, tiles in enumerate(PG):
                            act.wait_ge(sem("dp_turned"), i * 4 + (2 * b + n + 1))
                            cols = slice(tiles[0] * P, (tiles[-1] + 1) * P)
                            nc.scalar.copy(pT[:, cols], ps[:, 4 + n, 0:len(tiles) * P]).then_inc(sem("dpT_ready"), 1)
                        act.wait_ge(sem("dmax_done"), i * 2 + (b + 2))
                        act.wait_ge(sem("du_free"), i * 2 + (b + 2))
                        exp_step(1 - b)

            @block.vector
            def _(dve):
                nc.vector.memset(one_b[:, :], 1.0).then_inc(sem("d_ones"), 1)
                nc.vector.memset(U[:, :], 0.0)
                nc.vector.memset(den[:, :], 0.0)
                nc.vector.memset(nm[:, :], BIG).then_inc(sem("du_free"), 2)
                norm_vector(dve, 3)

                def mask(b, chunk):
                    nc.vector.tensor_scalar(mneg[b][:, :], mrow[:, bass.ds(chunk * CK, CK)], -BIG, None,
                                            ALU.mult).then_inc(sem("dmask_ready"), 1)

                def turned_keys(b, n):
                    k = min(2, NT - 2 * n)
                    nc.vector.tensor_copy(kN[b][:, 2 * n:2 * n + k, :].rearrange("p a d -> p (a d)"),
                                          ps[:, 4 + n % 2, 0:k * D]).then_inc(sem("dkN_ready"), 1)

                def chunk_max():
                    nc.vector.tensor_reduce(nmx[:, :], S, mybir.AxisListType.XY, ALU.max, negate=True).then_inc(sem("dchunk_max"), 1)

                def new_max(b):
                    nc.vector.tensor_tensor(nm[:, b:b + 1], nm[:, 1 - b:2 - b], nmx[:, :], ALU.min).then_inc(sem("dmax_done"), 1)

                dve.wait_ge(sem("dmask_in"), 32)
                mask(0, 0)
                for n in range(TG_):
                    dve.wait_ge(sem("dk_turned"), n + 1)
                    turned_keys(0, n)
                dve.wait_ge(sem("ds_done"), 1)
                chunk_max()
                dve.wait_ge(sem("dchunk_max"), 1)
                new_max(0)
                with dve.Fori(0, chunks // 2) as i:
                    for b in range(2):
                        mask(1 - b, i * 2 + (b + 1))
                        for n in range(TG_):
                            dve.wait_ge(sem("dk_turned"), i * (2 * TG_) + (TG_ * (b + 1) + n + 1))
                            turned_keys(1 - b, n)
                        dve.wait_ge(sem("dmax_done"), i * 2 + (b + 1))
                        dve.wait_ge(sem("ds_done"), i * 2 + (b + 2))
                        chunk_max()
                        dve.wait_ge(sem("dchunk_max"), i * 2 + (b + 2))
                        new_max(1 - b)
                        dve.wait_ge(sem("du_free"), i * 2 + (b + 2))
                        nc.vector.scalar_tensor_tensor(den[:, :], den[:, :], al[:, b:b + 1], rs[:, b:b + 1],
                                                       ALU.mult, ALU.add)
                        dve.wait_ge(sem("dpv_done"), i * 2 + (b + 1))
                        nc.vector.scalar_tensor_tensor(U[:, :], U[:, :], al[:, b:b + 1], ps[:, 6 + b, 0:D],
                                                       ALU.mult, ALU.add).then_inc(sem("du_free"), 1)
                dve.wait_ge(sem("du_free"), chunks + 2)
                link(dve, nc.vector.reciprocal(rden[:, :], den[:, :]), "relu_chain")
                nc.vector.scalar_tensor_tensor(res[:, :], U[:, :], rden[:, 0:1], res[:, :], ALU.mult,
                                               ALU.add).then_inc(sem("res_ready"), 1)

            @block.tensor
            def _(pe):
                norm_tensor(pe, 3)
                pe.wait_ge(sem("wx_in"), 32)
                for m in range(KT):
                    for k in range(KT):
                        mm = nc.tensor.matmul(ps[:, 6, m * P:(m + 1) * P], wx[:, k, m * P:(m + 1) * P], xnT[:, k, :],
                                              start=(k == 0), stop=(k == KT - 1))
                mm.then_inc(sem("dq_done"), 1)

                def keys(b, g):
                    m, half = g // 2, g % 2
                    for k in range(KT):
                        mm = nc.tensor.matmul(ps[:, g % 2, 0:HK], wx[:, k, m * P:(m + 1) * P],
                                              cT[b][:, k, half * HK:(half + 1) * HK], start=(k == 0), stop=(k == KT - 1))
                    mm.then_inc(sem("dk_done"), 1)

                def turn_keys(n):
                    k = min(2, NT - 2 * n)
                    for a in range(k):
                        for m in range(KT):
                            mm = nc.tensor.transpose(ps[:, 4 + n % 2, a * D + m * P:a * D + (m + 1) * P],
                                                     kT[:, m, (2 * n + a) * P:(2 * n + a + 1) * P], ident[:, :])
                    mm.then_inc(sem("dk_turned"), 1)

                def scores(b):
                    for half in range(2):
                        cols = slice(half * HK, (half + 1) * HK)
                        nc.tensor.matmul(S[:, half, :], one_b[:, :], mneg[b][:, cols], start=True, stop=False)
                        for k in range(KT):
                            mm = nc.tensor.matmul(S[:, half, :], qT[:, k, :], kT[:, k, cols], start=False, stop=(k == KT - 1))
                    mm.then_inc(sem("ds_done"), 1)

                pe.wait_ge(sem("dctx_in0"), 16)
                for g in range(KG):
                    if g >= 2:
                        pe.wait_ge(sem("dkT_ready"), g - 1)
                    keys(0, g)
                pe.wait_ge(sem("dkT_ready"), KG)
                for n in range(TG_):
                    if n >= 2:
                        pe.wait_ge(sem("dkN_ready"), n - 1)
                    turn_keys(n)
                pe.wait_ge(sem("dq_ready"), KT)
                pe.wait_ge(sem("d_ones"), 1)
                pe.wait_ge(sem("dmask_ready"), 1)
                scores(0)
                pe.wait_ge(sem("dkN_ready"), TG_)
                with pe.Fori(0, chunks // 2) as i:
                    for b in range(2):
                        pe.wait_ge(sem(f"dctx_in{1 - b}"), i * 16 + 16 * (b + 1))
                        for g in range(KG):
                            if g >= 2:
                                pe.wait_ge(sem("dkT_ready"), i * (2 * KG) + (KG * (b + 1) + g - 1))
                            keys(1 - b, g)
                        pe.wait_ge(sem("dkT_ready"), i * (2 * KG) + KG * (b + 2))
                        for n in range(TG_):
                            if n >= 2:
                                pe.wait_ge(sem("dkN_ready"), i * (2 * TG_) + (TG_ * (b + 1) + n - 1))
                            turn_keys(n)
                        pe.wait_ge(sem("dexp_done"), i * 2 + (b + 1))
                        for n, tiles in enumerate(PG):
                            pe.wait_ge(sem("dkN_ready"), i * (2 * TG_) + (TG_ * (b + 1) + 3 + n))
                            for k in tiles:
                                mm = nc.tensor.transpose(ps[:, 4 + n, (k - tiles[0]) * P:(k - tiles[0] + 1) * P],
                                                         prob[:, :, :].rearrange("p a n -> p (a n)")[:, k * P:(k + 1) * P],
                                                         ident[:, :])
                            mm.then_inc(sem("dp_turned"), 1)
                        pe.wait_ge(sem("dmask_ready"), i * 2 + (b + 2))
                        scores(1 - b)
                        pe.wait_ge(sem("du_free"), i * 2 + (b + 1))
                        for n, tiles in enumerate(PG):
                            pe.wait_ge(sem("dpT_ready"), i * 4 + (2 * b + n + 1))
                            for k in tiles:
                                mm = nc.tensor.matmul(ps[:, 6 + b, 0:D], pT[:, k * P:(k + 1) * P], kN[b][:, k, :],
                                                      start=(k == 0), stop=(k == NT - 1))
                        mm.then_inc(sem("dpv_done"), 1)


def rank_select(nc, dve, link, name, val, n, k, wins, ties, rank, sel, below):
    by_i = val.unsqueeze(2).broadcast_to([P, n, n])
    by_j = val.unsqueeze(1).broadcast_to([P, n, n])
    nc.vector.tensor_tensor(wins, by_j, by_i, ALU.is_gt)
    link(dve, nc.vector.tensor_tensor(ties, by_j, by_i, ALU.is_equal), name)
    link(dve, nc.vector.tensor_tensor(ties, ties, below[:, 0:n, 0:n], ALU.mult), name)
    link(dve, nc.vector.tensor_tensor(wins, wins, ties, ALU.add), name)
    link(dve, nc.vector.tensor_reduce(rank, wins, AX_X, ALU.add), name)
    link(dve, nc.vector.tensor_scalar(sel, rank, float(k), None, ALU.is_lt), name)


def stage_mix0(nc, t, sb, sem, link, ps, norms, v):
    norm_vector, norm_scalar, norm_tensor = norms
    res, xnT, ident = v["res"], v["xnT"], v["ident"]
    w1, w2, b1 = v["w1"], v["w2"], v["b1"]
    FT = F0 // P
    with ExitStack() as own:
        h = sb("c_h", [P, E0, F0], F32, own)
        hT = sb("c_hT", [P, 2 * FT, P], F32, own)
        lg = sb("c_lg", [P, E0], F32, own)
        ex = sb("c_ex", [P, E0], F32, own)
        sel = sb("c_sel", [P, E0], F32, own)
        rank = sb("c_rank", [P, E0], F32, own)
        comb = sb("c_comb", [P, E0], F32, own)
        one = sb("c_one", [P, 4], F32, own)
        wins = sb("c_wins", [P, E0, E0], F32, own)
        ties = sb("c_ties", [P, E0, E0], F32, own)
        combT = sb("c_combT", [E0, P], F32, own)

        with nc.Block() as block:
            @block.vector
            def _(dve):
                norm_vector(dve, 2)
                dve.wait_ge(sem("logits0_done"), 1)
                dve.wait_ge(sem("router0_in"), 48)
                link(dve, nc.vector.tensor_tensor(lg[:, :], ps[:, 6, 0:E0], v["bg"][:, :], ALU.add), "mix0_chain")
                nc.vector.tensor_reduce(one[:, 0:1], lg[:, :], AX_X, ALU.max, negate=True).then_inc(sem("lmax0_ready"), 1)
                dve.wait_ge(sem("lexp0_ready"), 1)
                link(dve, nc.vector.reciprocal(one[:, 2:3], one[:, 1:2]), "mix0_chain")
                link(dve, nc.vector.tensor_scalar(ex[:, :], ex[:, :], one[:, 2:3], None, ALU.mult), "mix0_chain")
                rank_select(nc, dve, link, "mix0_chain", ex[:, :], E0, 2, wins[:, :, :], ties[:, :, :], rank[:, :],
                            sel[:, :], v["below"])
                link(dve, nc.vector.tensor_tensor(ex[:, :], ex[:, :], sel[:, :], ALU.mult), "mix0_chain")
                link(dve, nc.vector.tensor_reduce(one[:, 3:4], ex[:, :], AX_X, ALU.add), "mix0_chain")
                link(dve, nc.vector.reciprocal(one[:, 3:4], one[:, 3:4]), "mix0_chain")
                nc.vector.tensor_scalar(comb[:, :], ex[:, :], one[:, 3:4], None, ALU.mult).then_inc(sem("comb0_ready"), 1)
                dve.wait_ge(sem("comb0_ready"), 1)
                dve.wait_ge(sem("b1_in"), 16)
                for e in range(E0):
                    dve.wait_ge(sem("h0_done"), e + 1)
                    nc.vector.tensor_tensor(h[:, e, :], ps[:, e % 4, :], b1[:, e, :], ALU.add).then_inc(sem("h0_biased"), 1)
                    dve.wait_ge(sem("h0_biased"), e + 1)
                    nc.vector.tensor_scalar(h[:, e, :], h[:, e, :], 0.0, comb[:, e:e + 1], ALU.max,
                                            ALU.mult).then_inc(sem("h0_ready"), 1)
                dve.wait_ge(sem("comb0_turned"), 1)
                nc.vector.tensor_copy(combT[:, :], ps[0:E0, 6, P:2 * P]).then_inc(sem("combT_ready"), 1)
                dve.wait_ge(sem("y2_done"), 1)
                nc.vector.tensor_tensor(res[:, :], res[:, :], ps[:, 7, 0:D], ALU.add).then_inc(sem("res_ready"), 1)

            @block.scalar
            def _(act):
                norm_scalar(act, 2)
                act.wait_ge(sem("lmax0_ready"), 1)
                nc.scalar.activation(ex[:, :], lg[:, :], ACT.Exp, bias=one[:, 0:1], scale=1.0,
                                     accum_out=one[:, 1:2]).then_inc(sem("lexp0_ready"), 1)
                for e in range(E0):
                    act.wait_ge(sem("h0_turned"), e + 1)
                    nc.scalar.copy(hT[:, e % 2 * FT:(e % 2 + 1) * FT, :].rearrange("p f q -> p (f q)"),
                                   ps[:, 4 + e % 2, :]).then_inc(sem("hT0_ready"), 1)

            @block.tensor
            def _(pe):
                norm_tensor(pe, 2)
                pe.wait_ge(sem("router0_in"), 48)
                for k in range(KT):
                    mm = nc.tensor.matmul(ps[:, 6, 0:E0], xnT[:, k, :], v["wg0"][:, k, :], start=(k == 0), stop=(k == KT - 1))
                mm.then_inc(sem("logits0_done"), 1)

                def hidden(e):
                    for k in range(KT):
                        mm = nc.tensor.matmul(ps[:, e % 4, :], xnT[:, k, :], w1[:, k, e, :], start=(k == 0), stop=(k == KT - 1))
                    mm.then_inc(sem("h0_done"), 1)

                def down(e):
                    pe.wait_ge(sem("hT0_ready"), e + 1)
                    for f in range(FT):
                        nc.tensor.matmul(ps[:, 7, 0:D], hT[:, e % 2 * FT + f, :], w2[:, e * FT + f, :],
                                         start=(e == 0 and f == 0), stop=False)

                pe.wait_ge(sem("w1_in"), 16)
                for e in range(4):
                    hidden(e)
                pe.wait_ge(sem("w2_in"), 16)
                for e in range(E0):
                    pe.wait_ge(sem("h0_ready"), e + 1)
                    for f in range(FT):
                        mm = nc.tensor.transpose(ps[:, 4 + e % 2, f * P:(f + 1) * P], h[:, e, f * P:(f + 1) * P], ident[:, :])
                    mm.then_inc(sem("h0_turned"), 1)
                    if e + 4 < E0:
                        hidden(e + 4)
                    if e > 0:
                        down(e - 1)
                nc.tensor.transpose(ps[0:E0, 6, P:2 * P], comb[:, :], ident[:, :]).then_inc(sem("comb0_turned"), 1)
                down(E0 - 1)
                pe.wait_ge(sem("combT_ready"), 1)
                nc.tensor.matmul(ps[:, 7, 0:D], combT[:, :], v["b2"][:, :], start=False, stop=True).then_inc(sem("y2_done"), 1)


def stage_band(nc, t, sb, sem, link, ps, norms, v):
    norm_vector, norm_scalar, norm_tensor = norms
    res, xnT, ident, ones, row0, hmask, dist = (v[n] for n in ("res", "xnT", "ident", "ones", "row0", "hmask", "dist"))
    SCALE = DH1 ** -0.5
    MAX_W, MIN_W = 120.0, 24.0
    with ExitStack() as own:
        qT = sb("b_qT", [P, KT, P], F32, own)
        kT = sb("b_kT", [P, KT, P], F32, own)
        kx = sb("b_kx", [P, KT, HPT, P], F32, own)
        val = sb("b_v", [P, D], F32, own)
        s = sb("b_s", [P, H1, P], F32, own)
        sT = kx[:, :, :, :].rearrange("p m h q -> p (m h) q")
        band = sb("b_band", [P, P], F32, own)
        diff = sb("b_diff", [P, KT], F32, own)
        flu = sb("b_flu", [P, KT], F32, own)
        sg = sb("b_sg", [P, 10], F32, own)
        mx = sb("b_mx", [P, H1], F32, own)
        sm = sb("b_sm", [P, H1], F32, own)
        rd = sb("b_rd", [P, H1], F32, own)
        o = sb("b_o", [P, D], F32, own)
        oT = sb("b_oT", [P, KT, P], F32, own)
        o2T = sb("b_o2T", [P, KT, P], F32, own)
        wox = sb("b_wox", [P, KT, HPT, DH1], F32, own)

        def by_head(x):
            return x.rearrange("p (h d) -> p h d", h=H1)

        with nc.Block() as block:
            @block.sync
            def _(sp):
                sp.dma_start(v["wg0"][:, :, :], t["wg0"]).then_inc(sem("router0_in"), 16)
                sp.dma_start(v["bg"][:, :], t["bg"].partition_broadcast(P)).then_inc(sem("router0_in"), 16)
                sp.dma_start(v["b2"][:, :], t["b2"]).then_inc(sem("router0_in"), 16)
                sp.dma_start(v["w1"][:, :, :, :], t["w1"]).then_inc(sem("w1_in"), 16)
                sp.dma_start(v["b1"][:, :, :].rearrange("p e f -> p (e f)"), t["b1"].partition_broadcast(P)).then_inc(sem("b1_in"), 16)
                sp.dma_start(v["w2"][:, :, :], t["w2"]).then_inc(sem("w2_in"), 16)
                sp.dma_start(v["wx"][:, :, :], t["wx"]).then_inc(sem("wx_in"), 16)
                sp.dma_start(v["bx"][:, :], t["bx"]).then_inc(sem("wx_in"), 16)
                sp.dma_start(v["wxp"][:, :, :], t["wxp"]).then_inc(sem("late_in"), 16)
                sp.dma_start(v["wdt"][:, :], t["wdt"]).then_inc(sem("late_in"), 16)
                sp.dma_start(v["bdt"][:, :], t["bdt"]).then_inc(sem("late_in"), 16)
                sp.dma_start(v["dskip"][:, :], t["dskip"].partition_broadcast(P)).then_inc(sem("late_in"), 16)
                sp.dma_start(v["wr1"][:, :, :], t["wr1"]).then_inc(sem("late_in"), 16)
                sp.dma_start(v["br1"][:, :], t["br1"].partition_broadcast(P)).then_inc(sem("late_in"), 16)
                sp.dma_start(v["wg"][:, :, :], t["wg1"]).then_inc(sem("mix1_in"), 16)
                sp.dma_start(v["wu"][:, :, :], t["wu1"]).then_inc(sem("mix1_in"), 16)

            @block.vector
            def _(dve):
                norm_vector(dve, 1)
                dve.wait_ge(sem("consts_ready"), 1)
                dve.wait_ge(sem("band_in"), 112)
                dve.wait_ge(sem("xnT_ready"), 2)
                link(dve, nc.vector.tensor_tensor(diff[:, :], xnT[:, :, P - 1], xnT[:, :, P - 2], ALU.subtract), "band_chain")
                nc.vector.scalar_tensor_tensor(flu[:, :], diff[:, :], -1.0, diff[:, :], ALU.mult,
                                               ALU.max).then_inc(sem("fluct_ready"), 1)
                nc.vector.tensor_tensor(dist[:, :], v["disti"][:, 0, :], v["disti"][:, 1, :], ALU.max)
                for m in range(KT):
                    nc.vector.tensor_tensor(wox[:, m, :, :], v["awo"][:, m, :].unsqueeze(1).broadcast_to([P, HPT, DH1]),
                                            hmask[:, :].unsqueeze(2).broadcast_to([P, HPT, DH1]),
                                            ALU.mult).then_inc(sem("wox_ready"), 1)
                dve.wait_ge(sem("qk1_done"), 1)
                for m in range(KT):
                    nc.vector.tensor_scalar(qT[:, m, :], ps[:, 0, m * P:(m + 1) * P], v["abqk"][:, m:m + 1], None,
                                            ALU.add).then_inc(sem("qk1_ready"), 1)
                    link(dve, nc.vector.tensor_scalar(kT[:, m, :], ps[:, 0, D + m * P:D + (m + 1) * P],
                                                      v["abqk"][:, KT + m:KT + m + 1], None, ALU.add), "band_chain")
                    nc.vector.tensor_tensor(kx[:, m, :, :], kT[:, m, :].unsqueeze(1).broadcast_to([P, HPT, P]),
                                            hmask[:, :].unsqueeze(2).broadcast_to([P, HPT, P]),
                                            ALU.mult).then_inc(sem("qk1_ready"), 1)
                dve.wait_ge(sem("ea_ready"), 1)
                link(dve, nc.vector.tensor_scalar(sg[:, 1:2], sg[:, 0:1], 1.0, None, ALU.add), "band_chain")
                link(dve, nc.vector.reciprocal(sg[:, 2:3], sg[:, 1:2]), "band_chain")
                link(dve, nc.vector.tensor_scalar(sg[:, 3:4], sg[:, 2:3], -1.0, 1.0, ALU.mult, ALU.add), "band_chain")
                dve.wait_ge(sem("fluct_sum"), 1)
                link(dve, nc.vector.tensor_scalar(sg[:, 4:5], ps[:, 6, 0:1], 1.0 / D, None, ALU.mult), "band_chain")
                link(dve, nc.vector.tensor_tensor(sg[:, 5:6], sg[:, 4:5], sg[:, 2:3], ALU.mult), "band_chain")
                nc.vector.scalar_tensor_tensor(sg[:, 6:7], ps[:, 6, 1:2], sg[:, 3:4], sg[:, 5:6], ALU.mult,
                                               ALU.add).then_inc(sem("signal_ready"), 1)
                dve.wait_ge(sem("es_ready"), 1)
                link(dve, nc.vector.tensor_scalar(sg[:, 8:9], sg[:, 7:8], 1.0, None, ALU.add), "band_chain")
                link(dve, nc.vector.reciprocal(sg[:, 8:9], sg[:, 8:9]), "band_chain")
                link(dve, nc.vector.tensor_scalar(sg[:, 9:10], sg[:, 8:9], MAX_W - MIN_W, MIN_W, ALU.mult, ALU.add), "band_chain")
                link(dve, nc.vector.tensor_scalar(band[:, :], dist[:, :], sg[:, 9:10], -BIG, ALU.is_gt, ALU.mult), "band_chain")
                dve.wait_ge(sem("s1_done"), 1)
                link(dve, nc.vector.scalar_tensor_tensor(s[:, :, :], ps[:, 2:6, :].rearrange("p b (h q) -> p (b h) q", h=4),
                                                         SCALE, band[:, :].unsqueeze(1).broadcast_to([P, H1, P]),
                                                         ALU.mult, ALU.add), "band_chain")
                link(dve, nc.vector.tensor_reduce(mx[:, :], s[:, :, :], AX_X, ALU.max), "band_chain")
                nc.vector.tensor_tensor(s[:, :, :], s[:, :, :], mx[:, :].unsqueeze(2).broadcast_to([P, H1, P]),
                                        ALU.subtract).then_inc(sem("s1_shifted"), 1)
                dve.wait_ge(sem("v1_done"), 1)
                nc.vector.tensor_copy(val[:, :], ps[:, 1, 0:D]).then_inc(sem("v1_ready"), 1)
                dve.wait_ge(sem("p1_ready"), 1)
                link(dve, nc.vector.tensor_reduce(sm[:, :], s[:, :, :], AX_X, ALU.add), "band_chain")
                link(dve, nc.vector.reciprocal(rd[:, :], sm[:, :]), "band_chain")
                dve.wait_ge(sem("p1_turned"), 2)
                nc.vector.tensor_copy(sT[:, 8:16, :], ps[:, 4:6, :].rearrange("p b (h q) -> p (b h) q", h=4)).then_inc(
                    sem("p1T_b"), 1)
                dve.wait_ge(sem("o1_done"), 1)
                nc.vector.tensor_tensor(by_head(o[:, :]), by_head(ps[:, 6, 0:D]),
                                        rd[:, :].unsqueeze(2).broadcast_to([P, H1, DH1]),
                                        ALU.mult).then_inc(sem("o1_ready"), 1)
                dve.wait_ge(sem("o1_turned"), 1)
                nc.vector.tensor_copy(oT[:, :, :], ps[:, 7, 0:D].rearrange("p (k q) -> p k q", k=KT)).then_inc(sem("o1T_ready"), 1)
                dve.wait_ge(sem("o2_done"), 1)
                nc.vector.tensor_copy(o2T[:, :, :], ps[:, 0, 0:D].rearrange("p (k q) -> p k q", k=KT)).then_inc(sem("o2T_ready"), 1)
                dve.wait_ge(sem("y1_done"), 1)
                nc.vector.tensor_tensor(res[:, :], res[:, :], ps[:, 1, 0:D], ALU.add).then_inc(sem("res_ready"), 1)

            @block.scalar
            def _(act):
                norm_scalar(act, 1)
                act.wait_ge(sem("band_in"), 112)
                nc.scalar.activation(sg[:, 0:1], v["alpha"][:, :], ACT.Exp, scale=-1.0).then_inc(sem("ea_ready"), 1)
                act.wait_ge(sem("signal_ready"), 1)
                nc.scalar.activation(sg[:, 7:8], sg[:, 6:7], ACT.Exp, scale=-1.0).then_inc(sem("es_ready"), 1)
                act.wait_ge(sem("s1_shifted"), 1)
                nc.scalar.activation(s[:, :, :], s[:, :, :], ACT.Exp).then_inc(sem("p1_ready"), 1)
                act.wait_ge(sem("p1_turned"), 1)
                nc.scalar.copy(sT[:, 0:8, :], ps[:, 2:4, :].rearrange("p b (h q) -> p (b h) q", h=4)).then_inc(sem("p1T_a"), 1)

            @block.tensor
            def _(pe):
                norm_tensor(pe, 1)
                pe.wait_ge(sem("band_in"), 112)
                for w, col in ((v["aq"], 0), (v["ak"], D)):
                    for m in range(KT):
                        for k in range(KT):
                            mm = nc.tensor.matmul(ps[:, 0, col + m * P:col + (m + 1) * P], w[:, k, m * P:(m + 1) * P],
                                                  xnT[:, k, :], start=(k == 0), stop=(k == KT - 1))
                mm.then_inc(sem("qk1_done"), 1)
                pe.wait_ge(sem("fluct_ready"), 1)
                for k in range(KT):
                    nc.tensor.matmul(ps[:, 6, 0:1], ones[:, :], flu[:, k:k + 1], start=(k == 0), stop=(k == KT - 1))
                nc.tensor.matmul(ps[:, 6, 1:2], row0[:, :], flu[:, 0:1], start=True, stop=True).then_inc(sem("fluct_sum"), 1)
                nc.tensor.matmul(ps[:, 1, 0:D], ones[0:1, :], v["brow"][0:1, D:2 * D], start=True, stop=False)
                for k in range(KT):
                    mm = nc.tensor.matmul(ps[:, 1, 0:D], xnT[:, k, :], v["av"][:, k, :], start=False, stop=(k == KT - 1))
                mm.then_inc(sem("v1_done"), 1)
                for m in range(KT):
                    pe.wait_ge(sem("qk1_ready"), 2 * m + 2)
                    for half in range(2):
                        mm = nc.tensor.matmul(ps[:, 2 + 2 * m + half, :], qT[:, m, :],
                                              kx[:, m, 4 * half:4 * half + 4, :].rearrange("p h q -> p (h q)"),
                                              start=True, stop=True)
                mm.then_inc(sem("s1_done"), 1)
                pe.wait_ge(sem("p1_ready"), 1)
                for h in range(H1):
                    mm = nc.tensor.transpose(ps[:, 2 + h // 4, (h % 4) * P:(h % 4 + 1) * P], s[:, h, :], ident[:, :])
                    if h % 8 == 7:
                        mm.then_inc(sem("p1_turned"), 1)
                pe.wait_ge(sem("v1_ready"), 1)
                for h in range(H1):
                    if h % 8 == 0:
                        pe.wait_ge(sem("p1T_a" if h == 0 else "p1T_b"), 1)
                    mm = nc.tensor.matmul(ps[:, 6, h * DH1:(h + 1) * DH1], sT[:, h, :], val[:, h * DH1:(h + 1) * DH1],
                                          start=True, stop=True)
                mm.then_inc(sem("o1_done"), 1)
                pe.wait_ge(sem("o1_ready"), 1)
                for k in range(KT):
                    mm = nc.tensor.transpose(ps[:, 7, k * P:(k + 1) * P], o[:, k * P:(k + 1) * P], ident[:, :])
                mm.then_inc(sem("o1_turned"), 1)
                pe.wait_ge(sem("wox_ready"), KT)
                pe.wait_ge(sem("o1T_ready"), 1)
                for m in range(KT):
                    mm = nc.tensor.matmul(ps[:, 0, m * P:(m + 1) * P], wox[:, m, :, :].rearrange("p h d -> p (h d)"),
                                          oT[:, m, :], start=True, stop=True)
                mm.then_inc(sem("o2_done"), 1)
                pe.wait_ge(sem("o2T_ready"), 1)
                nc.tensor.matmul(ps[:, 1, 0:D], ones[0:1, :], v["brow"][0:1, 2 * D:3 * D], start=True, stop=False)
                for k in range(KT):
                    mm = nc.tensor.matmul(ps[:, 1, 0:D], o2T[:, k, :], v["afc"][:, k, :], start=False, stop=(k == KT - 1))
                mm.then_inc(sem("y1_done"), 1)


def layout(inputs):
    import numpy as np

    a = {k: np.asarray(x) for k, x in inputs.items()}

    def rows(w):
        return w.reshape(w.shape[0] // P, P, -1).transpose(1, 0, 2)

    def cols(b):
        return b.reshape(-1, P).T

    def side_by_side(routed, shared):
        return rows(np.concatenate([a[routed].reshape(E1 * F1, D), a[shared]], 0).T)

    ctx = a["ctx_1024"][0]
    n = ctx.shape[0] // CK
    t = {
        "x": a["x"][0],
        "ctxN": ctx.reshape(n, NT, P, D).transpose(0, 2, 1, 3),
        "ctxT": ctx.reshape(n, CK, KT, P).transpose(0, 3, 2, 1),
        "wq0": rows(a["L0_xattn_Wq"]),
        "wkT0": a["L0_xattn_Wkv"][:, :H0 * DH0].reshape(D, H0, DH0).transpose(2, 1, 0),
        "wv0": rows(a["L0_xattn_Wkv"][:, H0 * DH0:]),
        "wo0": a["L0_xattn_Wo"].reshape(H0, DH0, D).transpose(1, 0, 2),
        "brow": np.concatenate([a["L0_xattn_bo"], a["L0_attn_bv"], a["L0_attn_bfc"]])[None, :],
        "aq": rows(a["L0_attn_Wq"]), "ak": rows(a["L0_attn_Wk"]), "av": rows(a["L0_attn_Wv"]),
        "afc": rows(a["L0_attn_Wfc"]), "awo": rows(a["L0_attn_W_o"].reshape(D, DH1)),
        "abqk": np.concatenate([cols(a["L0_attn_bq"]), cols(a["L0_attn_bk"])], 1),
        "alpha": a["L0_attn_alpha"].reshape(1),
        "wg0": rows(a["L0_ffn_Wg"]), "bg": a["L0_ffn_bg"], "b2": a["L0_ffn_b2"],
        "w1": a["L0_ffn_W1"].reshape(E0, KT, P, F0).transpose(2, 1, 0, 3), "b1": a["L0_ffn_b1"].reshape(-1),
        "w2": rows(a["L0_ffn_W2"].reshape(E0 * F0, D)),
        "wx": rows(a["L1_xattn_W"].T), "bx": cols(a["L1_xattn_b"]),
        "mask": a["mask_BxS2_bk0"].reshape(-1)[None, :],
        "wxp": rows(a["L1_attn_W_xproj"]), "wdt": a["L1_attn_W_dt"], "bdt": a["L1_attn_b_dt"][None, :],
        "dskip": a["L1_attn_D"], "alog": a["L1_attn_A_log"].reshape(-1),
        "wr1": rows(a["L1_ffn_gate_w"].T), "br1": a["L1_ffn_gate_bias"],
        "wg1": side_by_side("L1_ffn_expert_gate", "L1_ffn_shared_gate"),
        "wu1": side_by_side("L1_ffn_expert_up", "L1_ffn_shared_up"),
        "wd1": np.concatenate([a["L1_ffn_expert_down"].transpose(2, 0, 1),
                               a["L1_ffn_shared_down"].reshape(D, NS1, F1).transpose(2, 1, 0)], 1),
    }
    return {k: np.ascontiguousarray(x) for k, x in t.items()}


def kernel(**inputs):
    import numpy as np
    import concourse.bacc as _bacc
    from concourse import mybir as _mybir
    from concourse.bass_utils import run_bass_kernel_spmd as _run

    arrays = layout(inputs)
    nc = _bacc.Bacc("TRN2", target_bir_lowering=False, num_devices=1)
    t = {}
    for name, a in arrays.items():
        t[name] = nc.dram_tensor(f"in_{name}", a.shape, _mybir.dt.from_np(a.dtype), kind="ExternalInput").ap()
    out = nc.dram_tensor("out", (P, D), F32, kind="ExternalOutput").ap()
    build(nc, t, out)
    r = _run(nc, [{f"in_{k}": a for k, a in arrays.items()}], core_ids=[0])
    return np.asarray(r.results[0]["out"]).reshape(1, P, D)
```

```python
from contextlib import ExitStack

import concourse.bass as bass
from concourse import mybir

F32 = mybir.dt.float32
F32R = mybir.dt.float32r
BF16 = mybir.dt.bfloat16
I32 = mybir.dt.int32
U8 = mybir.dt.uint8
ALU = mybir.AluOpType
ACT = mybir.ActivationFunctionType
AX_X = mybir.AxisListType.X

P = 128
D = 256
KT = D // P
EPS = 1e-5
BIG = 1e30
NT = 7
CK = NT * P
HK = CK // 2
H0, DH0 = 16, 64
H1, DH1 = 16, 16
HPT = P // DH1
E0, F0 = 8, 512
E1, F1 = 32, 128
NS1 = 2
EA = E1 + NS1
GR, TG, TE = 4, 2, 8
NST, DTR = 16, 64


def build(nc, t, out):
    with ExitStack() as top:
        def sb(name, shape, dt=F32, ctx=top):
            return ctx.enter_context(nc.sbuf_tensor(name, shape, dt))

        ps = top.enter_context(nc.psum_tensor("ps", [P, 8, 512], F32))
        named = {}

        def sem(name):
            if name not in named:
                named[name] = top.enter_context(nc.semaphore(name))
            return named[name]

        count = {}

        def link(eng, ins, name):
            count[name] = count.get(name, 0) + 1
            ins.then_inc(sem(name), 1)
            eng.wait_ge(sem(name), count[name])

        v = {}

        def keep(name, shape, dt=F32):
            v[name] = sb(name, shape, dt)
            return v[name]

        res = keep("res", [P, D])
        xn = keep("xn", [P, D])
        xnT = keep("xnT", [P, KT, P])
        st6 = keep("st6", [P, 6])
        mv = keep("mv", [P, 2])
        vare = keep("vare", [P, 1])
        sd = keep("sd", [P, 1])
        rstd = keep("rstd", [P, 1])
        ident = keep("ident", [P, P])
        keep("ones", [P, P])
        keep("row0", [P, P])
        keep("tri", [P, P])
        keep("hmask", [P, HPT])
        keep("below", [P, E1, E1])
        keep("disti", [P, 2, P], I32)
        keep("dist", [P, P])
        keep("brow", [1, 3 * D])
        for name in ("aq", "ak", "av", "afc"):
            keep(name, [P, KT, D])
        keep("awo", [P, KT, DH1])
        keep("abqk", [P, 2 * KT])
        keep("alpha", [P, 1])
        keep("zero", [P, 1])
        keep("wg0", [P, KT, E0])
        keep("bg", [P, E0])
        keep("b2", [E0, D])
        keep("wx", [P, KT, D])
        keep("bx", [P, KT])
        keep("wxp", [P, KT, DTR + 2 * NST])
        keep("wdt", [DTR, D])
        keep("bdt", [1, D])
        keep("dskip", [P, D])
        keep("wr1", [P, KT, E1])
        keep("br1", [P, E1])

        def norm_vector(dve, n):
            if n > 0:
                dve.wait_ge(sem("res_ready"), n)
            link(dve, nc.vector.bn_stats(st6[:, :], res[:, :]), "norm_chain")
            link(dve, nc.vector.bn_aggr(mv[:, :], st6[:, :]), "norm_chain")
            nc.vector.tensor_scalar(vare[:, :], mv[:, 1:2], EPS, None, ALU.add).then_inc(sem("var_ready"), 1)
            dve.wait_ge(sem("sd_ready"), n + 1)
            link(dve, nc.vector.reciprocal(rstd[:, :], sd[:, :]), "norm_chain")
            nc.vector.tensor_scalar(xn[:, :], res[:, :], mv[:, 0:1], rstd[:, 0:1], ALU.subtract,
                                    ALU.mult).then_inc(sem("xn_ready"), 1)
            dve.wait_ge(sem("xn_turned"), n + 1)
            nc.vector.tensor_copy(xnT[:, :, :], ps[:, 7, 0:D].rearrange("p (k q) -> p k q", k=KT)).then_inc(
                sem("xnT_ready"), 1)

        def norm_scalar(act, n):
            act.wait_ge(sem("var_ready"), n + 1)
            nc.scalar.activation(sd[:, :], vare[:, :], ACT.Sqrt).then_inc(sem("sd_ready"), 1)

        def norm_tensor(pe, n):
            pe.wait_ge(sem("xn_ready"), n + 1)
            for k in range(KT):
                mm = nc.tensor.transpose(ps[:, 7, k * P:(k + 1) * P], xn[:, k * P:(k + 1) * P], ident[:, :])
            mm.then_inc(sem("xn_turned"), 1)
            pe.wait_ge(sem("xnT_ready"), n + 1)

        norms = (norm_vector, norm_scalar, norm_tensor)
        stage_context(nc, t, sb, sem, link, ps, norms, v)
        with ExitStack() as experts:
            v["wg"] = sb("wg", [P, KT, EA * F1], F32, experts)
            v["wu"] = sb("wu", [P, KT, EA * F1], F32, experts)
            with ExitStack() as first:
                v["w1"] = sb("w1", [P, KT, E0, F0], F32, first)
                v["w2"] = sb("w2", [P, E0 * F0 // P, D], F32, first)
                v["b1"] = sb("b1", [P, E0, F0], F32, first)
                stage_band(nc, t, sb, sem, link, ps, norms, v)
                stage_mix0(nc, t, sb, sem, link, ps, norms, v)
            stage_relu_context(nc, t, sb, sem, link, ps, norms, v)
            v["wd"] = sb("wd", [P, EA, D], F32, experts)
            stage_scan(nc, t, sb, sem, link, ps, norms, v)
            stage_mix1(nc, t, sb, sem, link, ps, norms, v)
            finish(nc, sem, res, out, 6)


def finish(nc, sem, res, out, stages):
    with nc.Block() as block:
        @block.sync
        def _(sp):
            sp.wait_ge(sem("res_ready"), stages)
            sp.dma_start(out[:, :], res[:, :]).then_inc(sem("out_stored"), 16)
            sp.wait_ge(sem("out_stored"), 16)


def by_pair(x):
    return x[:, :, :].rearrange("p (m s) q -> p m s q", s=2)


def q_ps(ps):
    return ps[:, 0:2, :].rearrange("p b (m q) -> p (b m) q", q=P)


def stage_context(nc, t, sb, sem, link, ps, norms, v):
    norm_vector, norm_scalar, norm_tensor = norms
    res, xnT, ident, ones = v["res"], v["xnT"], v["ident"], v["ones"]
    chunks = t["ctxN"].shape[0]
    pairs = chunks // 2
    steps = H0 * 2
    last = pairs - 1
    PIECES = H0
    FIRST = 6
    SCALE = DH0 ** -0.5
    W = H0 * DH0
    with ExitStack() as keep:
        U = sb("U", [P, H0, D], F32, keep)
        den = sb("den", [P, H0], F32, keep)
        with ExitStack() as loop:
            flat = U[:, :, :].rearrange("p h d -> p (h d)")
            wq = flat[:, 0:KT * W].rearrange("p (k n) -> p k n", k=KT)
            wk = flat[:, KT * W:2 * KT * W].rearrange("p (k n) -> p k n", k=KT)
            qh = sb("qh", [P, H0, P], F32R, loop)
            ql = sb("ql", [P, H0, P], F32R, loop)
            K = sb("K", [P, H0, CK], F32R, loop)
            raw = sb("raw", [P, CK * KT], F32, loop)
            rawT = raw[:, :].rearrange("p (k n) -> p k n", k=KT)
            rawN = raw[:, :].rearrange("p (t d) -> p t d", t=NT)
            cTh = [sb(f"cTh{i}", [P, KT, CK], F32R, loop) for i in range(2)]
            cTl = [sb(f"cTl{i}", [P, KT, CK], F32R, loop) for i in range(2)]
            cNh = [sb(f"cNh{i}", [P, NT, D], F32R, loop) for i in range(2)]
            cNl = [sb(f"cNl{i}", [P, NT, D], F32R, loop) for i in range(2)]
            prob = sb("prob", [P, 2, HK], F32, loop)
            pTh = sb("pTh", [P, CK], F32R, loop)
            pTl = sb("pTl", [P, CK], F32R, loop)
            nm = sb("nm", [P, 2, H0], F32, loop)
            nmx = sb("nmx", [P, 1], F32, loop)
            al = sb("al", [P, 2], F32, loop)
            rs = sb("rs", [P, 2], F32, loop)
            rden = sb("rden", [P, H0], F32, loop)
            with ExitStack() as keys:
                wkh = sb("wkh", [P, KT, W], F32R, keys)
                wkl = sb("wkl", [P, KT, W], F32R, keys)
            wv = sb("wv", [P, KT, W], F32, loop)
            wo = sb("wo", [P, H0 // 2, D], F32, loop)
            UT = raw[:, 0:2 * D].rearrange("p (s k q) -> p s k q", s=2, k=KT)
            oT = raw[:, 2 * D:2 * D + H0 // 2 * P].rearrange("p (m q) -> p m q", q=P)

            S = [ps[:, 2 * i:2 * i + 2, 0:HK] for i in range(2)]
            pT_ps = ps[:, 4:6, :].rearrange("p b n -> p (b n)")[:, 0:CK]
            O = ps[:, 6, 0:D]
            halves = (slice(0, DH0), slice(DH0, P))

            def piece_bank(g, first):
                return 4 + g % 4 if first else 7

            def piece_of(g, s):
                return 2 * (g // 2) + s, slice((g % 2) * HK, (g % 2 + 1) * HK)

            with nc.Block() as block:
                @block.sync
                def _(sp):
                    sp.dma_start(res[:, :], t["x"]).then_inc(sem("x_in"), 16)
                    sp.dma_start(wq, t["wq0"]).then_inc(sem("wq_in"), 16)
                    sp.dma_start(rawT[:, :, :], t["ctxT"][0]).then_inc(sem("rawT_in"), 16)
                    sp.dma_start(wk, t["wk0"]).then_inc(sem("wk_in"), 16)
                    sp.wait_ge(sem("cT_ready"), 1)
                    sp.dma_start(rawN[:, :, :], t["ctxN"][0]).then_inc(sem("rawN_in"), 16)
                    with sp.Fori(1, chunks) as c:
                        sp.wait_ge(sem("cN_ready"), c)
                        sp.dma_start(rawT[:, :, :], t["ctxT"][bass.ds(c, 1)].rearrange("o p k n -> p (o k) n")).then_inc(sem("rawT_in"), 16)
                        sp.wait_ge(sem("cT_ready"), c + 1)
                        sp.dma_start(rawN[:, :, :], t["ctxN"][bass.ds(c, 1)].rearrange("o p k n -> p (o k) n")).then_inc(sem("rawN_in"), 16)
                    sp.wait_ge(sem("piece_done"), PIECES * chunks)
                    sp.dma_start(wv[:, :, :], t["wv0"]).then_inc(sem("post_in"), 16)
                    sp.dma_start(wo[:, :, :], t["wo0"]).then_inc(sem("post_in"), 16)

                @block.gpsimd
                def _(pool):
                    def nought(x):
                        return v["zero"][:, 0:1].unsqueeze(2).broadcast_to([P, x.shape[1], x.shape[2]])

                    def split(raw, hi, lo, ready, n):
                        nc.gpsimd.tensor_tensor(hi[:, :, :], raw[:, :, :], nought(raw), ALU.add).then_inc(sem("split_hi"), 1)
                        pool.wait_ge(sem("split_hi"), n)
                        nc.gpsimd.tensor_tensor(lo[:, :, :], raw[:, :, :], hi[:, :, :].bitcast(F32),
                                                ALU.subtract).then_inc(sem(ready), 1)

                    link(pool, nc.gpsimd.memset(v["zero"][:, :], 0.0), "pool_chain")
                    link(pool, nc.gpsimd.memset(v["ident"][:, :], 0.0), "pool_chain")
                    nc.gpsimd.affine_select(out=v["ident"][:, :], in_=v["ident"][:, :], compare_op=ALU.not_equal,
                                            fill=1.0, base=0, pattern=[[1, P]],
                                            channel_multiplier=-1).then_inc(sem("ident_ready"), 1)
                    pool.wait_ge(sem("rawT_in"), 16)
                    split(rawT, cTh[0], cTl[0], "cT_ready", 1)
                    pool.wait_ge(sem("rawN_in"), 16)
                    split(rawN, cNh[0], cNl[0], "cN_ready", 2)
                    pool.wait_ge(sem("q_done"), 1)
                    pool.wait_ge(sem("wk_split"), 2)
                    nc.gpsimd.memset(flat, 0.0).then_inc(sem("U_zeroed"), 1)
                    pool.wait_ge(sem("rawT_in"), 32)
                    split(rawT, cTh[1], cTl[1], "cT_ready", 3)
                    pool.wait_ge(sem("rawN_in"), 32)
                    split(rawN, cNh[1], cNl[1], "cN_ready", 4)
                    link(pool, nc.gpsimd.memset(v["ones"][:, :], 1.0), "pool_chain")
                    link(pool, nc.gpsimd.memset(v["row0"][:, :], 0.0), "pool_chain")
                    nc.gpsimd.memset(v["row0"][0:1, :], 1.0)
                    link(pool, nc.gpsimd.memset(v["hmask"][:, :], 1.0), "pool_chain")
                    link(pool, nc.gpsimd.affine_select(out=v["hmask"][:, :], in_=v["hmask"][:, :], compare_op=ALU.is_ge,
                                                       fill=0.0, base=0, pattern=[[-DH1, HPT]],
                                                       channel_multiplier=1), "pool_chain")
                    nc.gpsimd.affine_select(out=v["hmask"][:, :], in_=v["hmask"][:, :], compare_op=ALU.is_ge,
                                            fill=0.0, base=DH1 - 1, pattern=[[DH1, HPT]], channel_multiplier=-1)
                    nc.gpsimd.affine_select(out=v["tri"][:, :], in_=v["ones"][:, :], compare_op=ALU.is_ge,
                                            fill=0.0, base=0, pattern=[[1, P]], channel_multiplier=-1)
                    link(pool, nc.gpsimd.memset(v["below"][:, :, :], 1.0), "pool_chain")
                    nc.gpsimd.affine_select(out=v["below"][:, :, :], in_=v["below"][:, :, :], compare_op=ALU.is_gt,
                                            fill=0.0, base=0, pattern=[[1, E1], [-1, E1]], channel_multiplier=0)
                    nc.gpsimd.iota(v["disti"][:, 0, :], pattern=[[2, P]], base=0, channel_multiplier=-2)
                    nc.gpsimd.iota(v["disti"][:, 1, :], pattern=[[-2, P]], base=0,
                                   channel_multiplier=2).then_inc(sem("consts_ready"), 1)
                    with pool.Fori(1, pairs) as i:
                        for b in range(2):
                            pool.wait_ge(sem("rawT_in"), i * 32 + 16 * (b + 1))
                            pool.wait_ge(sem("piece_done"), i * (2 * PIECES) + PIECES * (b - 1))
                            split(rawT, cTh[b], cTl[b], "cT_ready", i * 4 + (2 * b + 1))
                            pool.wait_ge(sem("rawN_in"), i * 32 + 16 * (b + 1))
                            pool.wait_ge(sem("pv_done"), i * steps + H0 * (b - 1))
                            split(rawN, cNh[b], cNl[b], "cN_ready", i * 4 + (2 * b + 2))

                @block.scalar
                def _(act):
                    act.dma_start(v["brow"][:, :], t["brow"]).then_inc(sem("post_in"), 16)
                    for name in ("aq", "ak", "av", "afc", "awo"):
                        act.dma_start(v[name][:, :, :], t[name]).then_inc(sem("band_in"), 16)
                    act.dma_start(v["abqk"][:, :], t["abqk"]).then_inc(sem("band_in"), 16)
                    act.dma_start(v["alpha"][:, :], t["alpha"].partition_broadcast(P)).then_inc(sem("band_in"), 16)
                    norm_scalar(act, 0)
                    act.wait_ge(sem("wk_in"), 16)
                    nc.scalar.copy(wkh[:, :, :], wk).then_inc(sem("wkh_ready"), 1)
                    act.wait_ge(sem("q_done"), 1)
                    for s in range(2):
                        for d in range(2):
                            nc.scalar.activation(by_pair(qh)[halves[d], :, s, :], q_ps(ps)[halves[s]], ACT.Copy,
                                                 scale=SCALE).then_inc(sem("qh_ready"), 1)

                    def high_parts(g, first=False):
                        for s in range(2):
                            h, cols = piece_of(g, s)
                            nc.scalar.copy(K[halves[s], h, cols], ps[halves[s], piece_bank(g, first), 0:HK]).then_inc(
                                sem("kh_ready"), 1)

                    def exp_step(u):
                        par, h, b = (u // H0) % 2, u % H0, u % 2
                        nc.scalar.activation(al[:, b:b + 1], nm[:, 1 - par, h:h + 1], ACT.Exp,
                                             bias=nm[:, par, h:h + 1], scale=-1.0)
                        nc.scalar.activation(prob[:, :, :], S[b], ACT.Exp, bias=nm[:, par, h:h + 1],
                                             scale=1.0, accum_out=rs[:, b:b + 1]).then_inc(sem("exp_done"), 1)

                    for g in range(PIECES):
                        if g == 2:
                            act.wait_ge(sem("ql_ready"), 1)
                            for s in range(2):
                                ins = nc.scalar.copy(by_pair(ql)[halves[1 - s], :, s, :],
                                                     by_pair(ql)[halves[s], :, s, :].bitcast(F32))
                            ins.then_inc(sem("ql_doubled"), 1)
                        act.wait_ge(sem("piece_done"), g + 1)
                        high_parts(g, True)
                    act.wait_ge(sem("max_done"), 1)
                    exp_step(0)
                    def round_of(i, end):
                        for u in range(steps):
                            makes = not end or u < H0
                            act.wait_ge(sem("p_turned"), i * steps + (u + 1))
                            nc.scalar.activation(pTh[:, :], pT_ps, ACT.Copy).then_inc(sem("pTh_ready"), 1)
                            if makes:
                                g = u % H0
                                act.wait_ge(sem("piece_done"), i * steps + (PIECES * (u // H0 + 1) + g + 1))
                                high_parts(g)
                            if end and u + 1 == steps:
                                break
                            act.wait_ge(sem("max_done"), i * steps + (u + 2))
                            act.wait_ge(sem("pv_free"), i * steps + (u + 2))
                            exp_step(u + 1)
                            if not makes and u % 2 == 0 and u > H0:
                                turned_sums((u - H0) // 2 - 1)

                    def turned_sums(m):
                        act.wait_ge(sem("U_turned"), m + 1)
                        nc.scalar.copy(raw[:, 0:2 * D], ps[:, 7, :]).then_inc(sem("UT_ready"), 1)

                    with act.Fori(0, last) as i:
                        round_of(i, False)
                    round_of(last, True)
                    turned_sums(H0 // 2 - 1)

                @block.vector
                def _(dve):
                    dve.wait_ge(sem("x_in"), 16)
                    nc.vector.memset(den[:, :], 0.0)
                    nc.vector.memset(nm[:, :, :].rearrange("p a h -> p (a h)"), BIG).then_inc(sem("pv_free"), 2)
                    norm_vector(dve, 0)
                    dve.wait_ge(sem("wkh_ready"), 1)
                    nc.vector.tensor_tensor(wkl[:, :, :], wk, wkh[:, :, :].bitcast(F32), ALU.subtract).then_inc(sem("wk_split"), 2)
                    dve.wait_ge(sem("qh_ready"), 4)
                    for s in range(2):
                        ins = nc.vector.scalar_tensor_tensor(
                            by_pair(ql)[halves[s], :, s, :], q_ps(ps)[halves[s]], SCALE,
                            by_pair(qh)[halves[s], :, s, :].bitcast(F32), ALU.mult, ALU.subtract)
                    ins.then_inc(sem("ql_ready"), 1)

                    def low_parts(g, first=False):
                        for s in range(2):
                            h, cols = piece_of(g, s)
                            ins = nc.vector.tensor_tensor(K[halves[1 - s], h, cols], ps[halves[s], piece_bank(g, first), 0:HK],
                                                          K[halves[s], h, cols].bitcast(F32), ALU.subtract)
                        ins.then_inc(sem("kl_ready"), 1)

                    def max_step(u):
                        nc.vector.tensor_reduce(nmx[:, :], S[u % 2], mybir.AxisListType.XY, ALU.max,
                                                negate=True).then_inc(sem("chunk_max"), 1)

                    def new_max(u):
                        par, h = (u // H0) % 2, u % H0
                        nc.vector.tensor_tensor(nm[:, par, h:h + 1], nm[:, 1 - par, h:h + 1], nmx[:, :],
                                                ALU.min).then_inc(sem("max_done"), 1)

                    for g in range(PIECES):
                        dve.wait_ge(sem("kh_ready"), 2 * g + 2)
                        low_parts(g, True)
                        if g == FIRST + 1:
                            dve.wait_ge(sem("scores_done"), 1)
                            max_step(0)
                            dve.wait_ge(sem("chunk_max"), 1)
                            new_max(0)
                    dve.wait_ge(sem("U_zeroed"), 1)

                    def round_of(i, end):
                        for u in range(steps):
                            h, b = u % H0, u % 2
                            makes = not end or u < H0
                            if not (end and u + 1 == steps):
                                dve.wait_ge(sem("max_done"), i * steps + (u + 1))
                                dve.wait_ge(sem("scores_done"), i * steps + (u + 2))
                                max_step(u + 1)
                                dve.wait_ge(sem("chunk_max"), i * steps + (u + 2))
                                new_max(u + 1)
                            dve.wait_ge(sem("pTh_ready"), i * steps + (u + 1))
                            nc.vector.tensor_tensor(pTl[:, :], pT_ps, pTh[:, :].bitcast(F32),
                                                    ALU.subtract).then_inc(sem("pTl_ready"), 1)
                            if makes:
                                dve.wait_ge(sem("kh_ready"), i * (2 * steps) + 2 * (PIECES * (u // H0 + 1) + h + 1))
                                low_parts(h)
                            elif h % 2 == 1 and h > 1:
                                outputs(h // 2 - 1)
                            elif h > 1:
                                scale_sums(h // 2 - 1)
                            dve.wait_ge(sem("pv_free"), i * steps + (u + 2))
                            nc.vector.scalar_tensor_tensor(den[:, h:h + 1], den[:, h:h + 1], al[:, b:b + 1],
                                                           rs[:, b:b + 1], ALU.mult, ALU.add)
                            dve.wait_ge(sem("pv_done"), i * steps + (u + 1))
                            nc.vector.scalar_tensor_tensor(U[:, h, :], U[:, h, :], al[:, b:b + 1], O,
                                                           ALU.mult, ALU.add).then_inc(sem("pv_free"), 1)

                    def scale_sums(m):
                        h = 2 * m
                        dve.wait_ge(sem("pv_free"), 2 + H0 * (chunks - 1) + h + 2)
                        link(dve, nc.vector.reciprocal(rden[:, h:h + 2], den[:, h:h + 2]), "post_chain")
                        nc.vector.tensor_scalar(U[:, h, :], U[:, h, :], rden[:, h:h + 1], None, ALU.mult)
                        nc.vector.tensor_scalar(U[:, h + 1, :], U[:, h + 1, :], rden[:, h + 1:h + 2], None,
                                                ALU.mult).then_inc(sem("U_scaled"), 1)

                    def outputs(m):
                        dve.wait_ge(sem("projected"), m + 1)
                        nc.vector.tensor_copy(oT[halves[0], m, :], ps[halves[0], 7, 0:P])
                        nc.vector.tensor_copy(oT[halves[1], m, :], ps[halves[0], 7, P:2 * P]).then_inc(sem("oT_ready"), 1)

                    with dve.Fori(0, last) as i:
                        round_of(i, False)
                    round_of(last, True)
                    scale_sums(H0 // 2 - 1)
                    outputs(H0 // 2 - 1)
                    dve.wait_ge(sem("y0_done"), 1)
                    nc.vector.tensor_tensor(res[:, :], res[:, :], ps[:, 0, 0:D], ALU.add).then_inc(sem("res_ready"), 1)

                @block.tensor
                def _(pe):
                    pe.wait_ge(sem("ident_ready"), 1)
                    norm_tensor(pe, 0)
                    pe.wait_ge(sem("wq_in"), 16)
                    for m in range(H0 // 2):
                        for k in range(KT):
                            mm = nc.tensor.matmul(ps[:, m // 4, (m % 4) * P:(m % 4 + 1) * P], wq[:, k, m * P:(m + 1) * P],
                                                  xnT[:, k, :], start=(k == 0), stop=(k == KT - 1))
                    mm.then_inc(sem("q_done"), 1)

                    def piece(g, b, first=False):
                        m, n = g // 2, 0
                        for w, c in ((wkh, cTh[b]), (wkl, cTh[b]), (wkh, cTl[b])):
                            if first and g == 0 and n == KT:
                                pe.wait_ge(sem("wk_split"), 2)
                            if first and g == 0 and n == 2 * KT:
                                pe.wait_ge(sem("cT_ready"), 1)
                            for k in range(KT):
                                mm = nc.tensor.matmul(ps[:, piece_bank(g, first), 0:HK], w[:, k, m * P:(m + 1) * P],
                                                      c[:, k, (g % 2) * HK:(g % 2 + 1) * HK],
                                                      start=(n == 0), stop=(n == 3 * KT - 1))
                                n += 1
                        mm.then_inc(sem("piece_done"), 1)

                    def scores(u):
                        h, b = u % H0, u % 2
                        for half in range(2):
                            cols = slice(half * HK, (half + 1) * HK)
                            nc.tensor.matmul(S[b][:, half, :], qh[:, h, :], K[:, h, cols], start=True, stop=False)
                            mm = nc.tensor.matmul(S[b][:, half, :], ql[:, h, :], K[:, h, cols], start=False, stop=True)
                        mm.then_inc(sem("scores_done"), 1)

                    pe.wait_ge(sem("split_hi"), 1)
                    pe.wait_ge(sem("wkh_ready"), 1)
                    for g in range(PIECES):
                        if g >= 4:
                            pe.wait_ge(sem("kl_ready"), g - 3)
                        piece(g, 0, True)
                        if g == FIRST:
                            pe.wait_ge(sem("ql_doubled"), 1)
                            scores(0)
                            scores(1)
                    pe.wait_ge(sem("kl_ready"), PIECES)

                    def round_of(i, end):
                        for u in range(steps):
                            c, g = u // H0, u % H0
                            pe.wait_ge(sem("exp_done"), i * steps + (u + 1))
                            for k in range(NT):
                                mm = nc.tensor.transpose(pT_ps[:, k * P:(k + 1) * P],
                                                         prob[:, :, :].rearrange("p a n -> p (a n)")[:, k * P:(k + 1) * P],
                                                         ident[:, :])
                            mm.then_inc(sem("p_turned"), 1)
                            makes = not end or c == 0
                            if makes:
                                if g == 0:
                                    pe.wait_ge(sem("cT_ready"), i * 2 + (c + 2))
                                pe.wait_ge(sem("kl_ready"), i * steps + (PIECES * (c + 1) + g))
                                piece(g, (c + 1) % 2)
                            if not (end and u + 2 >= steps):
                                if u % 2 == 0:
                                    pe.wait_ge(sem("kl_ready"), i * steps + ((u + 2) // H0 * PIECES + (u + 2) % H0 + 2))
                                scores(u + 2)
                            if not makes and g % 2 == 1 and g > 1:
                                project(g // 2 - 1)
                            if g == 0:
                                pe.wait_ge(sem("cN_ready"), i * 2 + (c + 1))
                            pe.wait_ge(sem("pv_free"), i * steps + (u + 2))
                            pe.wait_ge(sem("pTh_ready"), i * steps + (u + 1))
                            n = 0
                            for p, cn in ((pTh, cNh[c]), (pTh, cNl[c]), (pTl, cNh[c])):
                                if n == 2 * NT:
                                    pe.wait_ge(sem("pTl_ready"), i * steps + (u + 1))
                                for k in range(NT):
                                    mm = nc.tensor.matmul(O, p[:, k * P:(k + 1) * P], cn[:, k, :],
                                                          start=(n == 0), stop=(n == 3 * NT - 1))
                                    n += 1
                            mm.then_inc(sem("pv_done"), 1)
                            if not makes and g % 2 == 0 and g > 0:
                                turn(g // 2 - 1)

                    def turn(m):
                        if m == 0:
                            pe.wait_ge(sem("kl_ready"), PIECES * chunks)
                        else:
                            pe.wait_ge(sem("oT_ready"), m)
                        pe.wait_ge(sem("U_scaled"), m + 1)
                        for s in range(2):
                            for k in range(KT):
                                col = s * D + k * P
                                mm = nc.tensor.transpose(ps[:, 7, col:col + P], U[:, 2 * m + s, k * P:(k + 1) * P],
                                                         ident[:, :])
                        mm.then_inc(sem("U_turned"), 1)

                    def project(m):
                        if m == 0:
                            pe.wait_ge(sem("post_in"), 48)
                        pe.wait_ge(sem("UT_ready"), m + 1)
                        for s in range(2):
                            for k in range(KT):
                                mm = nc.tensor.matmul(ps[0:DH0, 7, s * P:(s + 1) * P],
                                                      wv[:, k, (2 * m + s) * DH0:(2 * m + s + 1) * DH0], UT[:, s, k, :],
                                                      start=(k == 0), stop=(k == KT - 1))
                        mm.then_inc(sem("projected"), 1)

                    with pe.Fori(0, last) as i:
                        round_of(i, False)
                    round_of(last, True)
                    pe.wait_ge(sem("consts_ready"), 1)
                    pe.wait_ge(sem("oT_ready"), H0 // 2 - 1)
                    nc.tensor.matmul(ps[:, 0, 0:D], ones[0:1, :], v["brow"][0:1, 0:D], start=True, stop=False)
                    for m in range(H0 // 2):
                        if m == H0 // 2 - 1:
                            turn(m)
                            project(m)
                            pe.wait_ge(sem("oT_ready"), m + 1)
                        mm = nc.tensor.matmul(ps[:, 0, 0:D], oT[:, m, :], wo[:, m, :], start=False,
                                              stop=(m == H0 // 2 - 1))
                    mm.then_inc(sem("y0_done"), 1)


def stage_mix1(nc, t, sb, sem, link, ps, norms, v):
    norm_vector, norm_scalar, norm_tensor = norms
    res, xnT, ident = v["res"], v["xnT"], v["ident"]
    wg, wu, wd, below = v["wg"], v["wu"], v["wd"], v["below"]
    FACTOR = 2.5
    EB = 4
    blocks = [range(e, min(e + EB, EA)) for e in range(0, EA, EB)]
    with ExitStack() as own:
        sc = sb("f_sc", [P, E1], F32, own)
        ch = sb("f_ch", [P, E1], F32, own)
        best = sb("f_best", [P, GR, 8], F32, own)
        gs = sb("f_gs", [P, GR], F32, own)
        gsel = sb("f_gsel", [P, GR], F32, own)
        grank = sb("f_grank", [P, GR], F32, own)
        gw = sb("f_gw", [P, GR, GR], F32, own)
        gt = sb("f_gt", [P, GR, GR], F32, own)
        wins = sb("f_wins", [P, E1, E1], F32, own)
        ties = sb("f_ties", [P, E1, E1], F32, own)
        rank = sb("f_rank", [P, E1], F32, own)
        sel = sb("f_sel", [P, E1], F32, own)
        one = sb("f_one", [P, 2], F32, own)
        comb = sb("f_comb", [P, EA], F32, own)
        gate = [sb(f"f_gate{i}", [P, EB * F1], F32, own) for i in range(2)]
        act_ = [sb(f"f_act{i}", [P, EB * F1], F32, own) for i in range(2)]
        actT = [sb(f"f_actT{i}", [P, EB, P], F32, own) for i in range(2)]

        with nc.Block() as block:
            @block.vector
            def _(dve):
                norm_vector(dve, 5)
                dve.wait_ge(sem("logits1_exp"), 1)
                link(dve, nc.vector.tensor_scalar(sc[:, :], sc[:, :], 1.0, None, ALU.add), "mix1_chain")
                link(dve, nc.vector.reciprocal(sc[:, :], sc[:, :]), "mix1_chain")
                link(dve, nc.vector.tensor_tensor(ch[:, :], sc[:, :], v["br1"][:, :], ALU.add), "mix1_chain")
                for k in range(GR):
                    ins = nc.vector.max(best[:, k, :], ch[:, k * 8:(k + 1) * 8])
                link(dve, ins, "mix1_chain")
                link(dve, nc.vector.tensor_tensor(gs[:, :], best[:, :, 0], best[:, :, 1], ALU.add), "mix1_chain")
                rank_select(nc, dve, link, "mix1_chain", gs[:, :], GR, TG, gw[:, :, :], gt[:, :, :], grank[:, :],
                            gsel[:, :], below)
                link(dve, nc.vector.tensor_tensor(ch[:, :].rearrange("p (g e) -> p g e", g=GR),
                                                  ch[:, :].rearrange("p (g e) -> p g e", g=GR),
                                                  gsel[:, :].unsqueeze(2).broadcast_to([P, GR, E1 // GR]), ALU.mult), "mix1_chain")
                rank_select(nc, dve, link, "mix1_chain", ch[:, :], E1, TE, wins[:, :, :], ties[:, :, :], rank[:, :],
                            sel[:, :], below)
                link(dve, nc.vector.tensor_tensor(sel[:, :], sel[:, :], sc[:, :], ALU.mult), "mix1_chain")
                link(dve, nc.vector.tensor_reduce(one[:, 0:1], sel[:, :], AX_X, ALU.add), "mix1_chain")
                link(dve, nc.vector.tensor_scalar(one[:, 0:1], one[:, 0:1], 1e-20, None, ALU.add), "mix1_chain")
                link(dve, nc.vector.reciprocal(one[:, 1:2], one[:, 0:1]), "mix1_chain")
                nc.vector.memset(comb[:, E1:EA], 1.0)
                link(dve, nc.vector.tensor_scalar(comb[:, 0:E1], sel[:, :], one[:, 1:2], FACTOR, ALU.mult, ALU.mult), "mix1_chain")
                for n, experts in enumerate(blocks):
                    b = n % 2
                    dve.wait_ge(sem("gate_ready"), n + 1)
                    for j, e in enumerate(experts):
                        cols = slice(j * F1, (j + 1) * F1)
                        ins = nc.vector.scalar_tensor_tensor(act_[b][:, cols], gate[b][:, cols], comb[:, e:e + 1],
                                                             ps[:, 2 + b, cols], ALU.mult, ALU.mult)
                    ins.then_inc(sem("act_ready"), 1)
                dve.wait_ge(sem("y5_done"), 1)
                nc.vector.tensor_tensor(res[:, :], res[:, :], ps[:, 7, 0:D], ALU.add).then_inc(sem("res_ready"), 1)

            @block.scalar
            def _(act):
                norm_scalar(act, 5)
                act.wait_ge(sem("logits1_done"), 1)
                nc.scalar.activation(sc[:, :], ps[:, 6, 0:E1], ACT.Exp, scale=-1.0).then_inc(sem("logits1_exp"), 1)

                def silu(n):
                    b, w = n % 2, len(blocks[n]) * F1
                    act.wait_ge(sem("gu_done"), n + 1)
                    if n >= 2:
                        act.wait_ge(sem("act_ready"), n - 1)
                    nc.scalar.activation(gate[b][:, 0:w], ps[:, b, 0:w], ACT.Silu).then_inc(sem("gate_ready"), 1)

                silu(0)
                for n, experts in enumerate(blocks):
                    b, w = n % 2, len(experts) * P
                    if n + 1 < len(blocks):
                        silu(n + 1)
                    act.wait_ge(sem("act_turned"), n + 1)
                    nc.scalar.copy(actT[b][:, 0:len(experts), :].rearrange("p e q -> p (e q)"),
                                   ps[:, 4 + b, 0:w]).then_inc(sem("actT_ready"), 1)

            @block.tensor
            def _(pe):
                norm_tensor(pe, 5)
                for k in range(KT):
                    mm = nc.tensor.matmul(ps[:, 6, 0:E1], xnT[:, k, :], v["wr1"][:, k, :], start=(k == 0), stop=(k == KT - 1))
                mm.then_inc(sem("logits1_done"), 1)
                pe.wait_ge(sem("mix1_in"), 32)
                pe.wait_ge(sem("wd_in"), 16)

                def gate_up(n):
                    e, w = blocks[n][0], len(blocks[n]) * F1
                    if n >= 2:
                        pe.wait_ge(sem("act_ready"), n - 1)
                    for bank, m in ((n % 2, wg), (2 + n % 2, wu)):
                        for k in range(KT):
                            mm = nc.tensor.matmul(ps[:, bank, 0:w], xnT[:, k, :], m[:, k, e * F1:e * F1 + w],
                                                  start=(k == 0), stop=(k == KT - 1))
                    mm.then_inc(sem("gu_done"), 1)

                def down(n):
                    pe.wait_ge(sem("actT_ready"), n + 1)
                    for j, e in enumerate(blocks[n]):
                        mm = nc.tensor.matmul(ps[:, 7, 0:D], actT[n % 2][:, j, :], wd[:, e, :],
                                              start=(e == 0), stop=(e == EA - 1))
                    return mm

                gate_up(0)
                gate_up(1)
                for n, experts in enumerate(blocks):
                    pe.wait_ge(sem("act_ready"), n + 1)
                    for j in range(len(experts)):
                        mm = nc.tensor.transpose(ps[:, 4 + n % 2, j * P:(j + 1) * P], act_[n % 2][:, j * F1:(j + 1) * F1], ident[:, :])
                    mm.then_inc(sem("act_turned"), 1)
                    if n + 2 < len(blocks):
                        gate_up(n + 2)
                    if n >= 1:
                        down(n - 1)
                down(len(blocks) - 1).then_inc(sem("y5_done"), 1)


def stage_scan(nc, t, sb, sem, link, ps, norms, v):
    norm_vector, norm_scalar, norm_tensor = norms
    res, xn, xnT, ones, tri = v["res"], v["xn"], v["xnT"], v["ones"], v["tri"]
    LOG_EPS, CLAMP = -7.0, 20.0
    BD = 64
    NB = D // BD
    W = BD * NST
    with ExitStack() as own:
        ea = sb("e_ea", [P, D * NST], F32, own)
        dtT = sb("e_dtT", [DTR, P], F32, own)
        bc = sb("e_bc", [P, 2 * NST], F32, own)
        z = sb("e_z", [P, D], F32, own)
        pos = sb("e_pos", [P, D], F32, own)
        u = sb("e_u", [P, D], F32, own)
        s1 = sb("e_s", [P, D], F32, own)
        s2 = sb("e_s2", [P, D], F32, own)
        poly = sb("e_poly", [P, D], F32, own)
        delta = sb("e_delta", [P, D], F32, own)
        dx = sb("e_dx", [P, D], F32, own)
        y = sb("e_y", [P, D], F32, own)
        la = [sb(f"e_la{i}", [P, W], F32, own) for i in range(2)]
        R = [sb(f"e_R{i}", [P, W], F32, own) for i in range(2)]
        inv = [sb(f"e_inv{i}", [P, W], F32, own) for i in range(2)]
        g = [sb(f"e_g{i}", [P, W], F32, own) for i in range(2)]

        def cn(x):
            return x.rearrange("p (c n) -> p c n", n=NST)

        def over_states(x):
            return x.unsqueeze(2).broadcast_to([P, BD, NST])

        def over_channels(x):
            return x.unsqueeze(1).broadcast_to([P, BD, NST])

        def bank2(n):
            return ps[:, n:n + 2, :].rearrange("p b n -> p (b n)")

        with nc.Block() as block:
            @block.sync
            def _(sp):
                sp.dma_start(ea[:, :], t["alog"].partition_broadcast(P)).then_inc(sem("alog_in"), 16)
                sp.dma_start(v["wd"][:, :, :], t["wd1"]).then_inc(sem("wd_in"), 16)

            @block.gpsimd
            def _(pool):
                for n in range(NB):
                    b, cols = n % 2, slice(n * BD, (n + 1) * BD)
                    if n == 0:
                        pool.wait_ge(sem("dx_ready"), 1)
                        pool.wait_ge(sem("bc_ready"), 1)
                    if n >= 2:
                        pool.wait_ge(sem("sum_done"), n - 1)
                        pool.wait_ge(sem("y4_ready"), n - 1)
                    nc.gpsimd.tensor_tensor(cn(g[b][:, :]), over_states(dx[:, cols]), over_channels(bc[:, 0:NST]),
                                            ALU.mult).then_inc(sem("g_ready"), 1)
                    pool.wait_ge(sem("R_ready"), n + 1)
                    nc.gpsimd.tensor_tensor(cn(R[b][:, :]), cn(R[b][:, :]), over_channels(bc[:, NST:2 * NST]),
                                            ALU.mult).then_inc(sem("CR_ready"), 1)

            @block.scalar
            def _(act):
                norm_scalar(act, 4)
                act.wait_ge(sem("alog_in"), 16)
                nc.scalar.activation(ea[:, :], ea[:, :], ACT.Exp).then_inc(sem("ea_done"), 1)
                act.wait_ge(sem("absz_ready"), 1)
                nc.scalar.activation(u[:, :], u[:, :], ACT.Exp, scale=-1.0).then_inc(sem("u_ready"), 1)
                for n in range(NB):
                    b = n % 2
                    act.wait_ge(sem("neg_ready"), n + 1)
                    nc.scalar.activation(inv[b][:, :], inv[b][:, :], ACT.Exp).then_inc(sem("inv_ready"), 1)
                    if n >= 2:
                        act.wait_ge(sem("y4_ready"), n - 1)
                    nc.scalar.activation(R[b][:, :], bank2(2 * b), ACT.Exp).then_inc(sem("R_ready"), 1)

            @block.vector
            def _(dve):
                norm_vector(dve, 4)
                dve.wait_ge(sem("dt_done"), 1)
                nc.vector.tensor_copy(dtT[:, :], ps[0:DTR, 4, 0:P]).then_inc(sem("dtT_ready"), 1)
                nc.vector.tensor_copy(bc[:, :], ps[:, 5, 0:2 * NST]).then_inc(sem("bc_ready"), 1)
                dve.wait_ge(sem("z_done"), 1)
                link(dve, nc.vector.tensor_copy(z[:, :], ps[:, 6, 0:D]), "scan_chain")
                nc.vector.scalar_tensor_tensor(u[:, :], z[:, :], -1.0, z[:, :], ALU.mult, ALU.max).then_inc(sem("absz_ready"), 1)
                nc.vector.tensor_scalar(pos[:, :], z[:, :], 0.0, None, ALU.max)
                dve.wait_ge(sem("u_ready"), 1)
                link(dve, nc.vector.tensor_scalar(s1[:, :], u[:, :], 2.0, None, ALU.add), "scan_chain")
                link(dve, nc.vector.reciprocal(s1[:, :], s1[:, :]), "scan_chain")
                link(dve, nc.vector.tensor_tensor(s1[:, :], s1[:, :], u[:, :], ALU.mult), "scan_chain")
                link(dve, nc.vector.tensor_tensor(s2[:, :], s1[:, :], s1[:, :], ALU.mult), "scan_chain")
                link(dve, nc.vector.tensor_scalar(poly[:, :], s2[:, :], 1.0 / 15, None, ALU.mult), "scan_chain")
                for k in (13, 11, 9, 7, 5, 3):
                    link(dve, nc.vector.scalar_tensor_tensor(poly[:, :], poly[:, :], 1.0 / k, s2[:, :], ALU.add, ALU.mult), "scan_chain")
                link(dve, nc.vector.scalar_tensor_tensor(poly[:, :], poly[:, :], 1.0, s1[:, :], ALU.add, ALU.mult), "scan_chain")
                link(dve, nc.vector.scalar_tensor_tensor(delta[:, :], poly[:, :], 2.0, pos[:, :], ALU.mult, ALU.add), "scan_chain")
                nc.vector.tensor_tensor(dx[:, :], delta[:, :], xn[:, :], ALU.mult).then_inc(sem("dx_ready"), 1)
                dve.wait_ge(sem("late_in"), 96)
                link(dve, nc.vector.tensor_tensor(y[:, :], xn[:, :], v["dskip"][:, :], ALU.mult), "scan_chain")
                link(dve, nc.vector.tensor_tensor(res[:, :], res[:, :], y[:, :], ALU.add), "scan_chain")
                dve.wait_ge(sem("ea_done"), 1)

                def decay(n):
                    b = n % 2
                    if n >= 2:
                        dve.wait_ge(sem("logR_done"), n - 1)
                    link(dve, nc.vector.tensor_tensor(cn(la[b][:, :]), over_states(delta[:, n * BD:(n + 1) * BD]),
                                                      cn(ea[:, n * W:(n + 1) * W]), ALU.mult), "scan_chain")
                    nc.vector.tensor_scalar(la[b][:, :], la[b][:, :], -1.0, LOG_EPS, ALU.mult, ALU.max).then_inc(sem("la_ready"), 1)

                def inputs(n):
                    b = n % 2
                    dve.wait_ge(sem("logR_done"), n + 1)
                    if n >= 2:
                        dve.wait_ge(sem("gi_ready"), n - 1)
                    nc.vector.tensor_scalar(inv[b][:, :], bank2(2 * b), -1.0, CLAMP, ALU.mult, ALU.min).then_inc(sem("neg_ready"), 1)
                    dve.wait_ge(sem("g_ready"), n + 1)
                    dve.wait_ge(sem("inv_ready"), n + 1)
                    nc.vector.tensor_tensor(g[b][:, :], g[b][:, :], inv[b][:, :], ALU.mult).then_inc(sem("gi_ready"), 1)

                def outputs(n):
                    b = n % 2
                    dve.wait_ge(sem("sum_done"), n + 1)
                    dve.wait_ge(sem("CR_ready"), n + 1)
                    link(dve, nc.vector.tensor_tensor(inv[b][:, :], bank2(4 + 2 * b), R[b][:, :], ALU.mult), "scan_chain")
                    nc.vector.tensor_reduce(y[:, n * BD:(n + 1) * BD], cn(inv[b][:, :]), AX_X, ALU.add).then_inc(sem("y4_ready"), 1)
                    dve.wait_ge(sem("y4_ready"), n + 1)

                decay(0)
                decay(1)
                for n in range(NB):
                    inputs(n)
                    if n + 2 < NB:
                        decay(n + 2)
                    if n >= 1:
                        outputs(n - 1)
                outputs(NB - 1)
                nc.vector.tensor_tensor(res[:, :], res[:, :], y[:, :], ALU.add).then_inc(sem("res_ready"), 1)

            @block.tensor
            def _(pe):
                norm_tensor(pe, 4)
                pe.wait_ge(sem("late_in"), 96)
                for k in range(KT):
                    mm = nc.tensor.matmul(ps[0:DTR, 4, 0:P], v["wxp"][:, k, 0:DTR], xnT[:, k, :], start=(k == 0), stop=(k == KT - 1))
                for k in range(KT):
                    mm = nc.tensor.matmul(ps[:, 5, 0:2 * NST], xnT[:, k, :], v["wxp"][:, k, DTR:DTR + 2 * NST],
                                          start=(k == 0), stop=(k == KT - 1))
                mm.then_inc(sem("dt_done"), 1)
                nc.tensor.matmul(ps[:, 6, 0:D], ones[0:1, :], v["bdt"][:, :], start=True, stop=False)
                pe.wait_ge(sem("dtT_ready"), 1)
                nc.tensor.matmul(ps[:, 6, 0:D], dtT[:, :], v["wdt"][:, :], start=False, stop=True).then_inc(sem("z_done"), 1)
                pe.wait_ge(sem("bc_ready"), 1)
                pe.wait_ge(sem("absz_ready"), 1)

                def log_R(n):
                    pe.wait_ge(sem("la_ready"), n + 1)
                    if n >= 2:
                        pe.wait_ge(sem("R_ready"), n - 1)
                        pe.wait_ge(sem("neg_ready"), n - 1)
                    for k in range(2):
                        mm = nc.tensor.matmul(ps[:, 2 * (n % 2) + k, :], tri[:, :], la[n % 2][:, k * 512:(k + 1) * 512],
                                              start=True, stop=True)
                    mm.then_inc(sem("logR_done"), 1)

                def sums(n):
                    pe.wait_ge(sem("gi_ready"), n + 1)
                    if n >= 2:
                        pe.wait_ge(sem("y4_ready"), n - 1)
                    for k in range(2):
                        mm = nc.tensor.matmul(ps[:, 4 + 2 * (n % 2) + k, :], tri[:, :], g[n % 2][:, k * 512:(k + 1) * 512],
                                              start=True, stop=True)
                    mm.then_inc(sem("sum_done"), 1)

                log_R(0)
                log_R(1)
                for n in range(NB):
                    sums(n)
                    if n + 2 < NB:
                        log_R(n + 2)


def stage_relu_context(nc, t, sb, sem, link, ps, norms, v):
    norm_vector, norm_scalar, norm_tensor = norms
    res, xnT, ident, wx, bx = v["res"], v["xnT"], v["ident"], v["wx"], v["bx"]
    chunks = t["ctxN"].shape[0]
    with ExitStack() as own:
        raw = [sb(f"d_raw{i}", [P, KT, CK], F32, own) for i in range(2)]
        cTh = sb("d_cTh", [P, KT, CK], F32R, own)
        cTl = sb("d_cTl", [P, KT, CK], F32R, own)
        mrow = [sb(f"d_mrow{i}", [1, CK], U8, own) for i in range(2)]
        mneg = [sb(f"d_mneg{i}", [1, CK], BF16, own) for i in range(2)]
        one_b = sb("d_one", [1, P], BF16, own)
        wxh = sb("d_wxh", [P, KT, D], F32R, own)
        wxl = sb("d_wxl", [P, KT, D], F32R, own)
        qT = sb("d_qT", [P, KT, P], F32, own)
        qh = sb("d_qh", [P, KT, P], F32R, own)
        ql = sb("d_ql", [P, KT, P], F32R, own)
        kT = sb("d_kT", [P, KT, CK], F32, own)
        kTh = sb("d_kTh", [P, KT, CK], F32R, own)
        kTl = sb("d_kTl", [P, KT, CK], F32R, own)
        kNh = [sb(f"d_kNh{i}", [P, NT, D], F32R, own) for i in range(2)]
        kNl = [sb(f"d_kNl{i}", [P, NT, D], F32R, own) for i in range(2)]
        prob = sb("d_prob", [P, 2, HK], F32, own)
        pTh = sb("d_pTh", [P, CK], F32R, own)
        pTl = sb("d_pTl", [P, CK], F32R, own)
        U = sb("d_U", [P, D], F32, own)
        den = sb("d_den", [P, 1], F32, own)
        rden = sb("d_rden", [P, 1], F32, own)
        nm = sb("d_nm", [P, 2], F32, own)
        nmx = sb("d_nmx", [P, 1], F32, own)
        al = sb("d_al", [P, 2], F32, own)
        rs = sb("d_rs", [P, 2], F32, own)
        S = ps[:, 2:4, 0:HK]
        O = ps[:, 6, 0:D]
        KG = 2 * KT
        NG = (NT + 1) // 2
        KB = [7, 4, 5, 7]
        PG = [range(0, 4), range(4, NT)]

        def part(x, g):
            return x[:, g // 2, (g % 2) * HK:(g % 2 + 1) * HK]

        def tiles_of(n):
            return slice(2 * n, min(2 * n + 2, NT))

        with nc.Block() as block:
            @block.sync
            def _(sp):
                for b in range(2):
                    sp.dma_start(raw[b][:, :, :], t["ctxT"][b]).then_inc(sem(f"dctx_in{b}"), 16)
                    sp.dma_start(mrow[b][:, :], t["mask"][b:b + 1, :]).then_inc(sem(f"dmask_in{b}"), 16)
                with sp.Fori(1, chunks // 2) as i:
                    for b in range(2):
                        sp.wait_ge(sem("ds_done"), i * 2 + (b - 1))
                        sp.dma_start(raw[b][:, :, :], t["ctxT"][bass.ds(i * 2 + b, 1)].rearrange(
                            "o p k n -> p (o k) n")).then_inc(sem(f"dctx_in{b}"), 16)
                        sp.dma_start(mrow[b][:, :], t["mask"][bass.ds(i * 2 + b, 1), :]).then_inc(sem(f"dmask_in{b}"), 16)
                for b in range(2):
                    sp.wait_ge(sem("ds_done"), chunks - 1 + b)
                    sp.dma_start(raw[b][:, :, :], t["ctxT"][b]).then_inc(sem(f"dctx_in{b}"), 16)
                    if b == 0:
                        sp.dma_start(mrow[b][:, :], t["mask"][b:b + 1, :]).then_inc(sem(f"dmask_in{b}"), 16)

            @block.gpsimd
            def _(pool):
                def split_low(b):
                    nc.gpsimd.tensor_tensor(cTl[:, :, :], raw[b][:, :, :], cTh[:, :, :].bitcast(F32),
                                            ALU.subtract).then_inc(sem("dcTl_ready"), 1)

                def keys_low(g):
                    nc.gpsimd.tensor_tensor(part(kTl, g), part(kT, g), part(kTh, g).bitcast(F32),
                                            ALU.subtract).then_inc(sem("dkTl_ready"), 1)

                pool.wait_ge(sem("dcTh_ready"), 1)
                split_low(0)
                for g in range(KG):
                    pool.wait_ge(sem("dkTh_ready"), g + 1)
                    keys_low(g)
                pool.wait_ge(sem("dcTh_ready"), 2)
                split_low(1)
                with pool.Fori(0, chunks // 2) as i:
                    for b in range(2):
                        for g in range(KG):
                            pool.wait_ge(sem("dkTh_ready"), i * (2 * KG) + (KG * (b + 1) + g + 1))
                            keys_low(g)
                        pool.wait_ge(sem("dcTh_ready"), i * 2 + (b + 3))
                        split_low(b)

            @block.scalar
            def _(act):
                def split_high(b):
                    nc.scalar.copy(cTh[:, :, :], raw[b][:, :, :]).then_inc(sem("dcTh_ready"), 1)

                act.wait_ge(sem("dctx_in0"), 16)
                split_high(0)
                norm_scalar(act, 3)
                act.wait_ge(sem("dq_done"), 1)
                act.wait_ge(sem("wx_in"), 32)
                for m in range(KT):
                    nc.scalar.activation(qT[:, m, :], ps[:, 6, m * P:(m + 1) * P], ACT.Relu, bias=bx[:, m:m + 1],
                                         scale=1.0).then_inc(sem("dq_ready"), 1)

                def keys(g):
                    nc.scalar.activation(part(kT, g), ps[:, g % 2, 0:HK], ACT.Relu, bias=bx[:, g // 2:g // 2 + 1],
                                         scale=1.0).then_inc(sem("dkT_ready"), 1)

                def rows_high(b, n):
                    dst = kNh[b][:, tiles_of(n), :].rearrange("p a d -> p (a d)")
                    nc.scalar.copy(dst, ps[:, KB[n], 0:dst.shape[1]]).then_inc(sem("dkNh_ready"), 1)

                def exp_step(b):
                    nc.scalar.activation(al[:, b:b + 1], nm[:, 1 - b:2 - b], ACT.Exp, bias=nm[:, b:b + 1], scale=-1.0)
                    nc.scalar.activation(prob[:, :, :], S, ACT.Exp, bias=nm[:, b:b + 1], scale=1.0,
                                         accum_out=rs[:, b:b + 1]).then_inc(sem("dexp_done"), 1)

                for g in range(KG):
                    act.wait_ge(sem("dk_done"), g + 1)
                    keys(g)
                act.wait_ge(sem("dctx_in1"), 16)
                split_high(1)
                for n in range(NG):
                    act.wait_ge(sem("dk_turned"), n + 1)
                    rows_high(0, n)
                act.wait_ge(sem("dmax_done"), 1)
                exp_step(0)
                with act.Fori(0, chunks // 2) as i:
                    for b in range(2):
                        act.wait_ge(sem("dk_turned"), i * (2 * NG) + NG * (b + 1))
                        for g in range(KG):
                            act.wait_ge(sem("dk_done"), i * (2 * KG) + (KG * (b + 1) + g + 1))
                            keys(g)
                        act.wait_ge(sem(f"dctx_in{b}"), i * 16 + 32)
                        split_high(b)
                        for n, tiles in enumerate(PG):
                            act.wait_ge(sem("dp_turned"), i * 4 + (2 * b + n + 1))
                            cols = slice(tiles[0] * P, (tiles[-1] + 1) * P)
                            nc.scalar.copy(pTh[:, cols], ps[:, 4 + n, 0:len(tiles) * P]).then_inc(sem("dpTh_ready"), 1)
                        for n in range(NG):
                            act.wait_ge(sem("dk_turned"), i * (2 * NG) + (NG * (b + 1) + n + 1))
                            rows_high(1 - b, n)
                        act.wait_ge(sem("dmax_done"), i * 2 + (b + 2))
                        act.wait_ge(sem("du_free"), i * 2 + (b + 2))
                        exp_step(1 - b)

            @block.vector
            def _(dve):
                nc.vector.memset(one_b[:, :], 1.0).then_inc(sem("d_ones"), 1)
                nc.vector.memset(U[:, :], 0.0)
                nc.vector.memset(den[:, :], 0.0)
                nc.vector.memset(nm[:, :], BIG).then_inc(sem("du_free"), 2)
                dve.wait_ge(sem("wx_in"), 32)
                link(dve, nc.vector.tensor_copy(wxh[:, :, :], wx[:, :, :]), "relu_chain")
                nc.vector.tensor_tensor(wxl[:, :, :], wx[:, :, :], wxh[:, :, :].bitcast(F32),
                                        ALU.subtract).then_inc(sem("wx_split"), 1)
                norm_vector(dve, 3)
                dve.wait_ge(sem("dq_ready"), KT)
                link(dve, nc.vector.tensor_copy(qh[:, :, :], qT[:, :, :]), "relu_chain")
                nc.vector.tensor_tensor(ql[:, :, :], qT[:, :, :], qh[:, :, :].bitcast(F32),
                                        ALU.subtract).then_inc(sem("dq_split"), 1)

                def mask(b):
                    nc.vector.tensor_scalar(mneg[b][:, :], mrow[b][:, :], -BIG, None, ALU.mult).then_inc(sem("dmask_ready"), 1)

                def keys_high(g):
                    nc.vector.tensor_copy(part(kTh, g), part(kT, g)).then_inc(sem("dkTh_ready"), 1)

                def rows_low(b, n):
                    hi = kNh[b][:, tiles_of(n), :].rearrange("p a d -> p (a d)").bitcast(F32)
                    nc.vector.tensor_tensor(kNl[b][:, tiles_of(n), :].rearrange("p a d -> p (a d)"),
                                            ps[:, KB[n], 0:hi.shape[1]], hi, ALU.subtract).then_inc(sem("dkNl_ready"), 1)

                def chunk_max():
                    nc.vector.tensor_reduce(nmx[:, :], S, mybir.AxisListType.XY, ALU.max, negate=True).then_inc(sem("dchunk_max"), 1)

                def new_max(b):
                    nc.vector.tensor_tensor(nm[:, b:b + 1], nm[:, 1 - b:2 - b], nmx[:, :], ALU.min).then_inc(sem("dmax_done"), 1)

                dve.wait_ge(sem("dmask_in0"), 16)
                mask(0)
                for g in range(KG):
                    dve.wait_ge(sem("dkT_ready"), g + 1)
                    keys_high(g)
                for n in range(NG):
                    dve.wait_ge(sem("dkNh_ready"), n + 1)
                    rows_low(0, n)
                dve.wait_ge(sem("ds_done"), 1)
                chunk_max()
                dve.wait_ge(sem("dchunk_max"), 1)
                new_max(0)
                with dve.Fori(0, chunks // 2) as i:
                    for b in range(2):
                        dve.wait_ge(sem("ds_done"), i * 2 + (b + 1))
                        dve.wait_ge(sem(f"dmask_in{1 - b}"), i * 16 + 16 * (b + 1))
                        mask(1 - b)
                        for g in range(KG):
                            dve.wait_ge(sem("dkT_ready"), i * (2 * KG) + (KG * (b + 1) + g + 1))
                            keys_high(g)
                        for n, tiles in enumerate(PG):
                            dve.wait_ge(sem("dpTh_ready"), i * 4 + (2 * b + n + 1))
                            cols = slice(tiles[0] * P, (tiles[-1] + 1) * P)
                            nc.vector.tensor_tensor(pTl[:, cols], ps[:, 4 + n, 0:len(tiles) * P],
                                                    pTh[:, cols].bitcast(F32), ALU.subtract).then_inc(sem("dpTl_ready"), 1)
                        dve.wait_ge(sem("dkNh_ready"), i * (2 * NG) + (NG * (b + 1) + 1))
                        rows_low(1 - b, 0)
                        dve.wait_ge(sem("dmax_done"), i * 2 + (b + 1))
                        dve.wait_ge(sem("ds_done"), i * 2 + (b + 2))
                        chunk_max()
                        dve.wait_ge(sem("dchunk_max"), i * 2 + (b + 2))
                        new_max(1 - b)
                        for n in range(1, NG):
                            dve.wait_ge(sem("dkNh_ready"), i * (2 * NG) + (NG * (b + 1) + n + 1))
                            rows_low(1 - b, n)
                        dve.wait_ge(sem("du_free"), i * 2 + (b + 2))
                        nc.vector.scalar_tensor_tensor(den[:, :], den[:, :], al[:, b:b + 1], rs[:, b:b + 1],
                                                       ALU.mult, ALU.add)
                        dve.wait_ge(sem("dpv_done"), i * 2 + (b + 1))
                        nc.vector.scalar_tensor_tensor(U[:, :], U[:, :], al[:, b:b + 1], O,
                                                       ALU.mult, ALU.add).then_inc(sem("du_free"), 1)
                dve.wait_ge(sem("du_free"), chunks + 2)
                link(dve, nc.vector.reciprocal(rden[:, :], den[:, :]), "relu_chain")
                nc.vector.scalar_tensor_tensor(res[:, :], U[:, :], rden[:, 0:1], res[:, :], ALU.mult,
                                               ALU.add).then_inc(sem("res_ready"), 1)

            @block.tensor
            def _(pe):
                norm_tensor(pe, 3)
                pe.wait_ge(sem("wx_in"), 32)
                for m in range(KT):
                    for k in range(KT):
                        mm = nc.tensor.matmul(ps[:, 6, m * P:(m + 1) * P], wx[:, k, m * P:(m + 1) * P], xnT[:, k, :],
                                              start=(k == 0), stop=(k == KT - 1))
                mm.then_inc(sem("dq_done"), 1)

                def keys(g):
                    m, n = g // 2, 0
                    for w, c in ((wxh, cTh), (wxl, cTh), (wxh, cTl)):
                        for k in range(KT):
                            mm = nc.tensor.matmul(ps[:, g % 2, 0:HK], w[:, k, m * P:(m + 1) * P],
                                                  c[:, k, (g % 2) * HK:(g % 2 + 1) * HK],
                                                  start=(n == 0), stop=(n == 3 * KT - 1))
                            n += 1
                    mm.then_inc(sem("dk_done"), 1)

                def turn_keys(n):
                    for a, tile in enumerate(range(NT)[tiles_of(n)]):
                        for m in range(KT):
                            mm = nc.tensor.transpose(ps[:, KB[n], a * D + m * P:a * D + (m + 1) * P],
                                                     kT[:, m, tile * P:(tile + 1) * P], ident[:, :])
                    mm.then_inc(sem("dk_turned"), 1)

                def scores(b, low_parts):
                    for half in range(2):
                        cols = slice(half * HK, (half + 1) * HK)
                        nc.tensor.matmul(S[:, half, :], one_b[:, :], mneg[b][:, cols], start=True, stop=False)
                        for n, (q, c) in enumerate(((qh, kTh), (ql, kTh), (qh, kTl))):
                            if n == 2 and half == 0:
                                pe.wait_ge(sem("dkTl_ready"), low_parts)
                            for k in range(KT):
                                mm = nc.tensor.matmul(S[:, half, :], q[:, k, :], c[:, k, cols], start=False,
                                                      stop=(n == 2 and k == KT - 1))
                    mm.then_inc(sem("ds_done"), 1)

                pe.wait_ge(sem("wx_split"), 1)
                pe.wait_ge(sem("dcTl_ready"), 1)
                for g in range(KG):
                    if g >= 2:
                        pe.wait_ge(sem("dkT_ready"), g - 1)
                    keys(g)
                pe.wait_ge(sem("dkT_ready"), KG)
                for n in range(NG):
                    if n == 3:
                        pe.wait_ge(sem("dkNl_ready"), 1)
                    turn_keys(n)
                pe.wait_ge(sem("dq_split"), 1)
                pe.wait_ge(sem("d_ones"), 1)
                pe.wait_ge(sem("dmask_ready"), 1)
                pe.wait_ge(sem("dkTh_ready"), KG)
                scores(0, KG)
                with pe.Fori(0, chunks // 2) as i:
                    for b in range(2):
                        pe.wait_ge(sem("dcTl_ready"), i * 2 + (b + 2))
                        for g in range(KG):
                            if g >= 2:
                                pe.wait_ge(sem("dkT_ready"), i * (2 * KG) + (KG * (b + 1) + g - 1))
                            keys(g)
                        pe.wait_ge(sem("dexp_done"), i * 2 + (b + 1))
                        for n, tiles in enumerate(PG):
                            pe.wait_ge(sem("dkNl_ready"), i * (2 * NG) + (NG * b + 2 + n))
                            for k in tiles:
                                mm = nc.tensor.transpose(ps[:, 4 + n, (k - tiles[0]) * P:(k - tiles[0] + 1) * P],
                                                         prob[:, :, :].rearrange("p a n -> p (a n)")[:, k * P:(k + 1) * P],
                                                         ident[:, :])
                            mm.then_inc(sem("dp_turned"), 1)
                        pe.wait_ge(sem("dkNl_ready"), i * (2 * NG) + NG * (b + 1))
                        pe.wait_ge(sem("dkT_ready"), i * (2 * KG) + KG * (b + 2))
                        turn_keys(0)
                        pe.wait_ge(sem("dmask_ready"), i * 2 + (b + 2))
                        pe.wait_ge(sem("dkTh_ready"), i * (2 * KG) + KG * (b + 2))
                        scores(1 - b, i * (2 * KG) + KG * (b + 2))
                        for n in range(1, 3):
                            pe.wait_ge(sem("dpTl_ready"), i * 4 + (2 * b + n))
                            turn_keys(n)
                        pe.wait_ge(sem("dkNl_ready"), i * (2 * NG) + (NG * (b + 1) + 1))
                        turn_keys(3)
                        pe.wait_ge(sem("du_free"), i * 2 + (b + 2))
                        n = 0
                        for p, c in ((pTh, kNh[b]), (pTh, kNl[b]), (pTl, kNh[b])):
                            for k in range(NT):
                                mm = nc.tensor.matmul(O, p[:, k * P:(k + 1) * P], c[:, k, :],
                                                      start=(n == 0), stop=(n == 3 * NT - 1))
                                n += 1
                        mm.then_inc(sem("dpv_done"), 1)


def rank_select(nc, dve, link, name, val, n, k, wins, ties, rank, sel, below):
    by_i = val.unsqueeze(2).broadcast_to([P, n, n])
    by_j = val.unsqueeze(1).broadcast_to([P, n, n])
    nc.vector.tensor_tensor(wins, by_j, by_i, ALU.is_gt)
    link(dve, nc.vector.tensor_tensor(ties, by_j, by_i, ALU.is_equal), name)
    link(dve, nc.vector.tensor_tensor(ties, ties, below[:, 0:n, 0:n], ALU.mult), name)
    link(dve, nc.vector.tensor_tensor(wins, wins, ties, ALU.add), name)
    link(dve, nc.vector.tensor_reduce(rank, wins, AX_X, ALU.add), name)
    link(dve, nc.vector.tensor_scalar(sel, rank, float(k), None, ALU.is_lt), name)


def stage_mix0(nc, t, sb, sem, link, ps, norms, v):
    norm_vector, norm_scalar, norm_tensor = norms
    res, xnT, ident = v["res"], v["xnT"], v["ident"]
    w1, w2, b1 = v["w1"], v["w2"], v["b1"]
    FT = F0 // P
    with ExitStack() as own:
        h = sb("c_h", [P, E0, F0], F32, own)
        hT = sb("c_hT", [P, 2 * FT, P], F32, own)
        lg = sb("c_lg", [P, E0], F32, own)
        ex = sb("c_ex", [P, E0], F32, own)
        sel = sb("c_sel", [P, E0], F32, own)
        rank = sb("c_rank", [P, E0], F32, own)
        comb = sb("c_comb", [P, E0], F32, own)
        one = sb("c_one", [P, 4], F32, own)
        wins = sb("c_wins", [P, E0, E0], F32, own)
        ties = sb("c_ties", [P, E0, E0], F32, own)
        combT = sb("c_combT", [E0, P], F32, own)

        with nc.Block() as block:
            @block.vector
            def _(dve):
                norm_vector(dve, 2)
                dve.wait_ge(sem("logits0_done"), 1)
                dve.wait_ge(sem("router0_in"), 48)
                link(dve, nc.vector.tensor_tensor(lg[:, :], ps[:, 6, 0:E0], v["bg"][:, :], ALU.add), "mix0_chain")
                nc.vector.tensor_reduce(one[:, 0:1], lg[:, :], AX_X, ALU.max, negate=True).then_inc(sem("lmax0_ready"), 1)
                dve.wait_ge(sem("lexp0_ready"), 1)
                link(dve, nc.vector.reciprocal(one[:, 2:3], one[:, 1:2]), "mix0_chain")
                link(dve, nc.vector.tensor_scalar(ex[:, :], ex[:, :], one[:, 2:3], None, ALU.mult), "mix0_chain")
                rank_select(nc, dve, link, "mix0_chain", ex[:, :], E0, 2, wins[:, :, :], ties[:, :, :], rank[:, :],
                            sel[:, :], v["below"])
                link(dve, nc.vector.tensor_tensor(ex[:, :], ex[:, :], sel[:, :], ALU.mult), "mix0_chain")
                link(dve, nc.vector.tensor_reduce(one[:, 3:4], ex[:, :], AX_X, ALU.add), "mix0_chain")
                link(dve, nc.vector.reciprocal(one[:, 3:4], one[:, 3:4]), "mix0_chain")
                nc.vector.tensor_scalar(comb[:, :], ex[:, :], one[:, 3:4], None, ALU.mult).then_inc(sem("comb0_ready"), 1)
                dve.wait_ge(sem("comb0_ready"), 1)
                dve.wait_ge(sem("b1_in"), 16)
                for e in range(E0):
                    dve.wait_ge(sem("h0_done"), e + 1)
                    nc.vector.tensor_tensor(h[:, e, :], ps[:, e % 4, :], b1[:, e, :], ALU.add).then_inc(sem("h0_biased"), 1)
                    dve.wait_ge(sem("h0_biased"), e + 1)
                    nc.vector.tensor_scalar(h[:, e, :], h[:, e, :], 0.0, comb[:, e:e + 1], ALU.max,
                                            ALU.mult).then_inc(sem("h0_ready"), 1)
                dve.wait_ge(sem("comb0_turned"), 1)
                nc.vector.tensor_copy(combT[:, :], ps[0:E0, 6, P:2 * P]).then_inc(sem("combT_ready"), 1)
                dve.wait_ge(sem("y2_done"), 1)
                nc.vector.tensor_tensor(res[:, :], res[:, :], ps[:, 7, 0:D], ALU.add).then_inc(sem("res_ready"), 1)

            @block.scalar
            def _(act):
                norm_scalar(act, 2)
                act.wait_ge(sem("lmax0_ready"), 1)
                nc.scalar.activation(ex[:, :], lg[:, :], ACT.Exp, bias=one[:, 0:1], scale=1.0,
                                     accum_out=one[:, 1:2]).then_inc(sem("lexp0_ready"), 1)
                for e in range(E0):
                    act.wait_ge(sem("h0_turned"), e + 1)
                    nc.scalar.copy(hT[:, e % 2 * FT:(e % 2 + 1) * FT, :].rearrange("p f q -> p (f q)"),
                                   ps[:, 4 + e % 2, :]).then_inc(sem("hT0_ready"), 1)

            @block.tensor
            def _(pe):
                norm_tensor(pe, 2)
                pe.wait_ge(sem("router0_in"), 48)
                for k in range(KT):
                    mm = nc.tensor.matmul(ps[:, 6, 0:E0], xnT[:, k, :], v["wg0"][:, k, :], start=(k == 0), stop=(k == KT - 1))
                mm.then_inc(sem("logits0_done"), 1)

                def hidden(e):
                    for k in range(KT):
                        mm = nc.tensor.matmul(ps[:, e % 4, :], xnT[:, k, :], w1[:, k, e, :], start=(k == 0), stop=(k == KT - 1))
                    mm.then_inc(sem("h0_done"), 1)

                def down(e):
                    pe.wait_ge(sem("hT0_ready"), e + 1)
                    for f in range(FT):
                        nc.tensor.matmul(ps[:, 7, 0:D], hT[:, e % 2 * FT + f, :], w2[:, e * FT + f, :],
                                         start=(e == 0 and f == 0), stop=False)

                pe.wait_ge(sem("w1_in"), 16)
                for e in range(4):
                    hidden(e)
                pe.wait_ge(sem("w2_in"), 16)
                for e in range(E0):
                    pe.wait_ge(sem("h0_ready"), e + 1)
                    for f in range(FT):
                        mm = nc.tensor.transpose(ps[:, 4 + e % 2, f * P:(f + 1) * P], h[:, e, f * P:(f + 1) * P], ident[:, :])
                    mm.then_inc(sem("h0_turned"), 1)
                    if e + 4 < E0:
                        hidden(e + 4)
                    if e > 0:
                        down(e - 1)
                nc.tensor.transpose(ps[0:E0, 6, P:2 * P], comb[:, :], ident[:, :]).then_inc(sem("comb0_turned"), 1)
                down(E0 - 1)
                pe.wait_ge(sem("combT_ready"), 1)
                nc.tensor.matmul(ps[:, 7, 0:D], combT[:, :], v["b2"][:, :], start=False, stop=True).then_inc(sem("y2_done"), 1)


def stage_band(nc, t, sb, sem, link, ps, norms, v):
    norm_vector, norm_scalar, norm_tensor = norms
    res, xnT, ident, ones, row0, hmask, dist = (v[n] for n in ("res", "xnT", "ident", "ones", "row0", "hmask", "dist"))
    SCALE = DH1 ** -0.5
    MAX_W, MIN_W = 120.0, 24.0
    with ExitStack() as own:
        qT = sb("b_qT", [P, KT, P], F32, own)
        kT = sb("b_kT", [P, KT, P], F32, own)
        kx = sb("b_kx", [P, KT, HPT, P], F32, own)
        val = sb("b_v", [P, D], F32, own)
        s = sb("b_s", [P, H1, P], F32, own)
        sT = kx[:, :, :, :].rearrange("p m h q -> p (m h) q")
        band = sb("b_band", [P, P], F32, own)
        diff = sb("b_diff", [P, KT], F32, own)
        flu = sb("b_flu", [P, KT], F32, own)
        sg = sb("b_sg", [P, 10], F32, own)
        mx = sb("b_mx", [P, H1], F32, own)
        sm = sb("b_sm", [P, H1], F32, own)
        rd = sb("b_rd", [P, H1], F32, own)
        o = sb("b_o", [P, D], F32, own)
        oT = sb("b_oT", [P, KT, P], F32, own)
        o2T = sb("b_o2T", [P, KT, P], F32, own)
        wox = sb("b_wox", [P, KT, HPT, DH1], F32, own)

        def by_head(x):
            return x.rearrange("p (h d) -> p h d", h=H1)

        with nc.Block() as block:
            @block.sync
            def _(sp):
                sp.dma_start(v["wg0"][:, :, :], t["wg0"]).then_inc(sem("router0_in"), 16)
                sp.dma_start(v["bg"][:, :], t["bg"].partition_broadcast(P)).then_inc(sem("router0_in"), 16)
                sp.dma_start(v["b2"][:, :], t["b2"]).then_inc(sem("router0_in"), 16)
                sp.dma_start(v["w1"][:, :, :, :], t["w1"]).then_inc(sem("w1_in"), 16)
                sp.dma_start(v["b1"][:, :, :].rearrange("p e f -> p (e f)"), t["b1"].partition_broadcast(P)).then_inc(sem("b1_in"), 16)
                sp.dma_start(v["w2"][:, :, :], t["w2"]).then_inc(sem("w2_in"), 16)
                sp.dma_start(v["wx"][:, :, :], t["wx"]).then_inc(sem("wx_in"), 16)
                sp.dma_start(v["bx"][:, :], t["bx"]).then_inc(sem("wx_in"), 16)
                sp.dma_start(v["wxp"][:, :, :], t["wxp"]).then_inc(sem("late_in"), 16)
                sp.dma_start(v["wdt"][:, :], t["wdt"]).then_inc(sem("late_in"), 16)
                sp.dma_start(v["bdt"][:, :], t["bdt"]).then_inc(sem("late_in"), 16)
                sp.dma_start(v["dskip"][:, :], t["dskip"].partition_broadcast(P)).then_inc(sem("late_in"), 16)
                sp.dma_start(v["wr1"][:, :, :], t["wr1"]).then_inc(sem("late_in"), 16)
                sp.dma_start(v["br1"][:, :], t["br1"].partition_broadcast(P)).then_inc(sem("late_in"), 16)
                sp.dma_start(v["wg"][:, :, :], t["wg1"]).then_inc(sem("mix1_in"), 16)
                sp.dma_start(v["wu"][:, :, :], t["wu1"]).then_inc(sem("mix1_in"), 16)

            @block.vector
            def _(dve):
                norm_vector(dve, 1)
                dve.wait_ge(sem("consts_ready"), 1)
                dve.wait_ge(sem("band_in"), 112)
                dve.wait_ge(sem("xnT_ready"), 2)
                link(dve, nc.vector.tensor_tensor(diff[:, :], xnT[:, :, P - 1], xnT[:, :, P - 2], ALU.subtract), "band_chain")
                nc.vector.scalar_tensor_tensor(flu[:, :], diff[:, :], -1.0, diff[:, :], ALU.mult,
                                               ALU.max).then_inc(sem("fluct_ready"), 1)
                nc.vector.tensor_tensor(dist[:, :], v["disti"][:, 0, :], v["disti"][:, 1, :], ALU.max)
                for m in range(KT):
                    nc.vector.tensor_tensor(wox[:, m, :, :], v["awo"][:, m, :].unsqueeze(1).broadcast_to([P, HPT, DH1]),
                                            hmask[:, :].unsqueeze(2).broadcast_to([P, HPT, DH1]),
                                            ALU.mult).then_inc(sem("wox_ready"), 1)
                dve.wait_ge(sem("qk1_done"), 1)
                for m in range(KT):
                    nc.vector.tensor_scalar(qT[:, m, :], ps[:, 0, m * P:(m + 1) * P], v["abqk"][:, m:m + 1], None,
                                            ALU.add).then_inc(sem("qk1_ready"), 1)
                    link(dve, nc.vector.tensor_scalar(kT[:, m, :], ps[:, 0, D + m * P:D + (m + 1) * P],
                                                      v["abqk"][:, KT + m:KT + m + 1], None, ALU.add), "band_chain")
                    nc.vector.tensor_tensor(kx[:, m, :, :], kT[:, m, :].unsqueeze(1).broadcast_to([P, HPT, P]),
                                            hmask[:, :].unsqueeze(2).broadcast_to([P, HPT, P]),
                                            ALU.mult).then_inc(sem("qk1_ready"), 1)
                dve.wait_ge(sem("ea_ready"), 1)
                link(dve, nc.vector.tensor_scalar(sg[:, 1:2], sg[:, 0:1], 1.0, None, ALU.add), "band_chain")
                link(dve, nc.vector.reciprocal(sg[:, 2:3], sg[:, 1:2]), "band_chain")
                link(dve, nc.vector.tensor_scalar(sg[:, 3:4], sg[:, 2:3], -1.0, 1.0, ALU.mult, ALU.add), "band_chain")
                dve.wait_ge(sem("fluct_sum"), 1)
                link(dve, nc.vector.tensor_scalar(sg[:, 4:5], ps[:, 6, 0:1], 1.0 / D, None, ALU.mult), "band_chain")
                link(dve, nc.vector.tensor_tensor(sg[:, 5:6], sg[:, 4:5], sg[:, 2:3], ALU.mult), "band_chain")
                nc.vector.scalar_tensor_tensor(sg[:, 6:7], ps[:, 6, 1:2], sg[:, 3:4], sg[:, 5:6], ALU.mult,
                                               ALU.add).then_inc(sem("signal_ready"), 1)
                dve.wait_ge(sem("es_ready"), 1)
                link(dve, nc.vector.tensor_scalar(sg[:, 8:9], sg[:, 7:8], 1.0, None, ALU.add), "band_chain")
                link(dve, nc.vector.reciprocal(sg[:, 8:9], sg[:, 8:9]), "band_chain")
                link(dve, nc.vector.tensor_scalar(sg[:, 9:10], sg[:, 8:9], MAX_W - MIN_W, MIN_W, ALU.mult, ALU.add), "band_chain")
                link(dve, nc.vector.tensor_scalar(band[:, :], dist[:, :], sg[:, 9:10], -BIG, ALU.is_gt, ALU.mult), "band_chain")
                dve.wait_ge(sem("s1_done"), 1)
                link(dve, nc.vector.scalar_tensor_tensor(s[:, :, :], ps[:, 2:6, :].rearrange("p b (h q) -> p (b h) q", h=4),
                                                         SCALE, band[:, :].unsqueeze(1).broadcast_to([P, H1, P]),
                                                         ALU.mult, ALU.add), "band_chain")
                link(dve, nc.vector.tensor_reduce(mx[:, :], s[:, :, :], AX_X, ALU.max), "band_chain")
                nc.vector.tensor_tensor(s[:, :, :], s[:, :, :], mx[:, :].unsqueeze(2).broadcast_to([P, H1, P]),
                                        ALU.subtract).then_inc(sem("s1_shifted"), 1)
                dve.wait_ge(sem("v1_done"), 1)
                nc.vector.tensor_copy(val[:, :], ps[:, 1, 0:D]).then_inc(sem("v1_ready"), 1)
                dve.wait_ge(sem("p1_ready"), 1)
                link(dve, nc.vector.tensor_reduce(sm[:, :], s[:, :, :], AX_X, ALU.add), "band_chain")
                link(dve, nc.vector.reciprocal(rd[:, :], sm[:, :]), "band_chain")
                dve.wait_ge(sem("p1_turned"), 2)
                nc.vector.tensor_copy(sT[:, 8:16, :], ps[:, 4:6, :].rearrange("p b (h q) -> p (b h) q", h=4)).then_inc(
                    sem("p1T_b"), 1)
                dve.wait_ge(sem("o1_done"), 1)
                nc.vector.tensor_tensor(by_head(o[:, :]), by_head(ps[:, 6, 0:D]),
                                        rd[:, :].unsqueeze(2).broadcast_to([P, H1, DH1]),
                                        ALU.mult).then_inc(sem("o1_ready"), 1)
                dve.wait_ge(sem("o1_turned"), 1)
                nc.vector.tensor_copy(oT[:, :, :], ps[:, 7, 0:D].rearrange("p (k q) -> p k q", k=KT)).then_inc(sem("o1T_ready"), 1)
                dve.wait_ge(sem("o2_done"), 1)
                nc.vector.tensor_copy(o2T[:, :, :], ps[:, 0, 0:D].rearrange("p (k q) -> p k q", k=KT)).then_inc(sem("o2T_ready"), 1)
                dve.wait_ge(sem("y1_done"), 1)
                nc.vector.tensor_tensor(res[:, :], res[:, :], ps[:, 1, 0:D], ALU.add).then_inc(sem("res_ready"), 1)

            @block.scalar
            def _(act):
                norm_scalar(act, 1)
                act.wait_ge(sem("band_in"), 112)
                nc.scalar.activation(sg[:, 0:1], v["alpha"][:, :], ACT.Exp, scale=-1.0).then_inc(sem("ea_ready"), 1)
                act.wait_ge(sem("signal_ready"), 1)
                nc.scalar.activation(sg[:, 7:8], sg[:, 6:7], ACT.Exp, scale=-1.0).then_inc(sem("es_ready"), 1)
                act.wait_ge(sem("s1_shifted"), 1)
                nc.scalar.activation(s[:, :, :], s[:, :, :], ACT.Exp).then_inc(sem("p1_ready"), 1)
                act.wait_ge(sem("p1_turned"), 1)
                nc.scalar.copy(sT[:, 0:8, :], ps[:, 2:4, :].rearrange("p b (h q) -> p (b h) q", h=4)).then_inc(sem("p1T_a"), 1)

            @block.tensor
            def _(pe):
                norm_tensor(pe, 1)
                pe.wait_ge(sem("band_in"), 112)
                for w, col in ((v["aq"], 0), (v["ak"], D)):
                    for m in range(KT):
                        for k in range(KT):
                            mm = nc.tensor.matmul(ps[:, 0, col + m * P:col + (m + 1) * P], w[:, k, m * P:(m + 1) * P],
                                                  xnT[:, k, :], start=(k == 0), stop=(k == KT - 1))
                mm.then_inc(sem("qk1_done"), 1)
                pe.wait_ge(sem("fluct_ready"), 1)
                for k in range(KT):
                    nc.tensor.matmul(ps[:, 6, 0:1], ones[:, :], flu[:, k:k + 1], start=(k == 0), stop=(k == KT - 1))
                nc.tensor.matmul(ps[:, 6, 1:2], row0[:, :], flu[:, 0:1], start=True, stop=True).then_inc(sem("fluct_sum"), 1)
                nc.tensor.matmul(ps[:, 1, 0:D], ones[0:1, :], v["brow"][0:1, D:2 * D], start=True, stop=False)
                for k in range(KT):
                    mm = nc.tensor.matmul(ps[:, 1, 0:D], xnT[:, k, :], v["av"][:, k, :], start=False, stop=(k == KT - 1))
                mm.then_inc(sem("v1_done"), 1)
                for m in range(KT):
                    pe.wait_ge(sem("qk1_ready"), 2 * m + 2)
                    for half in range(2):
                        mm = nc.tensor.matmul(ps[:, 2 + 2 * m + half, :], qT[:, m, :],
                                              kx[:, m, 4 * half:4 * half + 4, :].rearrange("p h q -> p (h q)"),
                                              start=True, stop=True)
                mm.then_inc(sem("s1_done"), 1)
                pe.wait_ge(sem("p1_ready"), 1)
                for h in range(H1):
                    mm = nc.tensor.transpose(ps[:, 2 + h // 4, (h % 4) * P:(h % 4 + 1) * P], s[:, h, :], ident[:, :])
                    if h % 8 == 7:
                        mm.then_inc(sem("p1_turned"), 1)
                pe.wait_ge(sem("v1_ready"), 1)
                for h in range(H1):
                    if h % 8 == 0:
                        pe.wait_ge(sem("p1T_a" if h == 0 else "p1T_b"), 1)
                    mm = nc.tensor.matmul(ps[:, 6, h * DH1:(h + 1) * DH1], sT[:, h, :], val[:, h * DH1:(h + 1) * DH1],
                                          start=True, stop=True)
                mm.then_inc(sem("o1_done"), 1)
                pe.wait_ge(sem("o1_ready"), 1)
                for k in range(KT):
                    mm = nc.tensor.transpose(ps[:, 7, k * P:(k + 1) * P], o[:, k * P:(k + 1) * P], ident[:, :])
                mm.then_inc(sem("o1_turned"), 1)
                pe.wait_ge(sem("wox_ready"), KT)
                pe.wait_ge(sem("o1T_ready"), 1)
                for m in range(KT):
                    mm = nc.tensor.matmul(ps[:, 0, m * P:(m + 1) * P], wox[:, m, :, :].rearrange("p h d -> p (h d)"),
                                          oT[:, m, :], start=True, stop=True)
                mm.then_inc(sem("o2_done"), 1)
                pe.wait_ge(sem("o2T_ready"), 1)
                nc.tensor.matmul(ps[:, 1, 0:D], ones[0:1, :], v["brow"][0:1, 2 * D:3 * D], start=True, stop=False)
                for k in range(KT):
                    mm = nc.tensor.matmul(ps[:, 1, 0:D], o2T[:, k, :], v["afc"][:, k, :], start=False, stop=(k == KT - 1))
                mm.then_inc(sem("y1_done"), 1)


def layout(inputs):
    import numpy as np

    a = {k: np.asarray(x) for k, x in inputs.items()}

    def rows(w):
        return w.reshape(w.shape[0] // P, P, -1).transpose(1, 0, 2)

    def cols(b):
        return b.reshape(-1, P).T

    def side_by_side(routed, shared):
        return rows(np.concatenate([a[routed].reshape(E1 * F1, D), a[shared]], 0).T)

    ctx = a["ctx_1024"][0]
    n = ctx.shape[0] // CK
    t = {
        "x": a["x"][0],
        "ctxN": ctx.reshape(n, NT, P, D).transpose(0, 2, 1, 3),
        "ctxT": ctx.reshape(n, CK, KT, P).transpose(0, 3, 2, 1),
        "wq0": rows(a["L0_xattn_Wq"]),
        "wk0": rows(a["L0_xattn_Wkv"][:, :H0 * DH0]),
        "wv0": rows(a["L0_xattn_Wkv"][:, H0 * DH0:]),
        "wo0": rows(a["L0_xattn_Wo"]),
        "brow": np.concatenate([a["L0_xattn_bo"], a["L0_attn_bv"], a["L0_attn_bfc"]])[None, :],
        "aq": rows(a["L0_attn_Wq"]), "ak": rows(a["L0_attn_Wk"]), "av": rows(a["L0_attn_Wv"]),
        "afc": rows(a["L0_attn_Wfc"]), "awo": rows(a["L0_attn_W_o"].reshape(D, DH1)),
        "abqk": np.concatenate([cols(a["L0_attn_bq"]), cols(a["L0_attn_bk"])], 1),
        "alpha": a["L0_attn_alpha"].reshape(1),
        "wg0": rows(a["L0_ffn_Wg"]), "bg": a["L0_ffn_bg"], "b2": a["L0_ffn_b2"],
        "w1": a["L0_ffn_W1"].reshape(E0, KT, P, F0).transpose(2, 1, 0, 3), "b1": a["L0_ffn_b1"].reshape(-1),
        "w2": rows(a["L0_ffn_W2"].reshape(E0 * F0, D)),
        "wx": rows(a["L1_xattn_W"].T), "bx": cols(a["L1_xattn_b"]),
        "mask": a["mask_BxS2_bk0"].reshape(n, CK),
        "wxp": rows(a["L1_attn_W_xproj"]), "wdt": a["L1_attn_W_dt"], "bdt": a["L1_attn_b_dt"][None, :],
        "dskip": a["L1_attn_D"], "alog": a["L1_attn_A_log"].reshape(-1),
        "wr1": rows(a["L1_ffn_gate_w"].T), "br1": a["L1_ffn_gate_bias"],
        "wg1": side_by_side("L1_ffn_expert_gate", "L1_ffn_shared_gate"),
        "wu1": side_by_side("L1_ffn_expert_up", "L1_ffn_shared_up"),
        "wd1": np.concatenate([a["L1_ffn_expert_down"].transpose(2, 0, 1),
                               a["L1_ffn_shared_down"].reshape(D, NS1, F1).transpose(2, 1, 0)], 1),
    }
    return {k: np.ascontiguousarray(x) for k, x in t.items()}


def kernel(**inputs):
    import numpy as np
    import concourse.bacc as _bacc
    from concourse import mybir as _mybir
    from concourse.bass_utils import run_bass_kernel_spmd as _run

    arrays = layout(inputs)
    nc = _bacc.Bacc("TRN2", target_bir_lowering=False, num_devices=1)
    t = {}
    for name, a in arrays.items():
        t[name] = nc.dram_tensor(f"in_{name}", a.shape, _mybir.dt.from_np(a.dtype), kind="ExternalInput").ap()
    out = nc.dram_tensor("out", (P, D), F32, kind="ExternalOutput").ap()
    build(nc, t, out)
    r = _run(nc, [{f"in_{k}": a for k, a in arrays.items()}], core_ids=[0])
    return np.asarray(r.results[0]["out"]).reshape(1, P, D)
```

```python
from contextlib import ExitStack

import concourse.bass as bass
from concourse import mybir

F32 = mybir.dt.float32
F32R = mybir.dt.float32r
BF16 = mybir.dt.bfloat16
I32 = mybir.dt.int32
U8 = mybir.dt.uint8
ALU = mybir.AluOpType
ACT = mybir.ActivationFunctionType
AX_X = mybir.AxisListType.X

P = 128
D = 256
KT = D // P
EPS = 1e-5
BIG = 1e30
NT = 7
CK = NT * P
HK = CK // 2
H0, DH0 = 16, 64
H1, DH1 = 16, 16
HPT = P // DH1
E0, F0 = 8, 512
E1, F1 = 32, 128
NS1 = 2
EA = E1 + NS1
GR, TG, TE = 4, 2, 8
NST, DTR = 16, 64


def build(nc, t, out):
    with ExitStack() as top:
        def sb(name, shape, dt=F32, ctx=top):
            return ctx.enter_context(nc.sbuf_tensor(name, shape, dt))

        ps = top.enter_context(nc.psum_tensor("ps", [P, 8, 512], F32))
        named = {}

        def sem(name):
            if name not in named:
                named[name] = top.enter_context(nc.semaphore(name))
            return named[name]

        count = {}

        def link(eng, ins, name):
            count[name] = count.get(name, 0) + 1
            ins.then_inc(sem(name), 1)
            eng.wait_ge(sem(name), count[name])

        v = {}

        def keep(name, shape, dt=F32):
            v[name] = sb(name, shape, dt)
            return v[name]

        res = keep("res", [P, D])
        xn = keep("xn", [P, D])
        xnT = keep("xnT", [P, KT, P])
        st6 = keep("st6", [P, 6])
        mv = keep("mv", [P, 2])
        vare = keep("vare", [P, 1])
        minus_half = keep("minus_half", [P, 1])
        rstd = keep("rstd", [P, 1])
        ident = keep("ident", [P, P])
        keep("ones", [P, P])
        keep("row0", [P, P])
        keep("tri", [P, P])
        keep("hmask", [P, HPT])
        keep("below", [P, E1, E1])
        keep("disti", [P, 2, P], I32)
        keep("dist", [P, P])
        keep("brow", [1, 3 * D])
        for name in ("aq", "ak", "av", "afc"):
            keep(name, [P, KT, D])
        keep("awo", [P, KT, DH1])
        keep("abqk", [P, 2 * KT])
        keep("alpha", [P, 1])
        keep("zero", [P, 1])
        keep("wg0", [P, KT, E0])
        keep("bg", [P, E0])
        keep("b2", [E0, D])
        keep("wx", [P, KT, D])
        keep("bx", [P, KT])
        keep("wxp", [P, KT, DTR + 2 * NST])
        keep("wdt", [DTR, D])
        keep("bdt", [1, D])
        keep("dskip", [P, D])
        keep("wr1", [P, KT, E1])
        keep("br1", [P, E1])

        def norm_vector(dve, n):
            if n > 0:
                dve.wait_ge(sem("res_ready"), n)
            link(dve, nc.vector.bn_stats(st6[:, :], res[:, :]), "norm_chain")
            link(dve, nc.vector.bn_aggr(mv[:, :], st6[:, :]), "norm_chain")
            nc.vector.tensor_scalar(vare[:, :], mv[:, 1:2], EPS, None, ALU.add).then_inc(sem("var_ready"), 1)
            dve.wait_ge(sem("rstd_ready"), n + 1)
            nc.vector.tensor_scalar(xn[:, :], res[:, :], mv[:, 0:1], rstd[:, 0:1], ALU.subtract,
                                    ALU.mult).then_inc(sem("xn_ready"), 1)
            dve.wait_ge(sem("xn_turned"), n + 1)
            nc.vector.tensor_copy(xnT[:, :, :], ps[:, 7, 0:D].rearrange("p (k q) -> p k q", k=KT)).then_inc(
                sem("xnT_ready"), 1)

        def norm_pool(pool, n):
            pool.wait_ge(sem("var_ready"), n + 1)
            nc.gpsimd.tensor_tensor(rstd[:, :], vare[:, :], minus_half[:, :], ALU.pow).then_inc(sem("rstd_ready"), 1)

        def norm_tensor(pe, n):
            pe.wait_ge(sem("xn_ready"), n + 1)
            for k in range(KT):
                mm = nc.tensor.transpose(ps[:, 7, k * P:(k + 1) * P], xn[:, k * P:(k + 1) * P], ident[:, :])
            mm.then_inc(sem("xn_turned"), 1)
            pe.wait_ge(sem("xnT_ready"), n + 1)

        norms = (norm_vector, norm_pool, norm_tensor)
        stage_context(nc, t, sb, sem, link, ps, norms, v)
        with ExitStack() as experts:
            v["wg"] = sb("wg", [P, KT, EA * F1], F32, experts)
            with ExitStack() as second:
                v["d_raw0"] = sb("d_raw0", [P, KT, CK], F32, second)
                for name, width in (("d_cTh", CK), ("d_cTl", CK), ("d_wxh", D), ("d_wxl", D)):
                    v[name] = sb(name, [P, KT, width], F32R, second)
                with ExitStack() as first:
                    v["w1"] = sb("w1", [P, KT, E0, F0], F32, first)
                    v["w2"] = sb("w2", [P, E0 * F0 // P, D], F32, first)
                    v["b1"] = sb("b1", [P, E0 * F0 // P], F32, first)
                    stage_band(nc, t, sb, sem, link, ps, norms, v)
                    stage_mix0(nc, t, sb, sem, link, ps, norms, v)
                stage_relu_context(nc, t, sb, sem, link, ps, norms, v)
            v["wu"] = sb("wu", [P, KT, EA * F1], F32, experts)
            v["wd"] = sb("wd", [P, EA, D], F32, experts)
            stage_scan(nc, t, sb, sem, link, ps, norms, v)
            stage_mix1(nc, t, sb, sem, link, ps, norms, v)
            finish(nc, sem, res, out, 6)


def finish(nc, sem, res, out, stages):
    with nc.Block() as block:
        @block.sync
        def _(sp):
            sp.wait_ge(sem("res_ready"), stages)
            sp.dma_start(out[:, :], res[:, :]).then_inc(sem("out_stored"), 16)
            sp.wait_ge(sem("out_stored"), 16)


def by_pair(x):
    return x[:, :, :].rearrange("p (m s) q -> p m s q", s=2)


def q_ps(ps):
    return ps[:, 0:2, :].rearrange("p b (m q) -> p (b m) q", q=P)


def stage_context(nc, t, sb, sem, link, ps, norms, v):
    norm_vector, norm_pool, norm_tensor = norms
    res, xnT, ident, ones = v["res"], v["xnT"], v["ident"], v["ones"]
    chunks = t["ctxN"].shape[0]
    pairs = chunks // 2
    steps = H0 * 2
    last = pairs - 1
    PIECES = H0
    FIRST = 8
    SCALE = DH0 ** -0.5
    W = H0 * DH0
    with ExitStack() as keep:
        U = sb("U", [P, H0, D], F32, keep)
        den = sb("den", [P, H0], F32, keep)
        with ExitStack() as loop:
            flat = U[:, :, :].rearrange("p h d -> p (h d)")
            wq = flat[:, 0:KT * W].rearrange("p (k n) -> p k n", k=KT)
            wk = flat[:, KT * W:2 * KT * W].rearrange("p (k n) -> p k n", k=KT)
            qh = sb("qh", [P, H0, P], F32R, loop)
            ql = sb("ql", [P, H0, P], F32R, loop)
            K = sb("K", [P, H0, CK], F32R, loop)
            raw = sb("raw", [P, CK * KT], F32, loop)
            rawT = raw[:, :].rearrange("p (k n) -> p k n", k=KT)
            rawN = raw[:, :].rearrange("p (t d) -> p t d", t=NT)
            cTh = [sb(f"cTh{i}", [P, KT, CK], F32R, loop) for i in range(2)]
            cTl = [sb(f"cTl{i}", [P, KT, CK], F32R, loop) for i in range(2)]
            cNh = [sb(f"cNh{i}", [P, NT, D], F32R, loop) for i in range(2)]
            cNl = [sb(f"cNl{i}", [P, NT, D], F32R, loop) for i in range(2)]
            prob = sb("prob", [P, 2, HK], F32, loop)
            pTh = sb("pTh", [P, CK], F32R, loop)
            pTl = sb("pTl", [P, CK], F32R, loop)
            nm = sb("nm", [P, 2, H0], F32, loop)
            nmx = sb("nmx", [P, 1], F32, loop)
            al = sb("al", [P, 2], F32, loop)
            rs = sb("rs", [P, 2], F32, loop)
            rden = sb("rden", [P, H0], F32, loop)
            with ExitStack() as keys:
                wkh = sb("wkh", [P, KT, W], F32R, keys)
                wkl = sb("wkl", [P, KT, W], F32R, keys)
            wv = sb("wv", [P, KT, W], F32, loop)
            wo = sb("wo", [P, H0 // 2, D], F32, loop)
            UT = raw[:, 0:2 * D].rearrange("p (s k q) -> p s k q", s=2, k=KT)
            oT = raw[:, 2 * D:2 * D + H0 // 2 * P].rearrange("p (m q) -> p m q", q=P)

            S = [ps[:, 2 * i:2 * i + 2, 0:HK] for i in range(2)]
            pT_ps = ps[:, 4:6, :].rearrange("p b n -> p (b n)")[:, 0:CK]
            O = ps[:, 6, 0:D]
            halves = (slice(0, DH0), slice(DH0, P))

            def piece_bank(g, first):
                return 4 + g % 4 if first else 7

            def piece_of(g, s):
                return 2 * (g // 2) + s, slice((g % 2) * HK, (g % 2 + 1) * HK)

            with nc.Block() as block:
                @block.sync
                def _(sp):
                    sp.dma_start(res[:, :], t["x"]).then_inc(sem("x_in"), 16)
                    sp.dma_start(wq, t["wq0"]).then_inc(sem("wq_in"), 16)
                    sp.dma_start(rawT[:, :, :], t["ctxT"][0]).then_inc(sem("rawT_in"), 16)
                    sp.dma_start(wk, t["wk0"]).then_inc(sem("wk_in"), 16)
                    sp.wait_ge(sem("cT_ready"), 1)
                    sp.dma_start(rawN[:, :, :], t["ctxN"][0]).then_inc(sem("rawN_in"), 16)
                    with sp.Fori(1, chunks) as c:
                        sp.wait_ge(sem("cN_ready"), c)
                        sp.dma_start(rawT[:, :, :], t["ctxT"][bass.ds(c, 1)].rearrange("o p k n -> p (o k) n")).then_inc(sem("rawT_in"), 16)
                        sp.wait_ge(sem("cT_ready"), c + 1)
                        sp.dma_start(rawN[:, :, :], t["ctxN"][bass.ds(c, 1)].rearrange("o p k n -> p (o k) n")).then_inc(sem("rawN_in"), 16)
                    sp.wait_ge(sem("piece_done"), PIECES * chunks)
                    sp.dma_start(wv[:, :, :], t["wv0"]).then_inc(sem("post_in"), 16)
                    sp.dma_start(wo[:, :, :], t["wo0"]).then_inc(sem("post_in"), 16)

                @block.gpsimd
                def _(pool):
                    def nought(x):
                        return v["zero"][:, 0:1].unsqueeze(2).broadcast_to([P, x.shape[1], x.shape[2]])

                    def split(raw, hi, lo, ready, n):
                        nc.gpsimd.tensor_tensor(hi[:, :, :], raw[:, :, :], nought(raw), ALU.add).then_inc(sem("split_hi"), 1)
                        pool.wait_ge(sem("split_hi"), n)
                        nc.gpsimd.tensor_tensor(lo[:, :, :], raw[:, :, :], hi[:, :, :].bitcast(F32),
                                                ALU.subtract).then_inc(sem(ready), 1)

                    link(pool, nc.gpsimd.memset(v["zero"][:, :], 0.0), "pool_chain")
                    link(pool, nc.gpsimd.memset(v["ident"][:, :], 0.0), "pool_chain")
                    nc.gpsimd.affine_select(out=v["ident"][:, :], in_=v["ident"][:, :], compare_op=ALU.not_equal,
                                            fill=1.0, base=0, pattern=[[1, P]],
                                            channel_multiplier=-1).then_inc(sem("ident_ready"), 1)
                    link(pool, nc.gpsimd.memset(v["minus_half"][:, :], -0.5), "pool_chain")
                    norm_pool(pool, 0)
                    pool.wait_ge(sem("rawT_in"), 16)
                    split(rawT, cTh[0], cTl[0], "cT_ready", 1)
                    pool.wait_ge(sem("rawN_in"), 16)
                    split(rawN, cNh[0], cNl[0], "cN_ready", 2)
                    pool.wait_ge(sem("q_done"), 1)
                    pool.wait_ge(sem("wk_split"), 2)
                    nc.gpsimd.memset(flat, 0.0).then_inc(sem("U_zeroed"), 1)
                    pool.wait_ge(sem("rawT_in"), 32)
                    split(rawT, cTh[1], cTl[1], "cT_ready", 3)
                    pool.wait_ge(sem("rawN_in"), 32)
                    split(rawN, cNh[1], cNl[1], "cN_ready", 4)
                    link(pool, nc.gpsimd.memset(v["ones"][:, :], 1.0), "pool_chain")
                    link(pool, nc.gpsimd.memset(v["row0"][:, :], 0.0), "pool_chain")
                    nc.gpsimd.memset(v["row0"][0:1, :], 1.0)
                    link(pool, nc.gpsimd.memset(v["hmask"][:, :], 1.0), "pool_chain")
                    link(pool, nc.gpsimd.affine_select(out=v["hmask"][:, :], in_=v["hmask"][:, :], compare_op=ALU.is_ge,
                                                       fill=0.0, base=0, pattern=[[-DH1, HPT]],
                                                       channel_multiplier=1), "pool_chain")
                    nc.gpsimd.affine_select(out=v["hmask"][:, :], in_=v["hmask"][:, :], compare_op=ALU.is_ge,
                                            fill=0.0, base=DH1 - 1, pattern=[[DH1, HPT]], channel_multiplier=-1)
                    nc.gpsimd.affine_select(out=v["tri"][:, :], in_=v["ones"][:, :], compare_op=ALU.is_ge,
                                            fill=0.0, base=0, pattern=[[1, P]], channel_multiplier=-1)
                    link(pool, nc.gpsimd.memset(v["below"][:, :, :], 1.0), "pool_chain")
                    nc.gpsimd.affine_select(out=v["below"][:, :, :], in_=v["below"][:, :, :], compare_op=ALU.is_gt,
                                            fill=0.0, base=0, pattern=[[1, E1], [-1, E1]], channel_multiplier=0)
                    nc.gpsimd.iota(v["disti"][:, 0, :], pattern=[[2, P]], base=0, channel_multiplier=-2)
                    nc.gpsimd.iota(v["disti"][:, 1, :], pattern=[[-2, P]], base=0,
                                   channel_multiplier=2).then_inc(sem("consts_ready"), 1)
                    with pool.Fori(1, pairs) as i:
                        for b in range(2):
                            pool.wait_ge(sem("rawT_in"), i * 32 + 16 * (b + 1))
                            pool.wait_ge(sem("piece_done"), i * (2 * PIECES) + PIECES * (b - 1))
                            split(rawT, cTh[b], cTl[b], "cT_ready", i * 4 + (2 * b + 1))
                            pool.wait_ge(sem("rawN_in"), i * 32 + 16 * (b + 1))
                            pool.wait_ge(sem("pv_done"), i * steps + H0 * (b - 1))
                            split(rawN, cNh[b], cNl[b], "cN_ready", i * 4 + (2 * b + 2))

                @block.scalar
                def _(act):
                    act.dma_start(v["brow"][:, :], t["brow"]).then_inc(sem("post_in"), 16)
                    for name in ("aq", "ak", "av", "afc", "awo"):
                        act.dma_start(v[name][:, :, :], t[name]).then_inc(sem("band_in"), 16)
                    act.dma_start(v["abqk"][:, :], t["abqk"]).then_inc(sem("band_in"), 16)
                    act.dma_start(v["alpha"][:, :], t["alpha"].partition_broadcast(P)).then_inc(sem("band_in"), 16)
                    act.wait_ge(sem("q_done"), 1)
                    for s in range(2):
                        for d in range(2):
                            nc.scalar.activation(by_pair(qh)[halves[d], :, s, :], q_ps(ps)[halves[s]], ACT.Copy,
                                                 scale=SCALE).then_inc(sem("qh_ready"), 1)

                    def high_parts(g, first=False):
                        for s in range(2):
                            h, cols = piece_of(g, s)
                            nc.scalar.copy(K[halves[s], h, cols], ps[halves[s], piece_bank(g, first), 0:HK]).then_inc(
                                sem("kh_ready"), 1)

                    def exp_step(u):
                        par, h, b = (u // H0) % 2, u % H0, u % 2
                        nc.scalar.activation(al[:, b:b + 1], nm[:, 1 - par, h:h + 1], ACT.Exp,
                                             bias=nm[:, par, h:h + 1], scale=-1.0)
                        nc.scalar.activation(prob[:, :, :], S[b], ACT.Exp, bias=nm[:, par, h:h + 1],
                                             scale=1.0, accum_out=rs[:, b:b + 1]).then_inc(sem("exp_done"), 1)

                    for g in range(PIECES):
                        if g == FIRST - 2:
                            act.wait_ge(sem("ql_ready"), 1)
                            for s in range(2):
                                ins = nc.scalar.copy(by_pair(ql)[halves[1 - s], :, s, :],
                                                     by_pair(ql)[halves[s], :, s, :].bitcast(F32))
                            ins.then_inc(sem("ql_doubled"), 1)
                        act.wait_ge(sem("piece_done"), g + 1)
                        high_parts(g, True)
                    act.wait_ge(sem("max_done"), 1)
                    exp_step(0)
                    def round_of(i, end):
                        for u in range(steps):
                            makes = not end or u < H0
                            act.wait_ge(sem("p_turned"), i * steps + (u + 1))
                            nc.scalar.activation(pTh[:, :], pT_ps, ACT.Copy).then_inc(sem("pTh_ready"), 1)
                            if makes:
                                g = u % H0
                                act.wait_ge(sem("piece_done"), i * steps + (PIECES * (u // H0 + 1) + g + 1))
                                high_parts(g)
                            if end and u + 1 == steps:
                                break
                            act.wait_ge(sem("max_done"), i * steps + (u + 2))
                            act.wait_ge(sem("pv_free"), i * steps + (u + 2))
                            exp_step(u + 1)
                            if not makes and u % 2 == 0 and u > H0:
                                turned_sums((u - H0) // 2 - 1)

                    def turned_sums(m):
                        act.wait_ge(sem("U_turned"), m + 1)
                        nc.scalar.copy(raw[:, 0:2 * D], ps[:, 7, :]).then_inc(sem("UT_ready"), 1)

                    with act.Fori(0, last) as i:
                        round_of(i, False)
                    round_of(last, True)
                    turned_sums(H0 // 2 - 1)

                @block.vector
                def _(dve):
                    dve.wait_ge(sem("x_in"), 16)
                    nc.vector.memset(den[:, :], 0.0)
                    nc.vector.memset(nm[:, :, :].rearrange("p a h -> p (a h)"), BIG).then_inc(sem("pv_free"), 2)
                    norm_vector(dve, 0)
                    dve.wait_ge(sem("wk_in"), 16)
                    nc.vector.tensor_copy(wkh[:, :, :], wk).then_inc(sem("wkh_ready"), 1)
                    dve.wait_ge(sem("wkh_ready"), 1)
                    nc.vector.tensor_tensor(wkl[:, :, :], wk, wkh[:, :, :].bitcast(F32), ALU.subtract).then_inc(sem("wk_split"), 2)
                    dve.wait_ge(sem("qh_ready"), 4)
                    for s in range(2):
                        ins = nc.vector.scalar_tensor_tensor(
                            by_pair(ql)[halves[s], :, s, :], q_ps(ps)[halves[s]], SCALE,
                            by_pair(qh)[halves[s], :, s, :].bitcast(F32), ALU.mult, ALU.subtract)
                    ins.then_inc(sem("ql_ready"), 1)

                    def low_parts(g, first=False):
                        for s in range(2):
                            h, cols = piece_of(g, s)
                            ins = nc.vector.tensor_tensor(K[halves[1 - s], h, cols], ps[halves[s], piece_bank(g, first), 0:HK],
                                                          K[halves[s], h, cols].bitcast(F32), ALU.subtract)
                        ins.then_inc(sem("kl_ready"), 1)

                    def max_step(u):
                        nc.vector.tensor_reduce(nmx[:, :], S[u % 2], mybir.AxisListType.XY, ALU.max,
                                                negate=True).then_inc(sem("chunk_max"), 1)

                    def new_max(u):
                        par, h = (u // H0) % 2, u % H0
                        nc.vector.tensor_tensor(nm[:, par, h:h + 1], nm[:, 1 - par, h:h + 1], nmx[:, :],
                                                ALU.min).then_inc(sem("max_done"), 1)

                    for g in range(PIECES):
                        dve.wait_ge(sem("kh_ready"), 2 * g + 2)
                        low_parts(g, True)
                        if g == FIRST + 1:
                            dve.wait_ge(sem("scores_done"), 1)
                            max_step(0)
                            dve.wait_ge(sem("chunk_max"), 1)
                            new_max(0)
                    dve.wait_ge(sem("U_zeroed"), 1)

                    def round_of(i, end):
                        for u in range(steps):
                            h, b = u % H0, u % 2
                            makes = not end or u < H0
                            if not (end and u + 1 == steps):
                                dve.wait_ge(sem("max_done"), i * steps + (u + 1))
                                dve.wait_ge(sem("scores_done"), i * steps + (u + 2))
                                max_step(u + 1)
                                dve.wait_ge(sem("chunk_max"), i * steps + (u + 2))
                                new_max(u + 1)
                            dve.wait_ge(sem("pTh_ready"), i * steps + (u + 1))
                            nc.vector.tensor_tensor(pTl[:, :], pT_ps, pTh[:, :].bitcast(F32),
                                                    ALU.subtract).then_inc(sem("pTl_ready"), 1)
                            if makes:
                                dve.wait_ge(sem("kh_ready"), i * (2 * steps) + 2 * (PIECES * (u // H0 + 1) + h + 1))
                                low_parts(h)
                            elif h % 2 == 1 and h > 1:
                                outputs(h // 2 - 1)
                            elif h > 1:
                                scale_sums(h // 2 - 1)
                            dve.wait_ge(sem("pv_free"), i * steps + (u + 2))
                            nc.vector.scalar_tensor_tensor(den[:, h:h + 1], den[:, h:h + 1], al[:, b:b + 1],
                                                           rs[:, b:b + 1], ALU.mult, ALU.add)
                            dve.wait_ge(sem("pv_done"), i * steps + (u + 1))
                            nc.vector.scalar_tensor_tensor(U[:, h, :], U[:, h, :], al[:, b:b + 1], O,
                                                           ALU.mult, ALU.add).then_inc(sem("pv_free"), 1)

                    def scale_sums(m):
                        h = 2 * m
                        dve.wait_ge(sem("pv_free"), 2 + H0 * (chunks - 1) + h + 2)
                        link(dve, nc.vector.reciprocal(rden[:, h:h + 2], den[:, h:h + 2]), "post_chain")
                        nc.vector.tensor_scalar(U[:, h, :], U[:, h, :], rden[:, h:h + 1], None, ALU.mult)
                        nc.vector.tensor_scalar(U[:, h + 1, :], U[:, h + 1, :], rden[:, h + 1:h + 2], None,
                                                ALU.mult).then_inc(sem("U_scaled"), 1)

                    def outputs(m):
                        dve.wait_ge(sem("projected"), m + 1)
                        nc.vector.tensor_copy(oT[halves[0], m, :], ps[halves[0], 7, 0:P])
                        nc.vector.tensor_copy(oT[halves[1], m, :], ps[halves[0], 7, P:2 * P]).then_inc(sem("oT_ready"), 1)

                    with dve.Fori(0, last) as i:
                        round_of(i, False)
                    round_of(last, True)
                    scale_sums(H0 // 2 - 1)
                    outputs(H0 // 2 - 1)
                    dve.wait_ge(sem("y0_done"), 1)
                    nc.vector.tensor_tensor(res[:, :], res[:, :], ps[:, 0, 0:D], ALU.add).then_inc(sem("res_ready"), 1)

                @block.tensor
                def _(pe):
                    pe.wait_ge(sem("ident_ready"), 1)
                    norm_tensor(pe, 0)
                    pe.wait_ge(sem("wq_in"), 16)
                    for m in range(H0 // 2):
                        for k in range(KT):
                            mm = nc.tensor.matmul(ps[:, m // 4, (m % 4) * P:(m % 4 + 1) * P], wq[:, k, m * P:(m + 1) * P],
                                                  xnT[:, k, :], start=(k == 0), stop=(k == KT - 1))
                    mm.then_inc(sem("q_done"), 1)

                    def piece(g, b, first=False):
                        m, n = g // 2, 0
                        for w, c in ((wkh, cTh[b]), (wkl, cTh[b]), (wkh, cTl[b])):
                            if first and g == 0 and n == KT:
                                pe.wait_ge(sem("wk_split"), 2)
                            if first and g == 0 and n == 2 * KT:
                                pe.wait_ge(sem("cT_ready"), 1)
                            for k in range(KT):
                                mm = nc.tensor.matmul(ps[:, piece_bank(g, first), 0:HK], w[:, k, m * P:(m + 1) * P],
                                                      c[:, k, (g % 2) * HK:(g % 2 + 1) * HK],
                                                      start=(n == 0), stop=(n == 3 * KT - 1))
                                n += 1
                        mm.then_inc(sem("piece_done"), 1)

                    def scores(u):
                        h, b = u % H0, u % 2
                        for half in range(2):
                            cols = slice(half * HK, (half + 1) * HK)
                            nc.tensor.matmul(S[b][:, half, :], qh[:, h, :], K[:, h, cols], start=True, stop=False)
                            mm = nc.tensor.matmul(S[b][:, half, :], ql[:, h, :], K[:, h, cols], start=False, stop=True)
                        mm.then_inc(sem("scores_done"), 1)

                    pe.wait_ge(sem("split_hi"), 1)
                    pe.wait_ge(sem("wkh_ready"), 1)
                    for g in range(PIECES):
                        if g >= 4:
                            pe.wait_ge(sem("kl_ready"), g - 3)
                        piece(g, 0, True)
                        if g == FIRST:
                            pe.wait_ge(sem("ql_doubled"), 1)
                            scores(0)
                            scores(1)
                    pe.wait_ge(sem("kl_ready"), PIECES)

                    def round_of(i, end):
                        for u in range(steps):
                            c, g = u // H0, u % H0
                            pe.wait_ge(sem("exp_done"), i * steps + (u + 1))
                            for k in range(NT):
                                mm = nc.tensor.transpose(pT_ps[:, k * P:(k + 1) * P],
                                                         prob[:, :, :].rearrange("p a n -> p (a n)")[:, k * P:(k + 1) * P],
                                                         ident[:, :])
                            mm.then_inc(sem("p_turned"), 1)
                            makes = not end or c == 0
                            if makes:
                                if g == 0:
                                    pe.wait_ge(sem("cT_ready"), i * 2 + (c + 2))
                                pe.wait_ge(sem("kl_ready"), i * steps + (PIECES * (c + 1) + g))
                                piece(g, (c + 1) % 2)
                            if not (end and u + 2 >= steps):
                                if u % 2 == 0:
                                    pe.wait_ge(sem("kl_ready"), i * steps + ((u + 2) // H0 * PIECES + (u + 2) % H0 + 2))
                                scores(u + 2)
                            if not makes and g % 2 == 1 and g > 1:
                                project(g // 2 - 1)
                            if g == 0:
                                pe.wait_ge(sem("cN_ready"), i * 2 + (c + 1))
                            pe.wait_ge(sem("pv_free"), i * steps + (u + 2))
                            pe.wait_ge(sem("pTh_ready"), i * steps + (u + 1))
                            n = 0
                            for p, cn in ((pTh, cNh[c]), (pTh, cNl[c]), (pTl, cNh[c])):
                                if n == 2 * NT:
                                    pe.wait_ge(sem("pTl_ready"), i * steps + (u + 1))
                                for k in range(NT):
                                    mm = nc.tensor.matmul(O, p[:, k * P:(k + 1) * P], cn[:, k, :],
                                                          start=(n == 0), stop=(n == 3 * NT - 1))
                                    n += 1
                            mm.then_inc(sem("pv_done"), 1)
                            if not makes and g % 2 == 0 and g > 0:
                                turn(g // 2 - 1)

                    def turn(m):
                        if m == 0:
                            pe.wait_ge(sem("kl_ready"), PIECES * chunks)
                        else:
                            pe.wait_ge(sem("oT_ready"), m)
                        pe.wait_ge(sem("U_scaled"), m + 1)
                        for s in range(2):
                            for k in range(KT):
                                col = s * D + k * P
                                mm = nc.tensor.transpose(ps[:, 7, col:col + P], U[:, 2 * m + s, k * P:(k + 1) * P],
                                                         ident[:, :])
                        mm.then_inc(sem("U_turned"), 1)

                    def project(m):
                        if m == 0:
                            pe.wait_ge(sem("post_in"), 48)
                        pe.wait_ge(sem("UT_ready"), m + 1)
                        for s in range(2):
                            for k in range(KT):
                                mm = nc.tensor.matmul(ps[0:DH0, 7, s * P:(s + 1) * P],
                                                      wv[:, k, (2 * m + s) * DH0:(2 * m + s + 1) * DH0], UT[:, s, k, :],
                                                      start=(k == 0), stop=(k == KT - 1))
                        mm.then_inc(sem("projected"), 1)

                    with pe.Fori(0, last) as i:
                        round_of(i, False)
                    round_of(last, True)
                    pe.wait_ge(sem("consts_ready"), 1)
                    pe.wait_ge(sem("oT_ready"), H0 // 2 - 1)
                    nc.tensor.matmul(ps[:, 0, 0:D], ones[0:1, :], v["brow"][0:1, 0:D], start=True, stop=False)
                    for m in range(H0 // 2):
                        if m == H0 // 4:
                            turn(H0 // 2 - 1)
                        if m == H0 // 2 - 1:
                            project(m)
                            pe.wait_ge(sem("oT_ready"), m + 1)
                        mm = nc.tensor.matmul(ps[:, 0, 0:D], oT[:, m, :], wo[:, m, :], start=False,
                                              stop=(m == H0 // 2 - 1))
                    mm.then_inc(sem("y0_done"), 1)


def stage_mix1(nc, t, sb, sem, link, ps, norms, v):
    norm_vector, norm_pool, norm_tensor = norms
    res, xnT = v["res"], v["xnT"]
    wg, wu, wd, below = v["wg"], v["wu"], v["wd"], v["below"]
    FACTOR = 2.5
    EB = 4
    blocks = [range(e, min(e + EB, EA)) for e in range(0, EA, EB)]
    with ExitStack() as own:
        sc = sb("f_sc", [P, E1], F32, own)
        ch = sb("f_ch", [P, E1], F32, own)
        best = sb("f_best", [P, GR, 8], F32, own)
        gs = sb("f_gs", [P, GR], F32, own)
        gsel = sb("f_gsel", [P, GR], F32, own)
        grank = sb("f_grank", [P, GR], F32, own)
        gw = sb("f_gw", [P, GR, GR], F32, own)
        gt = sb("f_gt", [P, GR, GR], F32, own)
        top = sb("f_top", [P, TE], F32, own)
        over = sb("f_over", [P, E1], F32, own)
        same = sb("f_same", [P, E1], F32, own)
        PAD = E1 // 2
        run = [sb(f"f_run{i}", [P, PAD + E1], F32, own) for i in range(2)]
        sel = sb("f_sel", [P, E1], F32, own)
        one = sb("f_one", [P, 2], F32, own)
        comb = sb("f_comb", [P, EA], F32, own)
        gate = [sb(f"f_gate{i}", [P, EB * F1], F32, own) for i in range(2)]
        act_ = [sb(f"f_act{i}", [P, EB, P], F32, own) for i in range(2)]
        acc = [res[:, :], sb("f_acc", [P, D], F32, own)[:, :]]

        def y_of(n, j):
            return ps[:, 4 + 2 * (n % 2) + j // 2, (j % 2) * D:(j % 2 + 1) * D]

        with nc.Block() as block:
            @block.vector
            def _(dve):
                for i in range(2):
                    nc.vector.memset(run[i][:, 0:PAD], 0.0)
                norm_vector(dve, 5)

                def gated(n):
                    b, w = n % 2, len(blocks[n]) * P
                    dve.wait_ge(sem("gate_ready"), n + 1)
                    if n >= 2:
                        dve.wait_ge(sem("y5_part"), EB // 2 * (n - 1))
                    nc.vector.tensor_tensor(act_[b][:, :, :].rearrange("p e q -> p (e q)")[:, 0:w], gate[b][:, 0:w],
                                            ps[:, 2 + b, 0:w], ALU.mult).then_inc(sem("act_ready"), 1)

                dve.wait_ge(sem("logits1_exp"), 1)
                link(dve, nc.vector.tensor_scalar(sc[:, :], sc[:, :], 1.0, None, ALU.add), "mix1_chain")
                link(dve, nc.vector.reciprocal(sc[:, :], sc[:, :]), "mix1_chain")
                link(dve, nc.vector.tensor_tensor(ch[:, :], sc[:, :], v["br1"][:, :], ALU.add), "mix1_chain")
                for k in range(GR):
                    ins = nc.vector.max(best[:, k, :], ch[:, k * 8:(k + 1) * 8])
                link(dve, ins, "mix1_chain")
                link(dve, nc.vector.tensor_tensor(gs[:, :], best[:, :, 0], best[:, :, 1], ALU.add), "mix1_chain")
                rank_select(nc, dve, link, "mix1_chain", gs[:, :], GR, TG, gw[:, :, :], gt[:, :, :], grank[:, :],
                            gsel[:, :], below)
                link(dve, nc.vector.tensor_tensor(ch[:, :].rearrange("p (g e) -> p g e", g=GR),
                                                  ch[:, :].rearrange("p (g e) -> p g e", g=GR),
                                                  gsel[:, :].unsqueeze(2).broadcast_to([P, GR, E1 // GR]), ALU.mult), "mix1_chain")
                gated(0)
                link(dve, nc.vector.max(top[:, :], ch[:, :]), "mix1_chain")
                link(dve, nc.vector.tensor_scalar(run[0][:, PAD:], ch[:, :], top[:, TE - 1:TE], None, ALU.is_equal), "mix1_chain")
                link(dve, nc.vector.tensor_scalar(over[:, :], ch[:, :], top[:, TE - 1:TE], None, ALU.is_gt), "mix1_chain")
                nc.vector.tensor_reduce(one[:, 0:1], over[:, :], AX_X, ALU.add)
                nc.vector.tensor_copy(same[:, :], run[0][:, PAD:])
                a, shift = 0, 1
                while shift < E1:
                    link(dve, nc.vector.tensor_tensor(run[1 - a][:, PAD:], run[a][:, PAD:],
                                                      run[a][:, PAD - shift:PAD + E1 - shift], ALU.add), "mix1_chain")
                    a, shift = 1 - a, 2 * shift
                link(dve, nc.vector.tensor_scalar(sel[:, :], run[a][:, PAD:], one[:, 0:1], float(TE), ALU.add,
                                                  ALU.is_le), "mix1_chain")
                link(dve, nc.vector.tensor_tensor(sel[:, :], sel[:, :], same[:, :], ALU.mult), "mix1_chain")
                link(dve, nc.vector.tensor_tensor(sel[:, :], sel[:, :], over[:, :], ALU.add), "mix1_chain")
                gated(1)
                link(dve, nc.vector.tensor_tensor(sel[:, :], sel[:, :], sc[:, :], ALU.mult), "mix1_chain")
                link(dve, nc.vector.tensor_reduce(one[:, 0:1], sel[:, :], AX_X, ALU.add), "mix1_chain")
                link(dve, nc.vector.tensor_scalar(one[:, 0:1], one[:, 0:1], 1e-20, None, ALU.add), "mix1_chain")
                link(dve, nc.vector.reciprocal(one[:, 1:2], one[:, 0:1]), "mix1_chain")
                nc.vector.memset(comb[:, E1:EA], 1.0)
                nc.vector.tensor_scalar(comb[:, 0:E1], sel[:, :], one[:, 1:2], FACTOR, ALU.mult,
                                        ALU.mult).then_inc(sem("comb1_ready"), 1)
                dve.wait_ge(sem("comb1_ready"), 1)

                def add(n):
                    for j, e in enumerate(blocks[n]):
                        if j % 2 == 0:
                            dve.wait_ge(sem("y5_part"), e // 2 + 1)
                        y, w = y_of(n, j), comb[:, e:e + 1]
                        if e == 1:
                            ins = nc.vector.tensor_scalar(acc[1], y, w, None, ALU.mult)
                        else:
                            if e > 1:
                                dve.wait_ge(sem("y5_added"), e - 1)
                            ins = nc.vector.scalar_tensor_tensor(acc[e % 2], y, w, acc[e % 2], ALU.mult, ALU.add)
                        ins.then_inc(sem("y5_added"), 1)

                for n in range(len(blocks)):
                    add(n)
                    if n + 2 < len(blocks):
                        gated(n + 2)
                dve.wait_ge(sem("y5_added"), EA)
                nc.vector.tensor_tensor(res[:, :], res[:, :], acc[1], ALU.add).then_inc(sem("res_ready"), 1)

            @block.gpsimd
            def _(pool):
                norm_pool(pool, 5)

            @block.scalar
            def _(act):
                act.wait_ge(sem("logits1_done"), 1)
                nc.scalar.activation(sc[:, :], ps[:, 6, 0:E1], ACT.Exp, scale=-1.0).then_inc(sem("logits1_exp"), 1)

                def silu(n):
                    b, w = n % 2, len(blocks[n]) * F1
                    act.wait_ge(sem("gu_done"), n + 1)
                    if n >= 2:
                        act.wait_ge(sem("act_ready"), n - 1)
                    nc.scalar.activation(gate[b][:, 0:w], ps[:, b, 0:w], ACT.Silu).then_inc(sem("gate_ready"), 1)

                for n in range(len(blocks)):
                    silu(n)

            @block.tensor
            def _(pe):
                norm_tensor(pe, 5)
                for k in range(KT):
                    mm = nc.tensor.matmul(ps[:, 6, 0:E1], xnT[:, k, :], v["wr1"][:, k, :], start=(k == 0), stop=(k == KT - 1))
                mm.then_inc(sem("logits1_done"), 1)
                pe.wait_ge(sem("mix1_in"), 32)
                pe.wait_ge(sem("wd_in"), 16)

                def gate_up(n):
                    if n >= 2:
                        pe.wait_ge(sem("act_ready"), n - 1)
                    for bank, m in ((n % 2, wg), (2 + n % 2, wu)):
                        for j, e in enumerate(blocks[n]):
                            for k in range(KT):
                                mm = nc.tensor.matmul(ps[:, bank, j * P:(j + 1) * P], m[:, k, e * F1:(e + 1) * F1],
                                                      xnT[:, k, :], start=(k == 0), stop=(k == KT - 1))
                    mm.then_inc(sem("gu_done"), 1)

                def down(n):
                    pe.wait_ge(sem("act_ready"), n + 1)
                    if n >= 2:
                        pe.wait_ge(sem("y5_added"), EB * (n - 1))
                    for j, e in enumerate(blocks[n]):
                        mm = nc.tensor.matmul(y_of(n, j), act_[n % 2][:, j, :], wd[:, e, :], start=True, stop=True)
                        if j % 2 == 1:
                            mm.then_inc(sem("y5_part"), 1)

                gate_up(0)
                pe.wait_ge(sem("logits1_exp"), 1)
                for n in range(len(blocks)):
                    if n + 1 < len(blocks):
                        gate_up(n + 1)
                    down(n)


def stage_scan(nc, t, sb, sem, link, ps, norms, v):
    norm_vector, norm_pool, norm_tensor = norms
    res, xn, xnT, ones, tri = v["res"], v["xn"], v["xnT"], v["ones"], v["tri"]
    LOG_EPS, CLAMP = -7.0, 20.0
    BD = 64
    NB = D // BD
    W = BD * NST
    with ExitStack() as own:
        ea = sb("e_ea", [P, D * NST], F32, own)
        dtT = sb("e_dtT", [DTR, P], F32, own)
        bc = sb("e_bc", [P, 2 * NST], F32, own)
        z = sb("e_z", [P, D], F32, own)
        pos = sb("e_pos", [P, D], F32, own)
        u = sb("e_u", [P, D], F32, own)
        s1 = sb("e_s", [P, D], F32, own)
        s2 = sb("e_s2", [P, D], F32, own)
        poly = sb("e_poly", [P, D], F32, own)
        delta = sb("e_delta", [P, D], F32, own)
        dx = sb("e_dx", [P, D], F32, own)
        y = sb("e_y", [P, D], F32, own)
        la = [sb(f"e_la{i}", [P, W], F32, own) for i in range(NB)]
        R = [sb(f"e_R{i}", [P, W], F32, own) for i in range(2)]
        inv = [sb(f"e_inv{i}", [P, W], F32, own) for i in range(2)]
        g = [sb(f"e_g{i}", [P, W], F32, own) for i in range(2)]

        def cn(x):
            return x.rearrange("p (c n) -> p c n", n=NST)

        def over_states(x):
            return x.unsqueeze(2).broadcast_to([P, BD, NST])

        def over_channels(x):
            return x.unsqueeze(1).broadcast_to([P, BD, NST])

        def bank2(n):
            return ps[:, n:n + 2, :].rearrange("p b n -> p (b n)")

        with nc.Block() as block:
            @block.sync
            def _(sp):
                sp.dma_start(ea[:, :], t["alog"].partition_broadcast(P)).then_inc(sem("alog_in"), 16)
                sp.dma_start(v["wu"][:, :, :], t["wu1"]).then_inc(sem("mix1_in"), 16)
                sp.dma_start(v["wd"][:, :, :], t["wd1"]).then_inc(sem("wd_in"), 16)

            @block.gpsimd
            def _(pool):
                norm_pool(pool, 4)
                def inputs(n):
                    b, cols = n % 2, slice(n * BD, (n + 1) * BD)
                    if n >= 2:
                        pool.wait_ge(sem("sum_done"), n - 1)
                    nc.gpsimd.tensor_tensor(cn(g[b][:, :]), over_states(dx[:, cols]), over_channels(bc[:, 0:NST]),
                                            ALU.mult).then_inc(sem("g_ready"), 1)

                pool.wait_ge(sem("dx_ready"), 1)
                pool.wait_ge(sem("bc_ready"), 1)
                inputs(0)
                pool.wait_ge(sem("ea_done"), 1)
                for n in range(2, NB):
                    nc.gpsimd.tensor_tensor(cn(la[n][:, :]), over_states(delta[:, n * BD:(n + 1) * BD]),
                                            cn(ea[:, n * W:(n + 1) * W]), ALU.mult).then_inc(sem("la_product"), 1)
                inputs(1)
                for n in range(NB):
                    b = n % 2
                    pool.wait_ge(sem("R_ready"), n + 1)
                    nc.gpsimd.tensor_tensor(cn(R[b][:, :]), cn(R[b][:, :]), over_channels(bc[:, NST:2 * NST]),
                                            ALU.mult).then_inc(sem("CR_ready"), 1)
                    if n + 2 < NB:
                        inputs(n + 2)

            @block.scalar
            def _(act):
                act.wait_ge(sem("absz_ready"), 1)
                nc.scalar.activation(u[:, :], u[:, :], ACT.Exp, scale=-1.0).then_inc(sem("u_ready"), 1)
                act.wait_ge(sem("alog_in"), 16)
                nc.scalar.activation(ea[:, :], ea[:, :], ACT.Exp).then_inc(sem("ea_done"), 1)
                for n in range(NB):
                    b = n % 2
                    act.wait_ge(sem("neg_ready"), n + 1)
                    nc.scalar.activation(inv[b][:, :], inv[b][:, :], ACT.Exp).then_inc(sem("inv_ready"), 1)
                    if n >= 2:
                        act.wait_ge(sem("y4_ready"), n - 1)
                    nc.scalar.activation(R[b][:, :], bank2(2 * b), ACT.Exp).then_inc(sem("R_ready"), 1)

            @block.vector
            def _(dve):
                norm_vector(dve, 4)
                dve.wait_ge(sem("dt_done"), 1)
                nc.vector.tensor_copy(dtT[:, :], ps[0:DTR, 4, 0:P]).then_inc(sem("dtT_ready"), 1)
                nc.vector.tensor_copy(bc[:, :], ps[:, 5, 0:2 * NST]).then_inc(sem("bc_ready"), 1)
                dve.wait_ge(sem("z_done"), 1)
                link(dve, nc.vector.tensor_copy(z[:, :], ps[:, 6, 0:D]), "scan_chain")
                nc.vector.scalar_tensor_tensor(u[:, :], z[:, :], -1.0, z[:, :], ALU.mult, ALU.max).then_inc(sem("absz_ready"), 1)
                nc.vector.tensor_scalar(pos[:, :], z[:, :], 0.0, None, ALU.max)
                dve.wait_ge(sem("u_ready"), 1)
                steps = 0

                def halved(op):
                    nonlocal steps
                    for cols in (slice(0, D // 2), slice(D // 2, D)):
                        if steps >= 2:
                            dve.wait_ge(sem("softplus_steps"), steps - 1)
                        op(cols).then_inc(sem("softplus_steps"), 1)
                        steps += 1

                halved(lambda c: nc.vector.tensor_scalar(s1[:, c], u[:, c], 2.0, None, ALU.add))
                halved(lambda c: nc.vector.reciprocal(s1[:, c], s1[:, c]))
                halved(lambda c: nc.vector.tensor_tensor(s1[:, c], s1[:, c], u[:, c], ALU.mult))
                halved(lambda c: nc.vector.tensor_tensor(s2[:, c], s1[:, c], s1[:, c], ALU.mult))
                halved(lambda c: nc.vector.tensor_scalar(poly[:, c], s2[:, c], 1.0 / 15, None, ALU.mult))
                for k in (13, 11, 9, 7, 5, 3):
                    halved(lambda c: nc.vector.scalar_tensor_tensor(poly[:, c], poly[:, c], 1.0 / k, s2[:, c], ALU.add, ALU.mult))
                halved(lambda c: nc.vector.scalar_tensor_tensor(poly[:, c], poly[:, c], 1.0, s1[:, c], ALU.add, ALU.mult))
                halved(lambda c: nc.vector.scalar_tensor_tensor(delta[:, c], poly[:, c], 2.0, pos[:, c], ALU.mult, ALU.add))
                dve.wait_ge(sem("softplus_steps"), steps)
                nc.vector.tensor_tensor(dx[:, :], delta[:, :], xn[:, :], ALU.mult).then_inc(sem("dx_ready"), 1)
                dve.wait_ge(sem("ea_done"), 1)

                def decay(n):
                    if n < 2:
                        link(dve, nc.vector.tensor_tensor(cn(la[n][:, :]), over_states(delta[:, n * BD:(n + 1) * BD]),
                                                          cn(ea[:, n * W:(n + 1) * W]), ALU.mult), "scan_chain")
                    else:
                        dve.wait_ge(sem("la_product"), n - 1)
                    nc.vector.tensor_scalar(la[n][:, :], la[n][:, :], -1.0, LOG_EPS, ALU.mult, ALU.max).then_inc(sem("la_ready"), 1)

                def inputs(n):
                    b = n % 2
                    dve.wait_ge(sem("logR_done"), n + 1)
                    if n >= 2:
                        dve.wait_ge(sem("gi_ready"), n - 1)
                    nc.vector.tensor_scalar(inv[b][:, :], bank2(2 * b), -1.0, CLAMP, ALU.mult, ALU.min).then_inc(sem("neg_ready"), 1)

                def weighted(n):
                    b = n % 2
                    dve.wait_ge(sem("g_ready"), n + 1)
                    dve.wait_ge(sem("inv_ready"), n + 1)
                    nc.vector.tensor_tensor(g[b][:, :], g[b][:, :], inv[b][:, :], ALU.mult).then_inc(sem("gi_ready"), 1)

                def outputs(n):
                    b = n % 2
                    dve.wait_ge(sem("sum_done"), n + 1)
                    dve.wait_ge(sem("CR_ready"), n + 1)
                    link(dve, nc.vector.tensor_tensor(la[n][:, :], bank2(4 + 2 * b), R[b][:, :], ALU.mult), "scan_chain")
                    nc.vector.tensor_reduce(y[:, n * BD:(n + 1) * BD], cn(la[n][:, :]), AX_X, ALU.add).then_inc(sem("y4_ready"), 1)
                    dve.wait_ge(sem("y4_ready"), n + 1)

                decay(0)
                decay(1)
                dve.wait_ge(sem("late_in"), 96)
                link(dve, nc.vector.tensor_tensor(y[:, :], xn[:, :], v["dskip"][:, :], ALU.mult), "scan_chain")
                link(dve, nc.vector.tensor_tensor(res[:, :], res[:, :], y[:, :], ALU.add), "scan_chain")
                for n in range(NB):
                    inputs(n)
                    if n + 2 < NB:
                        decay(n + 2)
                    if n >= 2:
                        outputs(n - 2)
                    weighted(n)
                outputs(NB - 2)
                outputs(NB - 1)
                nc.vector.tensor_tensor(res[:, :], res[:, :], y[:, :], ALU.add).then_inc(sem("res_ready"), 1)

            @block.tensor
            def _(pe):
                norm_tensor(pe, 4)
                pe.wait_ge(sem("late_in"), 96)
                for k in range(KT):
                    mm = nc.tensor.matmul(ps[0:DTR, 4, 0:P], v["wxp"][:, k, 0:DTR], xnT[:, k, :], start=(k == 0), stop=(k == KT - 1))
                for k in range(KT):
                    mm = nc.tensor.matmul(ps[:, 5, 0:2 * NST], xnT[:, k, :], v["wxp"][:, k, DTR:DTR + 2 * NST],
                                          start=(k == 0), stop=(k == KT - 1))
                mm.then_inc(sem("dt_done"), 1)
                nc.tensor.matmul(ps[:, 6, 0:D], ones[0:1, :], v["bdt"][:, :], start=True, stop=False)
                pe.wait_ge(sem("dtT_ready"), 1)
                nc.tensor.matmul(ps[:, 6, 0:D], dtT[:, :], v["wdt"][:, :], start=False, stop=True).then_inc(sem("z_done"), 1)
                pe.wait_ge(sem("bc_ready"), 1)
                pe.wait_ge(sem("absz_ready"), 1)

                def log_R(n):
                    pe.wait_ge(sem("la_ready"), n + 1)
                    if n >= 2:
                        pe.wait_ge(sem("R_ready"), n - 1)
                        pe.wait_ge(sem("neg_ready"), n - 1)
                    for k in range(2):
                        mm = nc.tensor.matmul(ps[:, 2 * (n % 2) + k, :], tri[:, :], la[n][:, k * 512:(k + 1) * 512],
                                              start=True, stop=True)
                    mm.then_inc(sem("logR_done"), 1)

                def sums(n):
                    pe.wait_ge(sem("gi_ready"), n + 1)
                    if n >= 2:
                        pe.wait_ge(sem("y4_ready"), n - 1)
                    for k in range(2):
                        mm = nc.tensor.matmul(ps[:, 4 + 2 * (n % 2) + k, :], tri[:, :], g[n % 2][:, k * 512:(k + 1) * 512],
                                              start=True, stop=True)
                    mm.then_inc(sem("sum_done"), 1)

                log_R(0)
                log_R(1)
                for n in range(NB):
                    sums(n)
                    if n + 2 < NB:
                        log_R(n + 2)


def stage_relu_context(nc, t, sb, sem, link, ps, norms, v):
    norm_vector, norm_pool, norm_tensor = norms
    res, xnT, ident, wx, bx = v["res"], v["xnT"], v["ident"], v["wx"], v["bx"]
    chunks = t["ctxN"].shape[0]
    last = chunks // 2 - 1
    with ExitStack() as own:
        raw = [v["d_raw0"], sb("d_raw1", [P, KT, CK], F32, own)]
        cTh, cTl, wxh, wxl = (v[n] for n in ("d_cTh", "d_cTl", "d_wxh", "d_wxl"))
        mrow = [sb(f"d_mrow{i}", [1, CK], U8, own) for i in range(2)]
        mneg = [sb(f"d_mneg{i}", [1, CK], BF16, own) for i in range(2)]
        one_b = sb("d_one", [1, P], BF16, own)
        qT = sb("d_qT", [P, KT, P], F32, own)
        qh = sb("d_qh", [P, KT, P], F32R, own)
        ql = sb("d_ql", [P, KT, P], F32R, own)
        kT = sb("d_kT", [P, KT, CK], F32, own)
        kTh = sb("d_kTh", [P, KT, CK], F32R, own)
        kTl = sb("d_kTl", [P, KT, CK], F32R, own)
        kNh = [sb(f"d_kNh{i}", [P, NT, D], F32R, own) for i in range(2)]
        kNl = [sb(f"d_kNl{i}", [P, NT, D], F32R, own) for i in range(2)]
        prob = sb("d_prob", [P, 2, HK], F32, own)
        pTh = sb("d_pTh", [P, CK], F32R, own)
        pTl = sb("d_pTl", [P, CK], F32R, own)
        U = sb("d_U", [P, D], F32, own)
        den = sb("d_den", [P, 1], F32, own)
        rden = sb("d_rden", [P, 1], F32, own)
        nm = sb("d_nm", [P, 2], F32, own)
        nmx = sb("d_nmx", [P, 1], F32, own)
        al = sb("d_al", [P, 2], F32, own)
        rs = sb("d_rs", [P, 2], F32, own)
        S = ps[:, 2:4, 0:HK]
        O = ps[:, 6, 0:D]
        KG = 2 * KT
        NG = (NT + 1) // 2
        KB = [7, 4, 5, 7]
        PG = [range(0, 4), range(4, NT)]

        def part(x, g):
            return x[:, g // 2, (g % 2) * HK:(g % 2 + 1) * HK]

        def tiles_of(n):
            return slice(2 * n, min(2 * n + 2, NT))

        with nc.Block() as block:
            @block.sync
            def _(sp):
                sp.dma_start(raw[1][:, :, :], t["ctxT"][1]).then_inc(sem("dctx_in1"), 16)
                for b in range(2):
                    sp.dma_start(mrow[b][:, :], t["mask"][b:b + 1, :]).then_inc(sem(f"dmask_in{b}"), 16)
                with sp.Fori(1, chunks // 2) as i:
                    for b in range(2):
                        sp.wait_ge(sem("ds_done"), i * 2 + (b - 1))
                        sp.dma_start(raw[b][:, :, :], t["ctxT"][bass.ds(i * 2 + b, 1)].rearrange(
                            "o p k n -> p (o k) n")).then_inc(sem(f"dctx_in{b}"), 16)
                        sp.dma_start(mrow[b][:, :], t["mask"][bass.ds(i * 2 + b, 1), :]).then_inc(sem(f"dmask_in{b}"), 16)

            @block.gpsimd
            def _(pool):
                norm_pool(pool, 3)
                def split_low(b):
                    nc.gpsimd.tensor_tensor(cTl[:, :, :], raw[b][:, :, :], cTh[:, :, :].bitcast(F32),
                                            ALU.subtract).then_inc(sem("dcTl_ready"), 1)

                def keys_low(g):
                    nc.gpsimd.tensor_tensor(part(kTl, g), part(kT, g), part(kTh, g).bitcast(F32),
                                            ALU.subtract).then_inc(sem("dkTl_ready"), 1)

                for g in range(KG):
                    pool.wait_ge(sem("dkTh_ready"), g + 1)
                    keys_low(g)
                pool.wait_ge(sem("dcTh_ready"), 2)
                split_low(1)

                def round_of(i, end):
                    for b in range(2):
                        if end and b == 1:
                            break
                        for g in range(KG):
                            pool.wait_ge(sem("dkTh_ready"), i * (2 * KG) + (KG * (b + 1) + g + 1))
                            keys_low(g)
                        if not end:
                            pool.wait_ge(sem("dcTh_ready"), i * 2 + (b + 3))
                            split_low(b)

                with pool.Fori(0, last) as i:
                    round_of(i, False)
                round_of(last, True)

            @block.scalar
            def _(act):
                def keys(g):
                    nc.scalar.activation(part(kT, g), ps[:, g % 2, 0:HK], ACT.Relu, bias=bx[:, g // 2:g // 2 + 1],
                                         scale=1.0).then_inc(sem("dkT_ready"), 1)

                def split_high(b):
                    nc.scalar.copy(cTh[:, :, :], raw[b][:, :, :]).then_inc(sem("dcTh_ready"), 1)

                act.wait_ge(sem("wx_in"), 32)
                for g in range(2):
                    act.wait_ge(sem("dk_done"), g + 1)
                    keys(g)
                act.wait_ge(sem("dq_done"), 1)
                for m in range(KT):
                    nc.scalar.activation(qT[:, m, :], ps[:, 6, m * P:(m + 1) * P], ACT.Relu, bias=bx[:, m:m + 1],
                                         scale=1.0).then_inc(sem("dq_ready"), 1)

                def rows_high(b, n):
                    dst = kNh[b][:, tiles_of(n), :].rearrange("p a d -> p (a d)")
                    nc.scalar.copy(dst, ps[:, KB[n], 0:dst.shape[1]]).then_inc(sem("dkNh_ready"), 1)

                def exp_step(b):
                    nc.scalar.activation(al[:, b:b + 1], nm[:, 1 - b:2 - b], ACT.Exp, bias=nm[:, b:b + 1], scale=-1.0)
                    nc.scalar.activation(prob[:, :, :], S, ACT.Exp, bias=nm[:, b:b + 1], scale=1.0,
                                         accum_out=rs[:, b:b + 1]).then_inc(sem("dexp_done"), 1)

                for g in range(2, KG):
                    act.wait_ge(sem("dk_done"), g + 1)
                    keys(g)
                act.wait_ge(sem("dctx_in1"), 16)
                split_high(1)
                for n in range(NG):
                    act.wait_ge(sem("dk_turned"), n + 1)
                    rows_high(0, n)
                act.wait_ge(sem("dmax_done"), 1)
                exp_step(0)

                def round_of(i, end):
                    for b in range(2):
                        more = not (end and b == 1)
                        if more:
                            act.wait_ge(sem("dk_turned"), i * (2 * NG) + NG * (b + 1))
                            for g in range(KG):
                                act.wait_ge(sem("dk_done"), i * (2 * KG) + (KG * (b + 1) + g + 1))
                                keys(g)
                        if not end:
                            act.wait_ge(sem(f"dctx_in{b}"), i * 16 + 32)
                            split_high(b)
                        for n, tiles in enumerate(PG):
                            act.wait_ge(sem("dp_turned"), i * 4 + (2 * b + n + 1))
                            cols = slice(tiles[0] * P, (tiles[-1] + 1) * P)
                            nc.scalar.copy(pTh[:, cols], ps[:, 4 + n, 0:len(tiles) * P]).then_inc(sem("dpTh_ready"), 1)
                        if more:
                            for n in range(NG):
                                act.wait_ge(sem("dk_turned"), i * (2 * NG) + (NG * (b + 1) + n + 1))
                                rows_high(1 - b, n)
                            act.wait_ge(sem("dmax_done"), i * 2 + (b + 2))
                            act.wait_ge(sem("du_free"), i * 2 + (b + 2))
                            exp_step(1 - b)

                with act.Fori(0, last) as i:
                    round_of(i, False)
                round_of(last, True)

            @block.vector
            def _(dve):
                norm_vector(dve, 3)
                nc.vector.memset(one_b[:, :], 1.0).then_inc(sem("d_ones"), 1)
                nc.vector.memset(U[:, :], 0.0)
                nc.vector.memset(den[:, :], 0.0)
                nc.vector.memset(nm[:, :], BIG).then_inc(sem("du_free"), 2)
                dve.wait_ge(sem("dq_ready"), KT)
                link(dve, nc.vector.tensor_copy(qh[:, :, :], qT[:, :, :]), "relu_chain")
                nc.vector.tensor_tensor(ql[:, :, :], qT[:, :, :], qh[:, :, :].bitcast(F32),
                                        ALU.subtract).then_inc(sem("dq_split"), 1)

                def mask(b):
                    nc.vector.tensor_scalar(mneg[b][:, :], mrow[b][:, :], -BIG, None, ALU.mult).then_inc(sem("dmask_ready"), 1)

                def keys_high(g):
                    nc.vector.tensor_copy(part(kTh, g), part(kT, g)).then_inc(sem("dkTh_ready"), 1)

                def rows_low(b, n):
                    hi = kNh[b][:, tiles_of(n), :].rearrange("p a d -> p (a d)").bitcast(F32)
                    nc.vector.tensor_tensor(kNl[b][:, tiles_of(n), :].rearrange("p a d -> p (a d)"),
                                            ps[:, KB[n], 0:hi.shape[1]], hi, ALU.subtract).then_inc(sem("dkNl_ready"), 1)

                def chunk_max():
                    nc.vector.tensor_reduce(nmx[:, :], S, mybir.AxisListType.XY, ALU.max, negate=True).then_inc(sem("dchunk_max"), 1)

                def new_max(b):
                    nc.vector.tensor_tensor(nm[:, b:b + 1], nm[:, 1 - b:2 - b], nmx[:, :], ALU.min).then_inc(sem("dmax_done"), 1)

                dve.wait_ge(sem("dmask_in0"), 16)
                mask(0)
                for g in range(KG):
                    dve.wait_ge(sem("dkT_ready"), g + 1)
                    keys_high(g)
                for n in range(NG):
                    dve.wait_ge(sem("dkNh_ready"), n + 1)
                    rows_low(0, n)
                dve.wait_ge(sem("ds_done"), 1)
                chunk_max()
                dve.wait_ge(sem("dchunk_max"), 1)
                new_max(0)

                def round_of(i, end):
                    for b in range(2):
                        more = not (end and b == 1)
                        if more:
                            dve.wait_ge(sem("ds_done"), i * 2 + (b + 1))
                            dve.wait_ge(sem(f"dmask_in{1 - b}"), i * 16 + 16 * (b + 1))
                            mask(1 - b)
                            for g in range(KG):
                                dve.wait_ge(sem("dkT_ready"), i * (2 * KG) + (KG * (b + 1) + g + 1))
                                keys_high(g)
                        for n, tiles in enumerate(PG):
                            dve.wait_ge(sem("dpTh_ready"), i * 4 + (2 * b + n + 1))
                            cols = slice(tiles[0] * P, (tiles[-1] + 1) * P)
                            nc.vector.tensor_tensor(pTl[:, cols], ps[:, 4 + n, 0:len(tiles) * P],
                                                    pTh[:, cols].bitcast(F32), ALU.subtract).then_inc(sem("dpTl_ready"), 1)
                        if more:
                            dve.wait_ge(sem("dkNh_ready"), i * (2 * NG) + (NG * (b + 1) + 1))
                            rows_low(1 - b, 0)
                            dve.wait_ge(sem("dmax_done"), i * 2 + (b + 1))
                            dve.wait_ge(sem("ds_done"), i * 2 + (b + 2))
                            chunk_max()
                            dve.wait_ge(sem("dchunk_max"), i * 2 + (b + 2))
                            new_max(1 - b)
                            for n in range(1, NG):
                                dve.wait_ge(sem("dkNh_ready"), i * (2 * NG) + (NG * (b + 1) + n + 1))
                                rows_low(1 - b, n)
                        dve.wait_ge(sem("du_free"), i * 2 + (b + 2))
                        nc.vector.scalar_tensor_tensor(den[:, :], den[:, :], al[:, b:b + 1], rs[:, b:b + 1],
                                                       ALU.mult, ALU.add)
                        dve.wait_ge(sem("dpv_done"), i * 2 + (b + 1))
                        nc.vector.scalar_tensor_tensor(U[:, :], U[:, :], al[:, b:b + 1], O,
                                                       ALU.mult, ALU.add).then_inc(sem("du_free"), 1)

                with dve.Fori(0, last) as i:
                    round_of(i, False)
                round_of(last, True)
                dve.wait_ge(sem("du_free"), chunks + 2)
                link(dve, nc.vector.reciprocal(rden[:, :], den[:, :]), "relu_chain")
                nc.vector.scalar_tensor_tensor(res[:, :], U[:, :], rden[:, 0:1], res[:, :], ALU.mult,
                                               ALU.add).then_inc(sem("res_ready"), 1)

            @block.tensor
            def _(pe):
                def keys(g):
                    m, n = g // 2, 0
                    for w, c in ((wxh, cTh), (wxl, cTh), (wxh, cTl)):
                        for k in range(KT):
                            mm = nc.tensor.matmul(ps[:, g % 2, 0:HK], w[:, k, m * P:(m + 1) * P],
                                                  c[:, k, (g % 2) * HK:(g % 2 + 1) * HK],
                                                  start=(n == 0), stop=(n == 3 * KT - 1))
                            n += 1
                    mm.then_inc(sem("dk_done"), 1)

                def turn_keys(n):
                    for a, tile in enumerate(range(NT)[tiles_of(n)]):
                        for m in range(KT):
                            mm = nc.tensor.transpose(ps[:, KB[n], a * D + m * P:a * D + (m + 1) * P],
                                                     kT[:, m, tile * P:(tile + 1) * P], ident[:, :])
                    mm.then_inc(sem("dk_turned"), 1)

                def scores(b, low_parts):
                    halves = [slice(half * HK, (half + 1) * HK) for half in range(2)]
                    for half, cols in enumerate(halves):
                        nc.tensor.matmul(S[:, half, :], one_b[:, :], mneg[b][:, cols], start=True, stop=False)
                    for n, (q, c) in enumerate(((qh, kTh), (ql, kTh), (qh, kTl))):
                        if n == 2:
                            pe.wait_ge(sem("dkTl_ready"), low_parts)
                        for half, cols in enumerate(halves):
                            for k in range(KT):
                                mm = nc.tensor.matmul(S[:, half, :], q[:, k, :], c[:, k, cols], start=False,
                                                      stop=(n == 2 and k == KT - 1))
                    mm.then_inc(sem("ds_done"), 1)

                pe.wait_ge(sem("wx_split"), 1)
                pe.wait_ge(sem("dcTl_ready"), 1)
                for g in range(KG):
                    if g == 2:
                        norm_tensor(pe, 3)
                        pe.wait_ge(sem("wx_in"), 32)
                        for m in range(KT):
                            for k in range(KT):
                                mm = nc.tensor.matmul(ps[:, 6, m * P:(m + 1) * P], wx[:, k, m * P:(m + 1) * P],
                                                      xnT[:, k, :], start=(k == 0), stop=(k == KT - 1))
                        mm.then_inc(sem("dq_done"), 1)
                    if g >= 2:
                        pe.wait_ge(sem("dkT_ready"), g - 1)
                    keys(g)
                pe.wait_ge(sem("dkT_ready"), KG)
                for n in range(NG):
                    if n == 3:
                        pe.wait_ge(sem("dkNl_ready"), 1)
                    turn_keys(n)
                pe.wait_ge(sem("dq_split"), 1)
                pe.wait_ge(sem("d_ones"), 1)
                pe.wait_ge(sem("dmask_ready"), 1)
                pe.wait_ge(sem("dkTh_ready"), KG)
                scores(0, KG)

                def round_of(i, end):
                    for b in range(2):
                        more = not (end and b == 1)
                        if more:
                            pe.wait_ge(sem("dcTl_ready"), i * 2 + (b + 2))
                            for g in range(KG):
                                if g >= 2:
                                    pe.wait_ge(sem("dkT_ready"), i * (2 * KG) + (KG * (b + 1) + g - 1))
                                keys(g)
                        pe.wait_ge(sem("dexp_done"), i * 2 + (b + 1))
                        for n, tiles in enumerate(PG):
                            pe.wait_ge(sem("dkNl_ready"), i * (2 * NG) + (NG * b + 2 + n))
                            for k in tiles:
                                mm = nc.tensor.transpose(ps[:, 4 + n, (k - tiles[0]) * P:(k - tiles[0] + 1) * P],
                                                         prob[:, :, :].rearrange("p a n -> p (a n)")[:, k * P:(k + 1) * P],
                                                         ident[:, :])
                            mm.then_inc(sem("dp_turned"), 1)
                        if more:
                            pe.wait_ge(sem("dkNl_ready"), i * (2 * NG) + NG * (b + 1))
                            pe.wait_ge(sem("dkT_ready"), i * (2 * KG) + KG * (b + 2))
                            turn_keys(0)
                            pe.wait_ge(sem("dmask_ready"), i * 2 + (b + 2))
                            pe.wait_ge(sem("dkTh_ready"), i * (2 * KG) + KG * (b + 2))
                            scores(1 - b, i * (2 * KG) + KG * (b + 2))
                            for n in range(1, 3):
                                pe.wait_ge(sem("dpTl_ready"), i * 4 + (2 * b + n))
                                turn_keys(n)
                            pe.wait_ge(sem("dkNl_ready"), i * (2 * NG) + (NG * (b + 1) + 1))
                            turn_keys(3)
                        pe.wait_ge(sem("du_free"), i * 2 + (b + 2))
                        if not more:
                            pe.wait_ge(sem("dkNl_ready"), NG * chunks)
                            pe.wait_ge(sem("dpTl_ready"), 2 * chunks)
                        n = 0
                        for p, c in ((pTh, kNh[b]), (pTh, kNl[b]), (pTl, kNh[b])):
                            for k in range(NT):
                                mm = nc.tensor.matmul(O, p[:, k * P:(k + 1) * P], c[:, k, :],
                                                      start=(n == 0), stop=(n == 3 * NT - 1))
                                n += 1
                        mm.then_inc(sem("dpv_done"), 1)

                with pe.Fori(0, last) as i:
                    round_of(i, False)
                round_of(last, True)


def rank_select(nc, dve, link, name, val, n, k, wins, ties, rank, sel, below):
    by_i = val.unsqueeze(2).broadcast_to([P, n, n])
    by_j = val.unsqueeze(1).broadcast_to([P, n, n])
    nc.vector.tensor_tensor(wins, by_j, by_i, ALU.is_gt)
    link(dve, nc.vector.tensor_tensor(ties, by_j, by_i, ALU.is_equal), name)
    link(dve, nc.vector.tensor_tensor(ties, ties, below[:, 0:n, 0:n], ALU.mult), name)
    link(dve, nc.vector.tensor_tensor(wins, wins, ties, ALU.add), name)
    link(dve, nc.vector.tensor_reduce(rank, wins, AX_X, ALU.add), name)
    link(dve, nc.vector.tensor_scalar(sel, rank, float(k), None, ALU.is_lt), name)


def stage_mix0(nc, t, sb, sem, link, ps, norms, v):
    norm_vector, norm_pool, norm_tensor = norms
    res, xnT, ident = v["res"], v["xnT"], v["ident"]
    w1, w2, b1 = v["w1"], v["w2"], v["b1"]
    FT = F0 // P
    with ExitStack() as own:
        hT = [sb(f"c_hT{i}", [P, FT, P], F32, own) for i in range(2)]
        acc = [res[:, :], sb("c_acc", [P, D], F32, own)[:, :]]
        lg = sb("c_lg", [P, E0], F32, own)
        ex = sb("c_ex", [P, E0], F32, own)
        sel = sb("c_sel", [P, E0], F32, own)
        rank = sb("c_rank", [P, E0], F32, own)
        comb = sb("c_comb", [P, E0], F32, own)
        one = sb("c_one", [P, 4], F32, own)
        wins = sb("c_wins", [P, E0, E0], F32, own)
        ties = sb("c_ties", [P, E0, E0], F32, own)
        combT = sb("c_combT", [E0, P], F32, own)

        with nc.Block() as block:
            @block.gpsimd
            def _(pool):
                norm_pool(pool, 2)
                pool.wait_ge(sem("wx_in"), 32)
                nc.gpsimd.tensor_copy(v["d_wxh"][:, :, :], v["wx"][:, :, :]).then_inc(sem("wxh_ready"), 1)
                pool.wait_ge(sem("wxh_ready"), 1)
                nc.gpsimd.tensor_tensor(v["d_wxl"][:, :, :], v["wx"][:, :, :], v["d_wxh"][:, :, :].bitcast(F32),
                                        ALU.subtract).then_inc(sem("wx_split"), 1)
                pool.wait_ge(sem("dctx_in0"), 16)
                nc.gpsimd.tensor_copy(v["d_cTh"][:, :, :], v["d_raw0"][:, :, :]).then_inc(sem("dcTh_ready"), 1)
                pool.wait_ge(sem("dcTh_ready"), 1)
                nc.gpsimd.tensor_tensor(v["d_cTl"][:, :, :], v["d_raw0"][:, :, :], v["d_cTh"][:, :, :].bitcast(F32),
                                        ALU.subtract).then_inc(sem("dcTl_ready"), 1)

            @block.vector
            def _(dve):
                norm_vector(dve, 2)
                dve.wait_ge(sem("logits0_done"), 1)
                dve.wait_ge(sem("router0_in"), 48)
                link(dve, nc.vector.tensor_tensor(lg[:, :], ps[:, 6, 0:E0], v["bg"][:, :], ALU.add), "mix0_chain")
                nc.vector.tensor_reduce(one[:, 0:1], lg[:, :], AX_X, ALU.max, negate=True).then_inc(sem("lmax0_ready"), 1)
                dve.wait_ge(sem("lexp0_ready"), 1)
                link(dve, nc.vector.reciprocal(one[:, 2:3], one[:, 1:2]), "mix0_chain")
                link(dve, nc.vector.tensor_scalar(ex[:, :], ex[:, :], one[:, 2:3], None, ALU.mult), "mix0_chain")
                rank_select(nc, dve, link, "mix0_chain", ex[:, :], E0, 2, wins[:, :, :], ties[:, :, :], rank[:, :],
                            sel[:, :], v["below"])
                link(dve, nc.vector.tensor_tensor(ex[:, :], ex[:, :], sel[:, :], ALU.mult), "mix0_chain")
                link(dve, nc.vector.tensor_reduce(one[:, 3:4], ex[:, :], AX_X, ALU.add), "mix0_chain")
                link(dve, nc.vector.reciprocal(one[:, 3:4], one[:, 3:4]), "mix0_chain")
                nc.vector.tensor_scalar(comb[:, :], ex[:, :], one[:, 3:4], None, ALU.mult).then_inc(sem("comb0_ready"), 1)
                dve.wait_ge(sem("comb0_ready"), 1)

                def add(e):
                    dve.wait_ge(sem("y2_part"), e + 1)
                    y, w = ps[:, 4 + e % 2, 0:D], comb[:, e:e + 1]
                    if e == 1:
                        ins = nc.vector.tensor_scalar(acc[1], y, w, None, ALU.mult)
                    else:
                        if e > 1:
                            dve.wait_ge(sem("y2_added"), e - 1)
                        ins = nc.vector.scalar_tensor_tensor(acc[e % 2], y, w, acc[e % 2], ALU.mult, ALU.add)
                    ins.then_inc(sem("y2_added"), 1)

                add(0)
                add(1)
                dve.wait_ge(sem("comb0_turned"), 1)
                nc.vector.tensor_copy(combT[:, :], ps[0:E0, 6, P:2 * P]).then_inc(sem("combT_ready"), 1)
                for e in range(2, E0):
                    if e == E0 - 1:
                        dve.wait_ge(sem("y2_done"), 1)
                        dve.wait_ge(sem("y2_added"), e - 1)
                        link(dve, nc.vector.tensor_tensor(acc[1], acc[1], ps[:, 7, 0:D], ALU.add), "mix0_chain")
                    add(e)
                dve.wait_ge(sem("y2_added"), E0)
                nc.vector.tensor_tensor(res[:, :], res[:, :], acc[1], ALU.add).then_inc(sem("res_ready"), 1)

            @block.scalar
            def _(act):
                def rectified(e):
                    act.wait_ge(sem("h0_done"), e + 1)
                    if e >= 2:
                        act.wait_ge(sem("y2_part"), e - 1)
                    for f in range(FT):
                        ins = nc.scalar.activation(hT[e % 2][:, f, :], ps[:, e % 4, f * P:(f + 1) * P], ACT.Relu,
                                                   bias=b1[:, e * FT + f:e * FT + f + 1], scale=1.0)
                    ins.then_inc(sem("hT0_ready"), 1)

                act.wait_ge(sem("lmax0_ready"), 1)
                nc.scalar.activation(ex[:, :], lg[:, :], ACT.Exp, bias=one[:, 0:1], scale=1.0,
                                     accum_out=one[:, 1:2]).then_inc(sem("lexp0_ready"), 1)
                act.wait_ge(sem("b1_in"), 16)
                rectified(0)
                for e in range(1, E0):
                    rectified(e)

            @block.tensor
            def _(pe):
                norm_tensor(pe, 2)
                pe.wait_ge(sem("router0_in"), 48)
                for k in range(KT):
                    mm = nc.tensor.matmul(ps[:, 6, 0:E0], xnT[:, k, :], v["wg0"][:, k, :], start=(k == 0), stop=(k == KT - 1))
                mm.then_inc(sem("logits0_done"), 1)

                def hidden(e):
                    if e >= 4:
                        pe.wait_ge(sem("hT0_ready"), e - 3)
                    for f in range(FT):
                        for k in range(KT):
                            mm = nc.tensor.matmul(ps[:, e % 4, f * P:(f + 1) * P], w1[:, k, e, f * P:(f + 1) * P],
                                                  xnT[:, k, :], start=(k == 0), stop=(k == KT - 1))
                    mm.then_inc(sem("h0_done"), 1)

                def down(e):
                    pe.wait_ge(sem("hT0_ready"), e + 1)
                    if e >= 2:
                        pe.wait_ge(sem("y2_added"), e - 1)
                    for f in range(FT):
                        mm = nc.tensor.matmul(ps[:, 4 + e % 2, 0:D], hT[e % 2][:, f, :], w2[:, e * FT + f, :],
                                              start=(f == 0), stop=(f == FT - 1))
                    mm.then_inc(sem("y2_part"), 1)

                pe.wait_ge(sem("w1_in"), 16)
                hidden(0)
                hidden(1)
                pe.wait_ge(sem("w2_in"), 16)
                for e in range(E0):
                    if e + 2 < E0:
                        hidden(e + 2)
                    down(e)
                    if e == 3:
                        nc.tensor.transpose(ps[0:E0, 6, P:2 * P], comb[:, :], ident[:, :]).then_inc(sem("comb0_turned"), 1)
                    if e == 5:
                        pe.wait_ge(sem("combT_ready"), 1)
                        nc.tensor.matmul(ps[:, 7, 0:D], combT[:, :], v["b2"][:, :], start=True, stop=True).then_inc(sem("y2_done"), 1)


def stage_band(nc, t, sb, sem, link, ps, norms, v):
    norm_vector, norm_pool, norm_tensor = norms
    res, xnT, ident, ones, row0, hmask, dist = (v[n] for n in ("res", "xnT", "ident", "ones", "row0", "hmask", "dist"))
    SCALE = DH1 ** -0.5
    MAX_W, MIN_W = 120.0, 24.0
    with ExitStack() as own:
        qT = sb("b_qT", [P, KT, P], F32, own)
        kT = sb("b_kT", [P, KT, P], F32, own)
        kx = sb("b_kx", [P, KT, HPT, P], F32, own)
        val = sb("b_v", [P, D], F32, own)
        s = sb("b_s", [P, H1, P], F32, own)
        sT = kx[:, :, :, :].rearrange("p m h q -> p (m h) q")
        band = sb("b_band", [P, P], F32, own)
        diff = sb("b_diff", [P, KT], F32, own)
        flu = sb("b_flu", [P, KT], F32, own)
        sg = sb("b_sg", [P, 10], F32, own)
        mx = sb("b_mx", [P, H1], F32, own)
        sm = sb("b_sm", [P, H1], F32, own)
        rd = sb("b_rd", [P, H1], F32, own)
        o = sb("b_o", [P, D], F32, own)
        oT = sb("b_oT", [P, KT, P], F32, own)
        o2T = sb("b_o2T", [P, KT, P], F32, own)
        wox = sb("b_wox", [P, KT, HPT, DH1], F32, own)

        def part(x, m):
            return x[:, m * HPT:(m + 1) * HPT, :]

        def heads(x, m):
            return x[:, m * HPT:(m + 1) * HPT]

        def by_head(x):
            return x.rearrange("p (h d) -> p h d", h=H1)

        with nc.Block() as block:
            @block.sync
            def _(sp):
                sp.dma_start(v["wg0"][:, :, :], t["wg0"]).then_inc(sem("router0_in"), 16)
                sp.dma_start(v["bg"][:, :], t["bg"].partition_broadcast(P)).then_inc(sem("router0_in"), 16)
                sp.dma_start(v["b2"][:, :], t["b2"]).then_inc(sem("router0_in"), 16)
                sp.dma_start(v["w1"][:, :, :, :], t["w1"]).then_inc(sem("w1_in"), 16)
                sp.dma_start(v["b1"][:, :], t["b1"]).then_inc(sem("b1_in"), 16)
                sp.dma_start(v["w2"][:, :, :], t["w2"]).then_inc(sem("w2_in"), 16)
                sp.dma_start(v["wx"][:, :, :], t["wx"]).then_inc(sem("wx_in"), 16)
                sp.dma_start(v["bx"][:, :], t["bx"]).then_inc(sem("wx_in"), 16)
                sp.dma_start(v["d_raw0"][:, :, :], t["ctxT"][0]).then_inc(sem("dctx_in0"), 16)
                sp.dma_start(v["wxp"][:, :, :], t["wxp"]).then_inc(sem("late_in"), 16)
                sp.dma_start(v["wdt"][:, :], t["wdt"]).then_inc(sem("late_in"), 16)
                sp.dma_start(v["bdt"][:, :], t["bdt"]).then_inc(sem("late_in"), 16)
                sp.dma_start(v["dskip"][:, :], t["dskip"].partition_broadcast(P)).then_inc(sem("late_in"), 16)
                sp.dma_start(v["wr1"][:, :, :], t["wr1"]).then_inc(sem("late_in"), 16)
                sp.dma_start(v["br1"][:, :], t["br1"].partition_broadcast(P)).then_inc(sem("late_in"), 16)
                sp.dma_start(v["wg"][:, :, :], t["wg1"]).then_inc(sem("mix1_in"), 16)

            @block.gpsimd
            def _(pool):
                norm_pool(pool, 1)
                pool.wait_ge(sem("s1_max"), 1)
                nc.gpsimd.tensor_tensor(part(s, 0), part(s, 0), heads(mx, 0).unsqueeze(2).broadcast_to([P, HPT, P]),
                                        ALU.subtract).then_inc(sem("s1_shifted0"), 1)

            @block.vector
            def _(dve):
                norm_vector(dve, 1)
                dve.wait_ge(sem("consts_ready"), 1)
                dve.wait_ge(sem("band_in"), 112)
                dve.wait_ge(sem("xnT_ready"), 2)
                link(dve, nc.vector.tensor_tensor(diff[:, :], xnT[:, :, P - 1], xnT[:, :, P - 2], ALU.subtract), "band_chain")
                nc.vector.scalar_tensor_tensor(flu[:, :], diff[:, :], -1.0, diff[:, :], ALU.mult,
                                               ALU.max).then_inc(sem("fluct_ready"), 1)
                nc.vector.tensor_tensor(dist[:, :], v["disti"][:, 0, :], v["disti"][:, 1, :], ALU.max)
                dve.wait_ge(sem("ea_ready"), 1)
                link(dve, nc.vector.tensor_scalar(sg[:, 1:2], sg[:, 0:1], 1.0, None, ALU.add), "band_chain")
                link(dve, nc.vector.reciprocal(sg[:, 2:3], sg[:, 1:2]), "band_chain")
                link(dve, nc.vector.tensor_scalar(sg[:, 3:4], sg[:, 2:3], -1.0, 1.0, ALU.mult, ALU.add), "band_chain")
                dve.wait_ge(sem("fluct_sum"), 1)
                link(dve, nc.vector.tensor_scalar(sg[:, 4:5], ps[:, 6, 0:1], 1.0 / D, None, ALU.mult), "band_chain")
                link(dve, nc.vector.tensor_tensor(sg[:, 5:6], sg[:, 4:5], sg[:, 2:3], ALU.mult), "band_chain")
                nc.vector.scalar_tensor_tensor(sg[:, 6:7], ps[:, 6, 1:2], sg[:, 3:4], sg[:, 5:6], ALU.mult,
                                               ALU.add).then_inc(sem("signal_ready"), 1)
                dve.wait_ge(sem("es_ready"), 1)
                link(dve, nc.vector.tensor_scalar(sg[:, 8:9], sg[:, 7:8], 1.0, None, ALU.add), "band_chain")
                link(dve, nc.vector.reciprocal(sg[:, 8:9], sg[:, 8:9]), "band_chain")
                link(dve, nc.vector.tensor_scalar(sg[:, 9:10], sg[:, 8:9], MAX_W - MIN_W, MIN_W, ALU.mult, ALU.add), "band_chain")
                link(dve, nc.vector.tensor_scalar(band[:, :], dist[:, :], sg[:, 9:10], -BIG, ALU.is_gt, ALU.mult), "band_chain")
                dve.wait_ge(sem("qk1_done"), 1)
                for m in range(KT):
                    nc.vector.tensor_scalar(qT[:, m, :], ps[:, 0, m * P:(m + 1) * P], v["abqk"][:, m:m + 1], None,
                                            ALU.add).then_inc(sem("qk1_ready"), 1)
                    link(dve, nc.vector.tensor_scalar(kT[:, m, :], ps[:, 0, D + m * P:D + (m + 1) * P],
                                                      v["abqk"][:, KT + m:KT + m + 1], None, ALU.add), "band_chain")
                    nc.vector.tensor_tensor(kx[:, m, :, :], kT[:, m, :].unsqueeze(1).broadcast_to([P, HPT, P]),
                                            hmask[:, :].unsqueeze(2).broadcast_to([P, HPT, P]),
                                            ALU.mult).then_inc(sem("qk1_ready"), 1)
                for m in range(KT):
                    dve.wait_ge(sem("s1_done"), m + 1)
                    link(dve, nc.vector.scalar_tensor_tensor(
                        part(s, m), ps[:, 2 + 2 * m:4 + 2 * m, :].rearrange("p b (h q) -> p (b h) q", h=4),
                        SCALE, band[:, :].unsqueeze(1).broadcast_to([P, HPT, P]), ALU.mult, ALU.add), "band_chain")
                    nc.vector.tensor_reduce(heads(mx, m), part(s, m), AX_X, ALU.max).then_inc(sem("s1_max"), 1)
                dve.wait_ge(sem("s1_max"), KT)
                nc.vector.tensor_tensor(part(s, 1), part(s, 1), heads(mx, 1).unsqueeze(2).broadcast_to([P, HPT, P]),
                                        ALU.subtract).then_inc(sem("s1_shifted"), 1)
                for m in range(KT):
                    nc.vector.tensor_tensor(wox[:, m, :, :], v["awo"][:, m, :].unsqueeze(1).broadcast_to([P, HPT, DH1]),
                                            hmask[:, :].unsqueeze(2).broadcast_to([P, HPT, DH1]),
                                            ALU.mult).then_inc(sem("wox_ready"), 1)
                dve.wait_ge(sem("v1_done"), 1)
                nc.vector.tensor_copy(val[:, :], ps[:, 1, 0:D]).then_inc(sem("v1_ready"), 1)
                for m in range(KT):
                    dve.wait_ge(sem(f"p1_ready{m}"), 1)
                    link(dve, nc.vector.tensor_reduce(heads(sm, m), part(s, m), AX_X, ALU.add), "band_chain")
                link(dve, nc.vector.reciprocal(rd[:, :], sm[:, :]), "band_chain")
                dve.wait_ge(sem("p1_turned"), 2)
                nc.vector.tensor_copy(sT[:, 8:16, :], ps[:, 4:6, :].rearrange("p b (h q) -> p (b h) q", h=4)).then_inc(
                    sem("p1T_b"), 1)
                dve.wait_ge(sem("o1_done"), 1)
                nc.vector.tensor_tensor(by_head(o[:, :]), by_head(ps[:, 6, 0:D]),
                                        rd[:, :].unsqueeze(2).broadcast_to([P, H1, DH1]),
                                        ALU.mult).then_inc(sem("o1_ready"), 1)
                dve.wait_ge(sem("o1_turned"), 1)
                nc.vector.tensor_copy(oT[:, :, :], ps[:, 7, 0:D].rearrange("p (k q) -> p k q", k=KT)).then_inc(sem("o1T_ready"), 1)
                dve.wait_ge(sem("o2_done"), 1)
                nc.vector.tensor_copy(o2T[:, :, :], ps[:, 0, 0:D].rearrange("p (k q) -> p k q", k=KT)).then_inc(sem("o2T_ready"), 1)
                dve.wait_ge(sem("y1_done"), 1)
                nc.vector.tensor_tensor(res[:, :], res[:, :], ps[:, 1, 0:D], ALU.add).then_inc(sem("res_ready"), 1)

            @block.scalar
            def _(act):
                act.wait_ge(sem("band_in"), 112)
                nc.scalar.activation(sg[:, 0:1], v["alpha"][:, :], ACT.Exp, scale=-1.0).then_inc(sem("ea_ready"), 1)
                act.wait_ge(sem("signal_ready"), 1)
                nc.scalar.activation(sg[:, 7:8], sg[:, 6:7], ACT.Exp, scale=-1.0).then_inc(sem("es_ready"), 1)
                for m, shifted in enumerate(("s1_shifted0", "s1_shifted")):
                    act.wait_ge(sem(shifted), 1)
                    nc.scalar.activation(part(s, m), part(s, m), ACT.Exp).then_inc(sem(f"p1_ready{m}"), 1)
                act.wait_ge(sem("p1_turned"), 1)
                nc.scalar.copy(sT[:, 0:8, :], ps[:, 2:4, :].rearrange("p b (h q) -> p (b h) q", h=4)).then_inc(sem("p1T_a"), 1)

            @block.tensor
            def _(pe):
                norm_tensor(pe, 1)
                pe.wait_ge(sem("band_in"), 112)
                pe.wait_ge(sem("fluct_ready"), 1)
                for k in range(KT):
                    nc.tensor.matmul(ps[:, 6, 0:1], ones[:, :], flu[:, k:k + 1], start=(k == 0), stop=(k == KT - 1))
                nc.tensor.matmul(ps[:, 6, 1:2], row0[:, :], flu[:, 0:1], start=True, stop=True).then_inc(sem("fluct_sum"), 1)
                for w, col in ((v["aq"], 0), (v["ak"], D)):
                    for m in range(KT):
                        for k in range(KT):
                            mm = nc.tensor.matmul(ps[:, 0, col + m * P:col + (m + 1) * P], w[:, k, m * P:(m + 1) * P],
                                                  xnT[:, k, :], start=(k == 0), stop=(k == KT - 1))
                mm.then_inc(sem("qk1_done"), 1)
                nc.tensor.matmul(ps[:, 1, 0:D], ones[0:1, :], v["brow"][0:1, D:2 * D], start=True, stop=False)
                for k in range(KT):
                    mm = nc.tensor.matmul(ps[:, 1, 0:D], xnT[:, k, :], v["av"][:, k, :], start=False, stop=(k == KT - 1))
                mm.then_inc(sem("v1_done"), 1)
                for m in range(KT):
                    pe.wait_ge(sem("qk1_ready"), 2 * m + 2)
                    for half in range(2):
                        mm = nc.tensor.matmul(ps[:, 2 + 2 * m + half, :], qT[:, m, :],
                                              kx[:, m, 4 * half:4 * half + 4, :].rearrange("p h q -> p (h q)"),
                                              start=True, stop=True)
                    mm.then_inc(sem("s1_done"), 1)
                for h in range(H1):
                    if h % HPT == 0:
                        pe.wait_ge(sem(f"p1_ready{h // HPT}"), 1)
                    mm = nc.tensor.transpose(ps[:, 2 + h // 4, (h % 4) * P:(h % 4 + 1) * P], s[:, h, :], ident[:, :])
                    if h % 8 == 7:
                        mm.then_inc(sem("p1_turned"), 1)
                pe.wait_ge(sem("v1_ready"), 1)
                for h in range(H1):
                    if h % 8 == 0:
                        pe.wait_ge(sem("p1T_a" if h == 0 else "p1T_b"), 1)
                    mm = nc.tensor.matmul(ps[:, 6, h * DH1:(h + 1) * DH1], sT[:, h, :], val[:, h * DH1:(h + 1) * DH1],
                                          start=True, stop=True)
                mm.then_inc(sem("o1_done"), 1)
                pe.wait_ge(sem("o1_ready"), 1)
                for k in range(KT):
                    mm = nc.tensor.transpose(ps[:, 7, k * P:(k + 1) * P], o[:, k * P:(k + 1) * P], ident[:, :])
                mm.then_inc(sem("o1_turned"), 1)
                pe.wait_ge(sem("wox_ready"), KT)
                pe.wait_ge(sem("o1T_ready"), 1)
                for m in range(KT):
                    mm = nc.tensor.matmul(ps[:, 0, m * P:(m + 1) * P], wox[:, m, :, :].rearrange("p h d -> p (h d)"),
                                          oT[:, m, :], start=True, stop=True)
                mm.then_inc(sem("o2_done"), 1)
                pe.wait_ge(sem("o2T_ready"), 1)
                nc.tensor.matmul(ps[:, 1, 0:D], ones[0:1, :], v["brow"][0:1, 2 * D:3 * D], start=True, stop=False)
                for k in range(KT):
                    mm = nc.tensor.matmul(ps[:, 1, 0:D], o2T[:, k, :], v["afc"][:, k, :], start=False, stop=(k == KT - 1))
                mm.then_inc(sem("y1_done"), 1)


def layout(inputs):
    import numpy as np

    a = {k: np.asarray(x) for k, x in inputs.items()}

    def rows(w):
        return w.reshape(w.shape[0] // P, P, -1).transpose(1, 0, 2)

    def cols(b):
        return b.reshape(-1, P).T

    def side_by_side(routed, shared):
        return rows(np.concatenate([a[routed].reshape(E1 * F1, D), a[shared]], 0).T)

    ctx = a["ctx_1024"][0]
    n = ctx.shape[0] // CK
    t = {
        "x": a["x"][0],
        "ctxN": ctx.reshape(n, NT, P, D).transpose(0, 2, 1, 3),
        "ctxT": ctx.reshape(n, CK, KT, P).transpose(0, 3, 2, 1),
        "wq0": rows(a["L0_xattn_Wq"]),
        "wk0": rows(a["L0_xattn_Wkv"][:, :H0 * DH0]),
        "wv0": rows(a["L0_xattn_Wkv"][:, H0 * DH0:]),
        "wo0": rows(a["L0_xattn_Wo"]),
        "brow": np.concatenate([a["L0_xattn_bo"], a["L0_attn_bv"], a["L0_attn_bfc"]])[None, :],
        "aq": rows(a["L0_attn_Wq"]), "ak": rows(a["L0_attn_Wk"]), "av": rows(a["L0_attn_Wv"]),
        "afc": rows(a["L0_attn_Wfc"]), "awo": rows(a["L0_attn_W_o"].reshape(D, DH1)),
        "abqk": np.concatenate([cols(a["L0_attn_bq"]), cols(a["L0_attn_bk"])], 1),
        "alpha": a["L0_attn_alpha"].reshape(1),
        "wg0": rows(a["L0_ffn_Wg"]), "bg": a["L0_ffn_bg"], "b2": a["L0_ffn_b2"],
        "w1": a["L0_ffn_W1"].reshape(E0, KT, P, F0).transpose(2, 1, 0, 3), "b1": cols(a["L0_ffn_b1"]),
        "w2": rows(a["L0_ffn_W2"].reshape(E0 * F0, D)),
        "wx": rows(a["L1_xattn_W"].T), "bx": cols(a["L1_xattn_b"]),
        "mask": a["mask_BxS2_bk0"].reshape(n, CK),
        "wxp": rows(a["L1_attn_W_xproj"]), "wdt": a["L1_attn_W_dt"], "bdt": a["L1_attn_b_dt"][None, :],
        "dskip": a["L1_attn_D"], "alog": a["L1_attn_A_log"].reshape(-1),
        "wr1": rows(a["L1_ffn_gate_w"].T), "br1": a["L1_ffn_gate_bias"],
        "wg1": side_by_side("L1_ffn_expert_gate", "L1_ffn_shared_gate"),
        "wu1": side_by_side("L1_ffn_expert_up", "L1_ffn_shared_up"),
        "wd1": np.concatenate([a["L1_ffn_expert_down"].transpose(2, 0, 1),
                               a["L1_ffn_shared_down"].reshape(D, NS1, F1).transpose(2, 1, 0)], 1),
    }
    return {k: np.ascontiguousarray(x) for k, x in t.items()}


def kernel(**inputs):
    import numpy as np
    import concourse.bacc as _bacc
    from concourse import mybir as _mybir
    from concourse.bass_utils import run_bass_kernel_spmd as _run

    arrays = layout(inputs)
    nc = _bacc.Bacc("TRN2", target_bir_lowering=False, num_devices=1)
    t = {}
    for name, a in arrays.items():
        t[name] = nc.dram_tensor(f"in_{name}", a.shape, _mybir.dt.from_np(a.dtype), kind="ExternalInput").ap()
    out = nc.dram_tensor("out", (P, D), F32, kind="ExternalOutput").ap()
    build(nc, t, out)
    r = _run(nc, [{f"in_{k}": a for k, a in arrays.items()}], core_ids=[0])
    return np.asarray(r.results[0]["out"]).reshape(1, P, D)
```
